# Optimizing a Trainium2 kernel written in Bass

```python
import numpy as np
import jax
import jax.numpy as jnp

def _softmax(x, axis=-1):
    return jax.nn.softmax(x, axis=axis)

def _gelu(x):
    return jax.nn.gelu(x, approximate=True)

def _silu(x):
    return jax.nn.silu(x)

def _sigmoid(x):
    return jax.nn.sigmoid(x)

def _layernorm(x, axis=-1, eps=1e-05):
    m = jnp.mean(x, axis=axis, keepdims=True)
    v = jnp.var(x, axis=axis, keepdims=True)
    return (x - m) / jnp.sqrt(v + eps)

def _scatter_add(tgt, idx, src, axis=0):
    return tgt.at[idx].add(src)

def _segment_sum(src, seg, n):
    return jax.ops.segment_sum(src, seg, n)
kernel_name = 'mk_decoder_postln_d1_seqx_r8_dc769d'

def setup_inputs(seed: int=0):
    np.random.seed(seed)
    _w = jnp.asarray

    def _rec_inputs():
        import jax
        import jax.numpy as jnp
        _rk = jax.random.key(seed)
        x = -0.0003929 + 0.9999 * jax.random.normal(jax.random.fold_in(_rk, 1), (2, 512, 128), jnp.float32)
        _lenS = 512 - jax.random.randint(jax.random.fold_in(_rk, 7), (2,), 0, max(1, 512 // 4) + 1, jnp.int32)
        _lenS2 = 32 - jax.random.randint(jax.random.fold_in(_rk, 8), (2,), 0, max(1, 32 // 4) + 1, jnp.int32)
        _ctx_1024P = jax.random.normal(jax.random.fold_in(_rk, 11), (2, 16, 128), jnp.float32)
        _ctx_1024c = jax.random.dirichlet(jax.random.fold_in(_rk, 511), 0.3 * jnp.ones((16,), jnp.float32), (2, 32))
        _ctx_1024t = jnp.einsum('bsk,bkd->bsd', _ctx_1024c, _ctx_1024P)
        _ctx_1024t = _ctx_1024t * jax.lax.rsqrt(jnp.mean(jnp.square(_ctx_1024t)) + 1e-12) * 0.953939
        ctx_1024 = 2.81802e-05 + 1.00001 * (_ctx_1024t + 0.3 * jax.random.normal(jax.random.fold_in(_rk, 611), (2, 32, 128), jnp.float32))
        return (x, ctx_1024)
    x, ctx_1024 = _rec_inputs()

    def _L0_attn_setup():
        import jax, jax.numpy as jnp
        import numpy as np
        EPS = 1e-05

        def layer_norm(x, w, b):
            mu = jnp.mean(x, axis=-1, keepdims=True)
            var = jnp.var(x, axis=-1, keepdims=True)
            return (x - mu) / jnp.sqrt(var + EPS) * w + b
        key = jax.random.key(seed)
        B, N, C = (4, 512, 128)
        H = 16
        MW = 4 * C
        ks = jax.random.split(key, 8)
        s = 0.02
        return {'x': jax.random.normal(ks[0], (B, N, C), dtype=jnp.float32), 'ln1_w': jnp.ones((C,), jnp.float32), 'ln1_b': jnp.zeros((C,), jnp.float32), 'q_w': jax.random.normal(ks[1], (C, C), jnp.float32) * s, 'q_b': jnp.zeros((C,), jnp.float32), 'k_w': jax.random.normal(ks[2], (C, C), jnp.float32) * s, 'k_b': jnp.zeros((C,), jnp.float32), 'v_w': jax.random.normal(ks[3], (C, C), jnp.float32) * s, 'v_b': jnp.zeros((C,), jnp.float32), 'o_w': jax.random.normal(ks[4], (C, C), jnp.float32) * s, 'o_b': jnp.zeros((C,), jnp.float32), 'ln2_w': jnp.ones((C,), jnp.float32), 'ln2_b': jnp.zeros((C,), jnp.float32), 'fc_w': jax.random.normal(ks[5], (MW, C), jnp.float32) * s, 'fc_b': jnp.zeros((MW,), jnp.float32), 'proj_w': jax.random.normal(ks[6], (C, MW), jnp.float32) * s, 'proj_b': jnp.zeros((C,), jnp.float32)}
    _L0_attn_all = _L0_attn_setup()
    _L0_attn_in = {k: v for k, v in _L0_attn_all.items() if k in ('ln1_w', 'ln1_b', 'q_w', 'q_b', 'k_w', 'k_b', 'v_w', 'v_b', 'o_w', 'o_b', 'ln2_w', 'ln2_b', 'fc_w', 'fc_b', 'proj_w', 'proj_b')}
    del _L0_attn_all

    def _L0_xattn_setup():
        import jax, jax.numpy as jnp
        import numpy as np
        key = jax.random.key(seed)
        ks = jax.random.split(key, 9)
        B, S, D = (8, 256, 128)
        Qd = Kd = Vd = 128
        s = 1.0 / np.sqrt(D)
        return {'query': jax.random.normal(ks[0], (B, S, D), jnp.float32), 'key': jax.random.normal(ks[1], (B, S, D), jnp.float32), 'value': jax.random.normal(ks[2], (B, S, D), jnp.float32), 'Wq': jax.random.normal(ks[3], (D, Qd), jnp.float32) * s, 'bq': jnp.zeros((Qd,), jnp.float32), 'Wk': jax.random.normal(ks[4], (D, Kd), jnp.float32) * s, 'bk': jnp.zeros((Kd,), jnp.float32), 'Wv': jax.random.normal(ks[5], (D, Vd), jnp.float32) * s, 'bv': jnp.zeros((Vd,), jnp.float32)}
    _L0_xattn_all = _L0_xattn_setup()
    _L0_xattn_in = {k: v for k, v in _L0_xattn_all.items() if k in ('Wq', 'bq', 'Wk', 'bk', 'Wv', 'bv')}
    del _L0_xattn_all

    def _L0_ffn_setup():
        import jax, jax.numpy as jnp
        import numpy as np
        import math
        N_EXP = 8
        TOP_K = 2
        CAPACITY_FACTOR = 1.25

        def _capacity(num_tokens):
            cap = math.floor(TOP_K * CAPACITY_FACTOR * num_tokens / N_EXP)
            cap += cap % 2
            return int(cap)
        key = jax.random.key(seed)
        k1, k2, k3, k4 = jax.random.split(key, 4)
        B, C, d = (4, 128, 128)
        x = jax.random.normal(k1, (B, C, d), dtype=jnp.float32)
        w_g = jax.random.normal(k2, (d, N_EXP), dtype=jnp.float32) * 0.02
        c_fc = jax.random.normal(k3, (N_EXP, d, 4 * d), dtype=jnp.float32) * 0.02
        c_proj = jax.random.normal(k4, (N_EXP, 4 * d, d), dtype=jnp.float32) * 0.02
        return {'x': x, 'w_g': w_g, 'c_fc': c_fc, 'c_proj': c_proj}
    _L0_ffn_all = _L0_ffn_setup()
    _L0_ffn_in = {k: v for k, v in _L0_ffn_all.items() if k in ('w_g', 'c_fc', 'c_proj')}
    del _L0_ffn_all
    return {'x': x, 'ctx_1024': ctx_1024, 'L0_attn_ln1_w': _L0_attn_in['ln1_w'], 'L0_attn_ln1_b': _L0_attn_in['ln1_b'], 'L0_attn_q_w': _L0_attn_in['q_w'], 'L0_attn_q_b': _L0_attn_in['q_b'], 'L0_attn_k_w': _L0_attn_in['k_w'], 'L0_attn_k_b': _L0_attn_in['k_b'], 'L0_attn_v_w': _L0_attn_in['v_w'], 'L0_attn_v_b': _L0_attn_in['v_b'], 'L0_attn_o_w': _L0_attn_in['o_w'], 'L0_attn_o_b': _L0_attn_in['o_b'], 'L0_attn_ln2_w': _L0_attn_in['ln2_w'], 'L0_attn_ln2_b': _L0_attn_in['ln2_b'], 'L0_attn_fc_w': _L0_attn_in['fc_w'], 'L0_attn_fc_b': _L0_attn_in['fc_b'], 'L0_attn_proj_w': _L0_attn_in['proj_w'], 'L0_attn_proj_b': _L0_attn_in['proj_b'], 'L0_xattn_Wq': _L0_xattn_in['Wq'], 'L0_xattn_bq': _L0_xattn_in['bq'], 'L0_xattn_Wk': _L0_xattn_in['Wk'], 'L0_xattn_bk': _L0_xattn_in['bk'], 'L0_xattn_Wv': _L0_xattn_in['Wv'], 'L0_xattn_bv': _L0_xattn_in['bv'], 'L0_ffn_w_g': _L0_ffn_in['w_g'], 'L0_ffn_c_fc': _L0_ffn_in['c_fc'], 'L0_ffn_c_proj': _L0_ffn_in['c_proj']}

def reference(x, ctx_1024, L0_attn_ln1_w, L0_attn_ln1_b, L0_attn_q_w, L0_attn_q_b, L0_attn_k_w, L0_attn_k_b, L0_attn_v_w, L0_attn_v_b, L0_attn_o_w, L0_attn_o_b, L0_attn_ln2_w, L0_attn_ln2_b, L0_attn_fc_w, L0_attn_fc_b, L0_attn_proj_w, L0_attn_proj_b, L0_xattn_Wq, L0_xattn_bq, L0_xattn_Wk, L0_xattn_bk, L0_xattn_Wv, L0_xattn_bv, L0_ffn_w_g, L0_ffn_c_fc, L0_ffn_c_proj):
    import jax
    import jax.numpy as jnp

    def _L0_attn_ref(x, ln1_w, ln1_b, q_w, q_b, k_w, k_b, v_w, v_b, o_w, o_b, ln2_w, ln2_b, fc_w, fc_b, proj_w, proj_b):
        import jax, jax.numpy as jnp
        import numpy as np
        EPS = 1e-05

        def layer_norm(x, w, b):
            mu = jnp.mean(x, axis=-1, keepdims=True)
            var = jnp.var(x, axis=-1, keepdims=True)
            return (x - mu) / jnp.sqrt(var + EPS) * w + b
        B, N, C = x.shape
        H = 16
        D = C // H
        xn = layer_norm(x, ln1_w, ln1_b)
        q = (xn @ q_w.T + q_b).reshape(B, N, H, D).transpose(0, 2, 1, 3)
        k = (xn @ k_w.T + k_b).reshape(B, N, H, D).transpose(0, 2, 1, 3)
        v = (xn @ v_w.T + v_b).reshape(B, N, H, D).transpose(0, 2, 1, 3)
        q = jax.nn.elu(q) + 1.0
        k = jax.nn.elu(k) + 1.0
        kv = jnp.einsum('bhnd,bhne->bnde', k, v)
        qkv = jnp.einsum('bhnd,bnde->bhne', q, kv)
        k_sum = k.sum(axis=1)
        qk = jnp.einsum('bhnd,bnd->bhn', q, k_sum)
        attn = qkv / qk[..., None]
        attn = attn.transpose(0, 2, 1, 3).reshape(B, N, C)
        attn = attn @ o_w.T + o_b
        x = x + attn
        xn2 = layer_norm(x, ln2_w, ln2_b)
        h = jax.nn.gelu(xn2 @ fc_w.T + fc_b, approximate=False)
        x = x + (h @ proj_w.T + proj_b)
        return x

    def _L0_xattn_ref(query, key, value, Wq, bq, Wk, bk, Wv, bv):
        import jax, jax.numpy as jnp
        import numpy as np
        Q = jnp.einsum('bsd,de->bse', query, Wq) + bq
        K = jnp.einsum('bsd,de->bse', key, Wk) + bk
        V = jnp.einsum('bsd,de->bse', value, Wv) + bv
        scale = 1.0 / jnp.sqrt(jnp.asarray(K.shape[-1], Q.dtype))
        scores = jnp.einsum('bqe,bke->bqk', Q, K) * scale
        attn = jax.nn.softmax(scores, axis=-1)
        return jnp.einsum('bqk,bkv->bqv', attn, V)

    def _L0_ffn_ref(x, w_g, c_fc, c_proj):
        import jax, jax.numpy as jnp
        import numpy as np
        import math
        N_EXP = 8
        TOP_K = 2
        CAPACITY_FACTOR = 1.25

        def _capacity(num_tokens):
            cap = math.floor(TOP_K * CAPACITY_FACTOR * num_tokens / N_EXP)
            cap += cap % 2
            return int(cap)
        B, C, d = x.shape
        T = B * C
        cap = _capacity(T)
        xt = x.reshape(T, d)
        logits = xt @ w_g
        top_v, top_i = jax.lax.top_k(logits, TOP_K)
        full = jnp.full_like(logits, -jnp.inf)
        full = full.at[jnp.arange(T)[:, None], top_i].set(top_v)
        probs = jax.nn.softmax(full, axis=-1)
        exp_mask = jax.nn.one_hot(top_i, N_EXP, dtype=jnp.int32)
        exp_mask = jnp.transpose(exp_mask, (1, 0, 2))
        exp_rank = jnp.cumsum(exp_mask.reshape(TOP_K * T, N_EXP), axis=0) - 1
        exp_rank = exp_rank.reshape(TOP_K, T, N_EXP)
        exp_mask = exp_mask * (exp_rank < cap).astype(jnp.int32)
        exp_rank = jnp.sum(exp_mask * exp_rank, axis=-1)
        exp_weights = exp_mask.astype(x.dtype) * probs[None]
        rank_oh = jax.nn.one_hot(exp_rank, cap, dtype=x.dtype)
        cb_weight = jnp.einsum('kte,ktc->tec', exp_weights, rank_oh)
        sec_mask = (cb_weight != 0).astype(x.dtype)
        exp_batches = jnp.einsum('tec,td->ecd', sec_mask, xt)
        h = jax.nn.gelu(jnp.einsum('ecd,edf->ecf', exp_batches, c_fc), approximate=False)
        exp_out = jnp.einsum('ecf,efd->ecd', h, c_proj)
        out = cb_weight.reshape(T, N_EXP * cap) @ exp_out.reshape(N_EXP * cap, d)
        return out.reshape(B, C, d)
    x = _layernorm(x + _L0_attn_ref(x, L0_attn_ln1_w, L0_attn_ln1_b, L0_attn_q_w, L0_attn_q_b, L0_attn_k_w, L0_attn_k_b, L0_attn_v_w, L0_attn_v_b, L0_attn_o_w, L0_attn_o_b, L0_attn_ln2_w, L0_attn_ln2_b, L0_attn_fc_w, L0_attn_fc_b, L0_attn_proj_w, L0_attn_proj_b), axis=-1)
    x = _layernorm(x + _L0_xattn_ref(x, ctx_1024, ctx_1024, L0_xattn_Wq, L0_xattn_bq, L0_xattn_Wk, L0_xattn_bk, L0_xattn_Wv, L0_xattn_bv), axis=-1)
    x = _layernorm(x + _L0_ffn_ref(x, L0_ffn_w_g, L0_ffn_c_fc, L0_ffn_c_proj), axis=-1)
    return x

_drawn_inputs = setup_inputs


def setup_inputs(seed=0):
    import zlib

    import numpy as np

    out = dict(_drawn_inputs(seed))
    spreads = {'L0_attn_ln1_w': (1.0, 0.6),
     'L0_attn_ln1_b': (0.0, 0.8),
     'L0_attn_q_b': (0.0, 0.8),
     'L0_attn_k_b': (0.0, 0.8),
     'L0_attn_v_b': (0.0, 0.8),
     'L0_attn_o_b': (0.0, 0.1),
     'L0_attn_ln2_w': (1.0, 0.6),
     'L0_attn_ln2_b': (0.0, 2.0),
     'L0_attn_fc_b': (0.0, 0.7),
     'L0_attn_proj_b': (0.0, 0.1),
     'L0_xattn_bq': (0.0, 0.347),
     'L0_xattn_bk': (0.0, 2.0),
     'L0_xattn_bv': (0.0, 0.1)}
    factors = {'L0_attn_q_w': 8.0, 'L0_attn_k_w': 8.0, 'L0_attn_v_w': 8.0, 'L0_attn_o_w': 7.873}
    for name, (base, spread) in spreads.items():
        noise = np.random.default_rng([zlib.crc32(name.encode()), seed]).standard_normal(out[name].shape)
        drawn = base * np.exp(spread * noise) if base else spread * noise
        out[name] = jnp.asarray(drawn.astype(out[name].dtype))
    for name, factor in factors.items():
        out[name] = (out[name] * factor).astype(out[name].dtype)
    return out
```

```python
import numpy as np
import concourse.bass as bass
from concourse import mybir
from contextlib import ExitStack

F32, BF16, U32 = mybir.dt.float32, mybir.dt.bfloat16, mybir.dt.uint32
ALU, ACT, AX = mybir.AluOpType, mybir.ActivationFunctionType, mybir.AxisListType

P = 128
C = 128
B, N = 2, 512
TILES = N // P
T = B * N
H, D = 16, 8
MW = 4 * C
FC = MW // P
S = 32
E, TOP = 8, 2
CAP = 2 * 5 * T // (4 * E)
GROUPS = TOP * T // P
SLOTS = E * CAP
PAIRS = E // 2
PT = 2 * CAP // P
ROW = C + 1
BLK = N // D
EPS = 1e-5
ZW = SLOTS * ROW // P // TILES
NP1 = 4

EARLY = dict(ident=P, ln1_w=1, ln1_b=1, q_b=1, k_b=1, v_b=1, o_b=1, ln2_w=1, ln2_b=1, fc_b=FC, proj_b=1,
             qkv=3 * C, same_d=P, head_block=H * (2 * D - 1), same_h=P, block=D)
CONTEXT = dict(ctxT=B * TILES * S, Wk=C, Wv=C, WqT=C, bk=1, bq=1, bv=C, quad=TILES, w_g=E, tri=P, expert=E,
               row=GROUPS, slot=PAIRS * PT)
MLP = dict(fcT=MW, projT=FC * C)


def places(columns):
    at, out = 0, {}
    for name, n in columns.items():
        out[name] = (at, at + n)
        at += n
    return out, at


def constants():
    p = np.arange(P)
    d_of, h_of = p // H, p % H
    same_d = d_of[:, None] == d_of[None]
    head_block = np.zeros((P, 2 * D - 1, H))
    head_block[p, D - 1, h_of] = 1
    same_h = h_of[:, None] == h_of[None]
    block = d_of[:, None] == np.arange(D)[None]
    quad = (p // S)[:, None] == np.arange(TILES)[None]
    row = p[:, None] + P * np.arange(GROUPS)[None]
    slot = p[:, None] + P * np.arange(PAIRS * PT)[None]
    tables = dict(ident=np.eye(P), same_d=same_d, head_block=head_block, same_h=same_h, block=block, quad=quad,
                  tri=p[:, None] < p[None], expert=np.tile(np.arange(E), (P, 1)), row=row, slot=slot + TOP * T)
    return {k: np.asarray(v, np.float32).reshape(P, -1) for k, v in tables.items()}


def program(nc, x, early, context, wo_rot, mlp, c_fc, c_proj, out):
    at_early, n_early = places(EARLY)
    at_context, n_context = places(CONTEXT)
    at_mlp, n_mlp = places(MLP)
    ctx = ExitStack()
    with ctx:
        def sb(name, shape, dt=F32):
            return ctx.enter_context(nc.sbuf_tensor(name, shape, dt))

        def sem(name):
            return ctx.enter_context(nc.semaphore(name))

        v_twice = nc.dram_tensor("v_twice", (B, 2, P, N), F32, kind="Internal").ap()
        slots = nc.dram_tensor("slots", (SLOTS + TOP * T, ROW), F32, kind="Internal").ap()
        results = nc.dram_tensor("results", (TOP * T + SLOTS, C), F32, kind="Internal").ap()

        early_sb = sb("early_sb", [P, n_early])
        context_sb = sb("context_sb", [P, n_context])
        mlp_sb = sb("mlp_sb", [P, n_mlp])
        wo_sb = sb("wo_sb", [P, D, C])
        c_fc_sb = sb("c_fc_sb", [P, E, MW])
        c_proj_sb = sb("c_proj_sb", [P, E, FC, C])

        def par(name):
            for sbuf, at in ((early_sb, at_early), (context_sb, at_context), (mlp_sb, at_mlp)):
                if name in at:
                    return sbuf[:, at[name][0]:at[name][1]]
            raise KeyError(name)

        zeros = sb("zeros", [P, ZW])
        minus_half = sb("minus_half", [P, TILES])
        ones_row = sb("ones_row", [1, P])
        ones_bf = sb("ones_bf", [P, P], BF16)
        tri_bf = sb("tri_bf", [P, P], BF16)
        spread = sb("spread", [P, D, P])

        def per_chunk(name, shape, dt=F32):
            return [sb(f"{name}{c}", shape, dt) for c in range(B)]
        x_sb = per_chunk("x_sb", [P, TILES, C])
        xn = per_chunk("xn", [P, TILES, C])
        xnT = per_chunk("xnT", [P, N])
        stats = per_chunk("stats", [P, TILES, 6])
        mean_var = per_chunk("mean_var", [P, TILES, 2])
        var_eps = per_chunk("var_eps", [P, TILES])
        rstd = per_chunk("rstd", [P, TILES])
        k_exp = sb("k_exp", [P, N])
        q_exp = sb("q_exp", [P, N])
        k_relu = sb("k_relu", [P, N])
        q_relu = sb("q_relu", [P, N])
        kT = per_chunk("kT", [P, N])
        qT = per_chunk("qT", [P, N])
        qkT = per_chunk("qkT", [P, N])
        qnT = per_chunk("qnT", [P, N])
        vT = per_chunk("vT", [P, N])
        late = sb("late", [P, D, N])
        v_rot = late[:, 0:D - 1, :]
        got = [late[:, TOP * TILES * C // N * c:TOP * TILES * C // N * (c + 1), :]
               .rearrange("p k (a c) -> p k a c", a=TILES) for c in range(B)]
        norm = per_chunk("norm", [P, BLK])
        p1 = [sb(f"p1_{i}", [P, N]) for i in range(NP1)]
        p2 = [sb(f"p2_{i}", [P, N]) for i in range(NP1)]
        yT = per_chunk("yT", [P, N])
        x2 = per_chunk("x2", [P, TILES, C])
        xx2 = per_chunk("xx2", [P, TILES, C])
        hT = sb("hT", [P, FC, N])
        x3 = per_chunk("x3", [P, TILES, C])
        KT = sb("KT", [P, B * S])
        WqK = sb("WqK", [P, B * S])
        bqK = sb("bqK", [1, B * S])
        V4 = per_chunk("V4", [P, TILES, C])
        s_max = per_chunk("s_max", [P, TILES])
        s_sub = per_chunk("s_sub", [P, TILES, S])
        s_exp = per_chunk("s_exp", [P, TILES, S])
        s_sum = per_chunk("s_sum", [P, TILES])
        s_inv = per_chunk("s_inv", [P, TILES])
        expT = per_chunk("expT", [P, P])
        pay = [per_chunk(f"pay{k}_", [P, TILES, ROW]) for k in range(TOP)]
        logits = per_chunk("logits", [P, TILES, E])
        top_v = per_chunk("top_v", [P, TILES, 8])
        top_i = per_chunk("top_i", [P, TILES, 8], U32)
        gap = per_chunk("gap", [P, TILES])
        gap_exp = per_chunk("gap_exp", [P, TILES])
        one_plus = per_chunk("one_plus", [P, TILES])
        prob = sb("prob", [P, GROUPS])
        which = sb("which", [P, GROUPS])
        one_hot = sb("one_hot", [P, GROUPS, E], BF16)
        rank_all = sb("rank_all", [P, GROUPS, E])
        rank = sb("rank", [P, GROUPS])
        slot_of = sb("slot_of", [P, GROUPS])
        kept = sb("kept", [P, GROUPS])
        trash = sb("trash", [P, GROUPS])
        away = sb("away", [P, GROUPS])
        away_kept = sb("away_kept", [P, GROUPS])
        target = sb("target", [P, GROUPS], U32)
        weight = sb("weight", [P, GROUPS])
        rows_in = [sb(f"rows_in{i}", [P, PT, ROW]) for i in range(2)]
        send_to = sb("send_to", [P, PAIRS, PT], U32)
        inT = [sb(f"inT{i}", [P, 2 * CAP]) for i in range(2)]
        heT = [sb(f"heT{i}", [P, FC, CAP]) for i in range(2)]
        outT = [sb(f"outT{i}", [P, 2 * CAP]) for i in range(2)]
        rows_out = [sb(f"rows_out{i}", [P, PT, C]) for i in range(2)]

        bank = [ctx.enter_context(nc.psum_tensor(f"bank{i}", [P, 512], F32)) for i in range(8)]
        b_t, b_k, b_v, b_q, b_s, b_m0, b_m1, b_y = bank
        b_m = (b_m0, b_m1)
        y_scores, y_expT, y_logits = slice(0, P), slice(P, 2 * P), slice(2 * P, 2 * P + TILES * E)
        ranks = b_y[:, 384:512].rearrange("p (g e) -> p g e", e=E)

        names = """x_in early_in context_in wo_in mlp_in experts_in zero_slots zero_results v_stored
            pool_order dve_order act_order pool_consts
            ln1_var ln1_rstd ln1_done ln2_var ln2_rstd ln2_done post1_var post1_rstd post1_done
            post2_var post2_rstd post2_done post3_var post3_rstd post3_done
            ln1T xn1T_sb kT_mm vT_mm qT_mm k_parts q_parts v_sb k_sb q_sb k_sum qk_sb norm_mm norm_inv
            norm_spread qn_sb p1_ready kv_mm p2_ready y_step y_sb yT_back x2_sb xx2_sb ln2T xn2T_sb fc_mm h_sb
            proj_mm mlpT_sb mlp_back x3_sum x3T x3T_sb KT_mm KT_sb fold_mm fold_sb V_mm V4_sb
            scores_mm score_sub exp_sb expT_mm expT_sb attend_mm x4_sum x4T x4T_sb logits_mm logits_read
            gap_ready gap_exp_sb hot_ready ranks_mm ranks_read pay1_sb targets slots_sent
            in_tr in_sb fce_mm he_sb proje_mm oute_sb out_tr out_sb send_ready out_stored"""
        s = {name: sem(name) for name in names.split()}
        v_back = [sem(f"v_back{i}") for i in range(3)]
        results_sent = [sem(f"results_sent{i}") for i in range(2)]
        rows_loaded = [sem(f"rows_loaded{i}") for i in range(2)]
        got_in = [sem(f"got_in{c}") for c in range(B)]
        V_PARTS = ((1, 3), (3, 5), (5, 8))

        class Order:

            def __init__(self, eng, semaphore):
                self.eng, self.sem, self.n = eng, semaphore, 0

            def __call__(self, ins):
                self.n += 1
                ins.then_inc(self.sem, 1)
                return ins

            def wait(self):
                self.eng.wait_ge(self.sem, self.n)

        block = ctx.enter_context(nc.Block())

        @block.sync
        def _(sp):
            sp.dma_start(x_sb[0][:, :, :], x[0].rearrange("(a p) c -> p a c", p=P)).then_inc(s["x_in"], 16)
            sp.dma_start(early_sb[:, :], early).then_inc(s["early_in"], 16)
            sp.dma_start(context_sb[:, :], context).then_inc(s["context_in"], 16)
            sp.wait_ge(s["x_in"], 16)
            sp.dma_start(x_sb[1][:, :, :], x[1].rearrange("(a p) c -> p a c", p=P)).then_inc(s["x_in"], 16)
            sp.dma_start(wo_sb[:, :, :], wo_rot).then_inc(s["wo_in"], 16)
            for c in range(B):
                sp.wait_ge(s["v_sb"], c + 1)
                sp.dma_start(v_twice[c].rearrange("r p t -> p r t"),
                             vT[c][:, :].unsqueeze(1).to_broadcast((P, 2, N))).then_inc(s["v_stored"], 16)
                sp.wait_ge(s["v_stored"], 16 * (c + 1))
                if c:
                    sp.wait_ge(s["p1_ready"], D * c)
                rows = v_twice[c].rearrange("r p t -> (r p) t")
                for i, (j0, j1) in enumerate(V_PARTS):
                    windows = rows[H * j0:H * j0 + P, :].unsqueeze(1)
                    windows = bass.AP(windows.tensor, windows.offset, [[N, P], [H * N, j1 - j0], [1, N]])
                    sp.dma_start(v_rot[:, j0 - 1:j1 - 1, :], windows).then_inc(v_back[i], 16)
                if c == 0:
                    sp.dma_start(mlp_sb[:, :], mlp).then_inc(s["mlp_in"], 16)
                    sp.wait_ge(s["pool_consts"], 1)
                    for dst, name in ((slots[0:SLOTS, :], "zero_slots"), (results[0:TOP * T, :], "zero_results")):
                        n = dst.shape[0] // P // TILES * dst.shape[1]
                        sp.dma_start(dst.rearrange("(p n i) r -> p n (i r)", p=P, n=TILES),
                                     zeros[:, 0:n].unsqueeze(1).to_broadcast((P, TILES, n))).then_inc(s[name], 16)
            for e in range(0, E, 2):
                sp.dma_start(c_fc_sb[:, e:e + 2, :], c_fc[:, e:e + 2, :]).then_inc(s["experts_in"], 16)
                sp.dma_start(c_proj_sb[:, e:e + 2, :, :], c_proj[:, e:e + 2, :, :]).then_inc(s["experts_in"], 16)
            sp.wait_ge(s["slots_sent"], 16 * GROUPS)
            for w in range(PAIRS):
                if w >= 2:
                    sp.wait_ge(s["in_tr"], 2 * (w - 1))
                    sp.wait_ge(s["send_ready"], w - 1)
                sp.dma_start(rows_in[w % 2][:, :, :],
                             slots[PT * P * w:PT * P * (w + 1), :].rearrange("(i p) r -> p i r", p=P))\
                  .then_inc(rows_loaded[w % 2], 16)
            for i in range(2):
                sp.wait_ge(results_sent[i], 16 * PT * PAIRS // 2)
            by_token = results[0:TOP * T, :].rearrange("(k c a p) r -> c k p a r", k=TOP, c=B, p=P)
            for c in range(B):
                for k in range(TOP):
                    sp.dma_start(got[c][:, k, :, :], by_token[c, k]).then_inc(got_in[c], 16)
            for c in range(B):
                sp.wait_ge(s["post3_done"], TILES * (c + 1))
                sp.dma_start(out[c].rearrange("(a p) c -> p a c", p=P), xn[c][:, :, :]).then_inc(s["out_stored"], 16)
            sp.wait_ge(s["out_stored"], 16 * B)

        @block.gpsimd
        def _(pool):
            order = Order(pool, s["pool_order"])
            order(nc.gpsimd.memset(minus_half[:, :], -0.5))
            order.wait()

            def rstd_of(name, c):
                pool.wait_ge(s[f"{name}_var"], c + 1)
                nc.gpsimd.tensor_tensor(rstd[c][:, :], var_eps[c][:, :], minus_half[:, :], ALU.pow)\
                  .then_inc(s[f"{name}_rstd"], 1)

            rstd_of("ln1", 0)
            order(nc.gpsimd.memset(ones_row[:, :], 1.0))
            order(nc.gpsimd.memset(ones_bf[:, :], 1.0))
            pool.wait_ge(s["early_in"], 16)
            for blk in range(D):
                order(nc.gpsimd.tensor_scalar(spread[:, blk, :], par("same_h"), par("block")[:, blk:blk + 1], None,
                                              ALU.mult))
            pool.wait_ge(s["context_in"], 16)
            order(nc.gpsimd.tensor_copy(tri_bf[:, :], par("tri")))
            order(nc.gpsimd.tensor_scalar(trash[:, :], par("row"), float(SLOTS), None, ALU.add))
            rstd_of("ln1", 1)
            order.wait()
            nc.gpsimd.memset(zeros[:, :], 0.0).then_inc(s["pool_consts"], 1)

            def product(c, j):
                n = D * c + j
                if j == 0:
                    pool.wait_ge(s["k_sb"], c + 1)
                    pool.wait_ge(s["v_sb"], c + 1)
                for i, (j0, _) in enumerate(V_PARTS):
                    if j == j0:
                        pool.wait_ge(v_back[i], 16 * (c + 1))
                if n >= NP1:
                    pool.wait_ge(s["kv_mm"], n - NP1 + 1)
                v = vT[c][:, :] if j == 0 else v_rot[:, j - 1, :]
                nc.gpsimd.tensor_tensor(p1[n % NP1][:, :], kT[c][:, :], v, ALU.mult).then_inc(s["p1_ready"], 1)

            def twice_residual(c):
                pool.wait_ge(s["x2_sb"], c + 1)
                nc.gpsimd.tensor_tensor(xx2[c][:, :, :], x_sb[c][:, :, :], x2[c][:, :, :], ALU.add)\
                  .then_inc(s["xx2_sb"], 1)

            for j in range(D):
                product(0, j)
            for j in range(D):
                product(1, j)
                if j == 4:
                    rstd_of("ln2", 0)
            twice_residual(0)
            rstd_of("ln2", 1)
            twice_residual(1)
            rstd_of("post1", 0)
            rstd_of("post2", 0)
            rstd_of("post1", 1)
            pool.wait_ge(s["zero_slots"], 16)

            def send(group):
                k, c, a = group // (B * TILES), group // TILES % B, group % TILES
                pool.indirect_dma_start(slots, bass.IndirectOffsetOnAxis(ap=target[:, group:group + 1], axis=0),
                                        pay[k][c][:, a, :], None).then_inc(s["slots_sent"], 16)

            pool.wait_ge(s["targets"], 1)
            for g in range(TILES):
                send(g)
            rstd_of("post2", 1)
            pool.wait_ge(s["targets"], 2)
            for g in range(TILES, GROUPS):
                send(g)
            pool.wait_ge(s["zero_results"], 16)
            for w in range(PAIRS):
                pool.wait_ge(s["send_ready"], w + 1)
                pool.wait_ge(s["out_sb"], 2 * (w + 1))
                for i in range(PT):
                    pool.indirect_dma_start(results, bass.IndirectOffsetOnAxis(ap=send_to[:, w, i:i + 1], axis=0),
                                            rows_out[w % 2][:, i, :], None).then_inc(results_sent[w % 2], 16)
            rstd_of("post3", 0)
            rstd_of("post3", 1)

        @block.scalar
        def _(act):
            order = Order(act, s["act_order"])
            A = nc.scalar.activation

            def col(name, i=0):
                return par(name)[:, i:i + 1]

            def heads(c):
                act.wait_ge(s["ln1T"], c + 1)
                if c == 0:
                    act.wait_ge(s["early_in"], 16)
                if c:
                    act.wait_ge(s["qT_mm"], c)
                A(xnT[c][:, :], b_t[:, :], ACT.Identity, bias=col("ln1_b"), scale=col("ln1_w")).then_inc(s["xn1T_sb"], 1)
                act.wait_ge(s["kT_mm"], c + 1)
                if c:
                    act.wait_ge(s["q_sb"], c)
                A(k_exp[:, :], b_k[:, :], ACT.Exp, bias=col("k_b")).then_inc(s["k_parts"], 1)
                A(k_relu[:, :], b_k[:, :], ACT.Relu, bias=col("k_b")).then_inc(s["k_parts"], 1)
                act.wait_ge(s["vT_mm"], c + 1)
                A(vT[c][:, :], b_v[:, :], ACT.Identity, bias=col("v_b")).then_inc(s["v_sb"], 1)
                act.wait_ge(s["qT_mm"], c + 1)
                A(q_exp[:, :], b_q[:, :], ACT.Exp, bias=col("q_b")).then_inc(s["q_parts"], 1)
                A(q_relu[:, :], b_q[:, :], ACT.Relu, bias=col("q_b")).then_inc(s["q_parts"], 1)

            def y_out(c):
                act.wait_ge(s["y_step"], D * (c + 1))
                A(yT[c][:, :], b_y[:, :], ACT.Identity, bias=col("o_b")).then_inc(s["y_sb"], 1)

            def ln2_in(c):
                act.wait_ge(s["ln2T"], c + 1)
                A(xnT[c][:, :], b_t[:, :], ACT.Identity, bias=col("ln2_b"), scale=col("ln2_w")).then_inc(s["xn2T_sb"], 1)

            def gelus(c):
                for f in range(FC):
                    act.wait_ge(s["fc_mm"], FC * c + f + 1)
                    if c:
                        act.wait_ge(s["proj_mm"], c)
                    A(hT[:, f, :], (b_k, b_v, b_q, b_s)[f][:, :], ACT.Gelu, bias=col("fc_b", f)).then_inc(s["h_sb"], 1)

            def mlp_out(c):
                act.wait_ge(s["proj_mm"], c + 1)
                A(yT[c][:, :], b_m[c][:, :], ACT.Identity, bias=col("proj_b")).then_inc(s["mlpT_sb"], 1)

            def cross_in(c):
                act.wait_ge(s["x3T"], c + 1)
                A(xnT[c][:, :], b_t[:, :], ACT.Copy).then_inc(s["x3T_sb"], 1)

            def cross_exp(c):
                act.wait_ge(s["score_sub"], c + 1)
                A(s_exp[c][:, :, :], s_sub[c][:, :, :], ACT.Exp, scale=float(C) ** -0.5).then_inc(s["exp_sb"], 1)
                act.wait_ge(s["expT_mm"], c + 1)
                A(expT[c][:, :], b_y[:, y_expT], ACT.Copy).then_inc(s["expT_sb"], 1)

            def route_in(c):
                act.wait_ge(s["x4T"], c + 1)
                A(xnT[c][:, :], b_t[:, :], ACT.Copy).then_inc(s["x4T_sb"], 1)
                A(pay[1][c][:, :, 0:C], pay[0][c][:, :, 0:C], ACT.Copy).then_inc(s["pay1_sb"], 1)

            def route_exp(c):
                act.wait_ge(s["gap_ready"], c + 1)
                A(gap_exp[c][:, :], gap[c][:, :], ACT.Exp).then_inc(s["gap_exp_sb"], 1)

            act.wait_ge(s["KT_mm"], 1)
            A(KT[:, :], b_s[:, 0:B * S], ACT.Identity, bias=col("bk")).then_inc(s["KT_sb"], 1)
            act.wait_ge(s["fold_mm"], 1)
            A(WqK[:, :], b_s[:, B * S:2 * B * S], ACT.Copy).then_inc(s["fold_sb"], 1)
            A(bqK[:, :], b_s[0:1, 2 * B * S:3 * B * S], ACT.Copy).then_inc(s["fold_sb"], 1)
            act.wait_ge(s["V_mm"], 1)
            for b in range(B):
                for a in range(TILES):
                    A(V4[b][:, a, :], b_m0[:, C * b:C * (b + 1)], ACT.Copy, scale=col("quad", a)).then_inc(s["V4_sb"], 1)
            heads(0)
            heads_1 = lambda: heads(1)
            y_out_0 = lambda: y_out(0)
            y_out_0()
            heads_1()
            ln2_in(0)
            gelus(0)
            y_out(1)
            mlp_out(0)
            ln2_in(1)
            gelus(1)
            cross_in(0)
            cross_exp(0)
            mlp_out(1)
            route_in(0)
            route_exp(0)
            cross_in(1)
            cross_exp(1)
            route_in(1)
            route_exp(1)
            for e in range(E):
                for f in range(FC):
                    n = FC * e + f
                    act.wait_ge(s["fce_mm"], n + 1)
                    if e >= 2 and f == 0:
                        act.wait_ge(s["proje_mm"], e - 1)
                    A(heT[e % 2][:, f, :], (b_k, b_v, b_q)[n % 3][:, 0:CAP], ACT.Gelu).then_inc(s["he_sb"], 1)

        @block.vector
        def _(dve):
            order = Order(dve, s["dve_order"])
            V = nc.vector

            def normalise(name, c, src, dst):
                for a in range(TILES):
                    order(V.bn_stats(stats[c][:, a, :], src[:, a, :]))
                order.wait()
                for a in range(TILES):
                    order(V.bn_aggr(mean_var[c][:, a, :], stats[c][:, a, :]))
                order.wait()
                V.tensor_scalar(var_eps[c][:, :], mean_var[c][:, :, 1], EPS, None, ALU.add)\
                 .then_inc(s[f"{name}_var"], 1)

            def scale(name, c, src, dst):
                dve.wait_ge(s[f"{name}_rstd"], c + 1)
                for a in range(TILES):
                    V.tensor_scalar(dst[:, a, 0:C], src[:, a, :], mean_var[c][:, a, 0:1], rstd[c][:, a:a + 1],
                                    ALU.subtract, ALU.mult).then_inc(s[f"{name}_done"], 1)

            def elu(c):
                dve.wait_ge(s["k_parts"], 2 * (c + 1))
                V.scalar_tensor_tensor(out=kT[c][:, :], in0=k_exp[:, :], scalar=1.0, in1=k_relu[:, :],
                                       op0=ALU.min, op1=ALU.add).then_inc(s["k_sb"], 1)
                dve.wait_ge(s["q_parts"], 2 * (c + 1))
                V.scalar_tensor_tensor(out=qT[c][:, :], in0=q_exp[:, :], scalar=1.0, in1=q_relu[:, :],
                                       op0=ALU.min, op1=ALU.add).then_inc(s["q_sb"], 1)

            def normalisers(c):
                dve.wait_ge(s["q_sb"], c + 1)
                dve.wait_ge(s["k_sum"], c + 1)
                V.tensor_tensor(qkT[c][:, :], qT[c][:, :], b_s[:, :], ALU.mult).then_inc(s["qk_sb"], 1)
                dve.wait_ge(s["norm_mm"], c + 1)
                V.reciprocal(norm[c][:, :], b_t[:, 0:BLK]).then_inc(s["norm_inv"], 1)
                dve.wait_ge(s["norm_spread"], c + 1)
                V.tensor_tensor(qnT[c][:, :], qT[c][:, :], b_s[:, :], ALU.mult).then_inc(s["qn_sb"], 1)

            def second(c, j):
                n = D * c + j
                if j == 0:
                    dve.wait_ge(s["qn_sb"], c + 1)
                dve.wait_ge(s["kv_mm"], n + 1)
                if n >= NP1:
                    dve.wait_ge(s["y_step"], n - NP1 + 1)
                V.tensor_tensor(p2[n % NP1][:, :], qnT[c][:, :], b_m[n % 2][:, :], ALU.mult).then_inc(s["p2_ready"], 1)

            def attended(c):
                dve.wait_ge(s["yT_back"], c + 1)
                flat = "p a c -> p (a c)"
                V.tensor_tensor(x2[c][:, :, :].rearrange(flat), x_sb[c][:, :, :].rearrange(flat), b_t[:, :], ALU.add)\
                 .then_inc(s["x2_sb"], 1)
                dve.wait_ge(s["x2_sb"], c + 1)
                normalise("ln2", c, x2[c], xn[c])

            def mlp_added(c):
                dve.wait_ge(s["mlp_back"], c + 1)
                dve.wait_ge(s["xx2_sb"], c + 1)
                flat = "p a c -> p (a c)"
                V.tensor_tensor(x2[c][:, :, :].rearrange(flat), xx2[c][:, :, :].rearrange(flat), b_t[:, :], ALU.add)\
                 .then_inc(s["x3_sum"], 1)
                dve.wait_ge(s["x3_sum"], c + 1)
                normalise("post1", c, x2[c], x3[c])

            def softmax_in(c):
                dve.wait_ge(s["scores_mm"], c + 1)
                scores = b_y[:, y_scores].rearrange("p (a k) -> p a k", k=S)
                order(V.tensor_reduce(s_max[c][:, :], scores, AX.X, ALU.max))
                order.wait()
                V.tensor_tensor(s_sub[c][:, :, :], scores, s_max[c][:, :].unsqueeze(2).to_broadcast((P, TILES, S)),
                                ALU.subtract).then_inc(s["score_sub"], 1)

            def cross_added(c):
                dve.wait_ge(s["exp_sb"], c + 1)
                order(V.tensor_reduce(s_sum[c][:, :], s_exp[c][:, :, :], AX.X, ALU.add))
                order.wait()
                order(V.reciprocal(s_inv[c][:, :], s_sum[c][:, :]))
                order.wait()
                dve.wait_ge(s["attend_mm"], c + 1)
                dve.wait_ge(s["post1_done"], TILES * (c + 1))
                for a in range(TILES):
                    V.scalar_tensor_tensor(out=x2[c][:, a, :], in0=b_m[c][:, C * a:C * (a + 1)], scalar=s_inv[c][:, a:a + 1],
                                           in1=x3[c][:, a, :], op0=ALU.mult, op1=ALU.add).then_inc(s["x4_sum"], 1)
                dve.wait_ge(s["x4_sum"], TILES * (c + 1))
                normalise("post2", c, x2[c], pay[0][c])

            def choose(c):
                dve.wait_ge(s["logits_mm"], c + 1)
                V.tensor_copy(logits[c][:, :, :], b_y[:, y_logits].rearrange("p (a e) -> p a e", e=E))\
                 .then_inc(s["logits_read"], 1)
                dve.wait_ge(s["logits_read"], c + 1)
                for a in range(TILES):
                    order(V.max(top_v[c][:, a, :], logits[c][:, a, :]))
                order.wait()
                V.tensor_tensor(gap[c][:, :], top_v[c][:, :, 1], top_v[c][:, :, 0], ALU.subtract)\
                 .then_inc(s["gap_ready"], 1)
                for a in range(TILES):
                    order(V.max_index(top_i[c][:, a, :], top_v[c][:, a, :], logits[c][:, a, :]))
                order.wait()
                for k in range(TOP):
                    g = slice((B * k + c) * TILES, (B * k + c + 1) * TILES)
                    order(V.tensor_copy(which[:, g], top_i[c][:, :, k]))
                order.wait()
                for k in range(TOP):
                    g = slice((B * k + c) * TILES, (B * k + c + 1) * TILES)
                    last = V.tensor_tensor(one_hot[:, g, :], which[:, g].unsqueeze(2).to_broadcast((P, TILES, E)),
                                           par("expert").unsqueeze(1).to_broadcast((P, TILES, E)), ALU.is_equal)
                    last.then_inc(s["hot_ready"], 1)
                dve.wait_ge(s["gap_exp_sb"], c + 1)
                order(V.tensor_scalar(one_plus[c][:, :], gap_exp[c][:, :], 1.0, None, ALU.add))
                order.wait()
                order(V.reciprocal(prob[:, TILES * c:TILES * (c + 1)], one_plus[c][:, :]))
                order.wait()
                order(V.tensor_tensor(prob[:, TILES * (B + c):TILES * (B + c + 1)], gap_exp[c][:, :],
                                      prob[:, TILES * c:TILES * (c + 1)], ALU.mult))

            def places_of(stage, g0, g1):
                g, n = slice(g0, g1), g1 - g0
                dve.wait_ge(s["ranks_mm"], stage + 1)
                dve.wait_ge(s["hot_ready"], TOP * (stage + 1))
                V.tensor_tensor(rank_all[:, g, :], ranks[:, g, :], one_hot[:, g, :], ALU.mult)\
                 .then_inc(s["ranks_read"], 1)
                dve.wait_ge(s["ranks_read"], stage + 1)
                order(V.tensor_reduce(rank[:, g], rank_all[:, g, :], AX.X, ALU.add))
                order.wait()
                order(V.scalar_tensor_tensor(out=slot_of[:, g], in0=which[:, g], scalar=float(CAP), in1=rank[:, g],
                                             op0=ALU.mult, op1=ALU.add))
                order(V.tensor_scalar(kept[:, g], rank[:, g], float(CAP), None, ALU.is_lt))
                order.wait()
                order(V.tensor_tensor(away[:, g], slot_of[:, g], trash[:, g], ALU.subtract))
                for k in range(TOP):
                    for c in range(B):
                        q0 = (B * k + c) * TILES
                        if g0 <= q0 < g1:
                            if k:
                                dve.wait_ge(s["pay1_sb"], c + 1)
                            qs = slice(q0, q0 + TILES)
                            order(V.scalar_tensor_tensor(out=pay[k][c][:, :, C], in0=par("row")[:, qs], scalar=float(-TOP * T),
                                                         in1=slot_of[:, qs], op0=ALU.add, op1=ALU.subtract))
                order.wait()
                order(V.tensor_tensor(away_kept[:, g], away[:, g], kept[:, g], ALU.mult))
                order(V.tensor_tensor(weight[:, g], prob[:, g], kept[:, g], ALU.mult))
                order.wait()
                V.tensor_tensor(target[:, g], away_kept[:, g], trash[:, g], ALU.add).then_inc(s["targets"], 1)

            dve.wait_ge(s["x_in"], 16)
            normalise("ln1", 0, x_sb[0], xn[0])
            scale("ln1", 0, x_sb[0], xn[0])
            dve.wait_ge(s["x_in"], 32)
            normalise("ln1", 1, x_sb[1], xn[1])
            scale("ln1", 1, x_sb[1], xn[1])
            elu(0)
            normalisers(0)
            for j in range(D):
                second(0, j)
            elu(1)
            normalisers(1)
            dve.wait_ge(s["ln1T"], 2)
            for j in range(D):
                second(1, j)
                if j == 1:
                    attended(0)
                if j == 4:
                    scale("ln2", 0, x2[0], xn[0])
            attended(1)
            scale("ln2", 1, x2[1], xn[1])
            mlp_added(0)
            scale("post1", 0, x2[0], x3[0])
            softmax_in(0)
            cross_added(0)
            scale("post2", 0, x2[0], pay[0][0])
            mlp_added(1)
            scale("post1", 1, x2[1], x3[1])
            choose(0)
            dve.wait_ge(s["context_in"], 16)
            order.wait()
            places_of(0, 0, TILES)
            softmax_in(1)
            cross_added(1)
            scale("post2", 1, x2[1], pay[0][1])
            choose(1)
            order.wait()
            places_of(1, TILES, GROUPS)

            def take_in(w):
                for i, (src, n0, n1) in enumerate(((b_t, 0, 3), (b_s, 3, PT))):
                    dve.wait_ge(s["in_tr"], 2 * w + i + 1)
                    if w >= 2 and i == 0:
                        dve.wait_ge(s["fce_mm"], FC * 2 * (w - 1))
                    V.tensor_copy(inT[w % 2][:, P * n0:P * n1], src[:, 0:P * (n1 - n0)]).then_inc(s["in_sb"], 1)
                dve.wait_ge(rows_loaded[w % 2], 16 * (w // 2 + 1))
                V.tensor_tensor(send_to[:, w, :], rows_in[w % 2][:, :, C],
                                par("slot")[:, PT * w:PT * (w + 1)], ALU.add).then_inc(s["send_ready"], 1)

            def expert_out(e):
                w = e // 2
                dve.wait_ge(s["proje_mm"], e + 1)
                if w >= 2 and e % 2 == 0:
                    dve.wait_ge(s["out_tr"], 2 * (w - 1))
                V.tensor_copy(outT[w % 2][:, CAP * (e % 2):CAP * (e % 2 + 1)], b_y[:, 0:CAP]).then_inc(s["oute_sb"], 1)

            def hand_out(w):
                for i, (src, n0, n1) in enumerate(((b_m0, 0, 3), (b_m1, 3, PT))):
                    dve.wait_ge(s["out_tr"], 2 * w + i + 1)
                    if w >= 2 and i == 0:
                        dve.wait_ge(results_sent[w % 2], 16 * PT * (w // 2))
                    V.tensor_copy(rows_out[w % 2][:, n0:n1, :],
                                  src[:, 0:P * (n1 - n0)].rearrange("p (i c) -> p i c", c=C)).then_inc(s["out_sb"], 1)

            take_in(0)
            for w in range(PAIRS):
                if w + 1 < PAIRS:
                    take_in(w + 1)
                expert_out(2 * w)
                expert_out(2 * w + 1)
                hand_out(w)
            for c in range(B):
                dve.wait_ge(got_in[c], 16 * TOP)
                for k in range(TOP):
                    for a in range(TILES):
                        g = TILES * (B * k + c) + a
                        order(V.scalar_tensor_tensor(out=x2[c][:, a, :], in0=got[c][:, k, a, :], scalar=weight[:, g:g + 1],
                                                     in1=pay[0][c][:, a, 0:C] if k == 0 else x2[c][:, a, :],
                                                     op0=ALU.mult, op1=ALU.add))
                    order.wait()
                normalise("post3", c, x2[c], xn[c])
            for c in range(B):
                scale("post3", c, x2[c], xn[c])

        @block.tensor
        def _(pe):
            M, TR = nc.tensor.matmul, nc.tensor.transpose
            ident = par("ident")

            def turn(dst, tiles, signal):
                for a in range(TILES):
                    last = TR(dst[:, P * a:P * (a + 1)], tiles(a), ident)
                last.then_inc(signal, 1)

            def ln1_in(c):
                for a in range(TILES):
                    pe.wait_ge(s["ln1_done"], TILES * c + a + 1)
                    if a == 0:
                        pe.wait_ge(s["early_in"], 16)
                        if c:
                            pe.wait_ge(s["norm_inv"], c)
                    last = TR(b_t[:, P * a:P * (a + 1)], xn[c][:, a, :], ident)
                last.then_inc(s["ln1T"], 1)

            def project(c):
                pe.wait_ge(s["xn1T_sb"], c + 1)
                if c:
                    pe.wait_ge(s["k_parts"], 2 * c)
                    pe.wait_ge(s["v_sb"], c)
                    pe.wait_ge(s["q_parts"], 2 * c)
                w = par("qkv")
                M(b_k[:, :], w[:, C:2 * C], xnT[c][:, :], start=True, stop=True).then_inc(s["kT_mm"], 1)
                M(b_v[:, :], w[:, 2 * C:3 * C], xnT[c][:, :], start=True, stop=True).then_inc(s["vT_mm"], 1)
                M(b_q[:, :], w[:, 0:C], xnT[c][:, :], start=True, stop=True).then_inc(s["qT_mm"], 1)

            def kv(c, j):
                n = D * c + j
                pe.wait_ge(s["p1_ready"], n + 1)
                if n >= 2:
                    pe.wait_ge(s["p2_ready"], n - 1)
                elif n == 0:
                    pe.wait_ge(s["V4_sb"], B * TILES)
                M(b_m[n % 2][:, :], par("same_d"), p1[n % NP1][:, :], start=True, stop=True).then_inc(s["kv_mm"], 1)

            def y_part(c, j):
                n = D * c + j
                pe.wait_ge(s["p2_ready"], n + 1)
                if n == 0:
                    pe.wait_ge(s["wo_in"], 16)
                if j == 0 and c:
                    pe.wait_ge(s["y_sb"], c)
                M(b_y[:, :], wo_sb[:, j, :], p2[n % NP1][:, :], start=(j == 0), stop=(j == D - 1)).then_inc(s["y_step"], 1)

            def head_sums(c):
                pe.wait_ge(s["k_sb"], c + 1)
                if c:
                    pe.wait_ge(s["qn_sb"], c)
                else:
                    pe.wait_ge(s["fold_sb"], 2)
                M(b_s[:, :], par("same_d"), kT[c][:, :], start=True, stop=True).then_inc(s["k_sum"], 1)

            def norm_sums(c):
                pe.wait_ge(s["qk_sb"], c + 1)
                marks = par("head_block")
                for b in range(D):
                    last = M(b_t[:, 0:BLK], marks[:, H * (D - 1 - b):H * (2 * D - 1 - b)], qkT[c][:, BLK * b:BLK * (b + 1)],
                             start=(b == 0), stop=(b == D - 1))
                last.then_inc(s["norm_mm"], 1)

            def norm_back(c):
                pe.wait_ge(s["norm_inv"], c + 1)
                if c == 0:
                    pe.wait_ge(s["pool_consts"], 1)
                for b in range(D):
                    last = M(b_s[:, BLK * b:BLK * (b + 1)], spread[:, b, :], norm[c][:, :], start=True, stop=True)
                last.then_inc(s["norm_spread"], 1)

            def y_back(c):
                pe.wait_ge(s["y_sb"], c + 1)
                if c == 0:
                    pe.wait_ge(s["norm_inv"], 2)
                else:
                    pe.wait_ge(s["xn2T_sb"], 1)
                turn(b_t, lambda a: yT[c][:, P * a:P * (a + 1)], s["yT_back"])

            def ln2_in(c):
                pe.wait_ge(s["x2_sb"], c + 1)
                if c:
                    pe.wait_ge(s["x3_sum"], 1)
                pe.wait_ge(s["ln2_done"], TILES * (c + 1))
                turn(b_t, lambda a: xn[c][:, a, :], s["ln2T"])

            def fc(c):
                pe.wait_ge(s["xn2T_sb"], c + 1)
                if c == 0:
                    pe.wait_ge(s["mlp_in"], 16)
                    pe.wait_ge(s["k_parts"], 2 * B)
                    pe.wait_ge(s["v_sb"], B)
                    pe.wait_ge(s["q_parts"], 2 * B)
                    pe.wait_ge(s["qn_sb"], B)
                for f in range(FC):
                    if c:
                        pe.wait_ge(s["h_sb"], FC * (c - 1) + f + 1)
                    M((b_k, b_v, b_q, b_s)[f][:, :], par("fcT")[:, P * f:P * (f + 1)], xnT[c][:, :], start=True, stop=True)\
                        .then_inc(s["fc_mm"], 1)

            def proj(c):
                if c == 0:
                    pe.wait_ge(s["p2_ready"], B * D)
                for f in range(FC):
                    pe.wait_ge(s["h_sb"], FC * c + f + 1)
                    last = M(b_m[c][:, :], par("projT")[:, C * f:C * (f + 1)], hT[:, f, :], start=(f == 0), stop=(f == FC - 1))
                last.then_inc(s["proj_mm"], 1)

            def mlp_back(c):
                pe.wait_ge(s["mlpT_sb"], c + 1)
                pe.wait_ge(s["x2_sb"], 2)
                if c:
                    pe.wait_ge(s["x3T_sb"], 1)
                turn(b_t, lambda a: yT[c][:, P * a:P * (a + 1)], s["mlp_back"])

            def cross_scores(c):
                pe.wait_ge(s["post1_done"], TILES * (c + 1))
                if c == 0:
                    pe.wait_ge(s["xn2T_sb"], 2)
                else:
                    pe.wait_ge(s["x4T_sb"], 1)
                    pe.wait_ge(s["x3_sum"], 2)
                turn(b_t, lambda a: x3[c][:, a, :], s["x3T"])

            def cross_scores_mm(c):
                pe.wait_ge(s["x3T_sb"], c + 1)
                if c == 0:
                    pe.wait_ge(s["y_sb"], B)
                else:
                    pe.wait_ge(s["ranks_read"], c)
                keys = slice(S * c, S * (c + 1))
                M(b_y[:, y_scores], ones_row[:, :], bqK[:, keys].unsqueeze(1).to_broadcast((1, TILES, S)), start=True,
                  stop=False)
                for a in range(TILES):
                    last = M(b_y[:, S * a:S * (a + 1)], xnT[c][:, P * a:P * (a + 1)], WqK[:, keys], start=False,
                             stop=(a == TILES - 1))
                last.then_inc(s["scores_mm"], 1)

            def cross_attend(c):
                pe.wait_ge(s["exp_sb"], c + 1)
                if c:
                    pe.wait_ge(s["expT_sb"], c)
                TR(b_y[:, y_expT], s_exp[c][:, :, :].rearrange("p a k -> p (a k)"), ident).then_inc(s["expT_mm"], 1)
                pe.wait_ge(s["expT_sb"], c + 1)
                pe.wait_ge(s["mlpT_sb"], c + 1)
                M(b_m[c][:, :], expT[c][:, :], V4[c][:, :, :].rearrange("p a c -> p (a c)"), start=True, stop=True)\
                    .then_inc(s["attend_mm"], 1)

            def route(c):
                pe.wait_ge(s["post2_done"], TILES * (c + 1))
                if c == 0:
                    pe.wait_ge(s["x3_sum"], 1)
                else:
                    pe.wait_ge(s["x3T_sb"], 2)
                turn(b_t, lambda a: pay[0][c][:, a, 0:C], s["x4T"])
                pe.wait_ge(s["x4T_sb"], c + 1)
                if c:
                    pe.wait_ge(s["logits_read"], c)
                for a in range(TILES):
                    last = M(b_y[:, 2 * P + E * a:2 * P + E * (a + 1)], xnT[c][:, P * a:P * (a + 1)], par("w_g"),
                             start=True, stop=True)
                last.then_inc(s["logits_mm"], 1)

            def count(stage, g0, g1):
                pe.wait_ge(s["hot_ready"], TOP * (stage + 1))
                M(ranks[:, g0:g1, :], tri_bf[:, :], one_hot[:, g0:g1, :], start=True, stop=False)
                for g in range(g1 - 1):
                    to = max(g + 1, g0)
                    last = M(ranks[:, to:g1, :], ones_bf[:, :], one_hot[:, g:g + 1, :].to_broadcast((P, g1 - to, E)),
                             start=False, stop=(g == g1 - 2))
                last.then_inc(s["ranks_mm"], 1)

            pe.wait_ge(s["context_in"], 16)
            M(b_s[:, 0:B * S], par("Wk"), par("ctxT").rearrange("p (b a k) -> p b a k", b=B, a=TILES)[:, :, 0, :], start=True, stop=True).then_inc(s["KT_mm"], 1)
            pe.wait_ge(s["pool_order"], 3)
            for b in range(B):
                M(b_m0[:, C * b:C * (b + 1)],
                  par("ctxT")[:, P * b:P * (b + 1)], par("Wv"),
                  start=True, stop=False)
                last = M(b_m0[:, C * b:C * (b + 1)], ones_row[:, :], par("bv")[0:1, :], start=False, stop=True)
            last.then_inc(s["V_mm"], 1)
            pe.wait_ge(s["KT_sb"], 1)
            M(b_s[:, B * S:2 * B * S], par("WqT"), KT[:, :], start=True, stop=True)
            M(b_s[0:1, 2 * B * S:3 * B * S], par("bq"), KT[:, :], start=True, stop=True).then_inc(s["fold_mm"], 1)

            ln1_in(0)
            project(0)
            head_sums(0)
            kv(0, 0)
            norm_sums(0)
            kv(0, 1)
            norm_back(0)
            for j in range(D):
                y_part(0, j)
                if j + 2 < D:
                    kv(0, j + 2)
                if j == D - 3:
                    ln1_in(1)
            project(1)
            head_sums(1)
            kv(1, 0)
            norm_sums(1)
            kv(1, 1)
            norm_back(1)
            for j in range(D):
                y_part(1, j)
                if j + 2 < D:
                    kv(1, j + 2)
                if j == 0:
                    y_back(0)
                if j == D - 2:
                    ln2_in(0)
            fc(0)
            y_back(1)
            proj(0)
            mlp_back(0)
            ln2_in(1)
            fc(1)
            cross_scores(0)
            cross_scores_mm(0)
            proj(1)
            cross_attend(0)
            route(0)
            mlp_back(1)
            pe.wait_ge(s["pool_consts"], 1)
            count(0, 0, TILES)
            cross_scores(1)
            cross_scores_mm(1)
            cross_attend(1)
            route(1)
            pe.wait_ge(s["ranks_read"], 1)
            count(1, TILES, GROUPS)

            def turn_in(w):
                pe.wait_ge(rows_loaded[w % 2], 16 * (w // 2 + 1))
                if w == 0:
                    pe.wait_ge(s["x4T_sb"], 2)
                else:
                    pe.wait_ge(s["in_sb"], 2 * w)
                for dst, n0, n1 in ((b_t, 0, 3), (b_s, 3, PT)):
                    for i in range(n0, n1):
                        last = TR(dst[:, P * (i - n0):P * (i - n0 + 1)], rows_in[w % 2][:, i, 0:C], ident)
                    last.then_inc(s["in_tr"], 1)

            def expert_fc(e):
                w = e // 2
                if e % 2 == 0:
                    pe.wait_ge(s["in_sb"], 2 * (w + 1))
                    pe.wait_ge(s["experts_in"], 32 * PAIRS)
                for f in range(FC):
                    n = FC * e + f
                    if n >= 3:
                        pe.wait_ge(s["he_sb"], n - 2)
                    M((b_k, b_v, b_q)[n % 3][:, 0:CAP], c_fc_sb[:, e, P * f:P * (f + 1)],
                      inT[w % 2][:, CAP * (e % 2):CAP * (e % 2 + 1)], start=True, stop=True).then_inc(s["fce_mm"], 1)

            def expert_proj(e):
                if e:
                    pe.wait_ge(s["oute_sb"], e)
                else:
                    pe.wait_ge(s["ranks_read"], 2)
                for f in range(FC):
                    pe.wait_ge(s["he_sb"], FC * e + f + 1)
                    last = M(b_y[:, 0:CAP], c_proj_sb[:, e, f, :], heT[e % 2][:, f, :], start=(f == 0), stop=(f == FC - 1))
                last.then_inc(s["proje_mm"], 1)

            def turn_out(w):
                pe.wait_ge(s["oute_sb"], 2 * (w + 1))
                if w:
                    pe.wait_ge(s["out_sb"], 2 * w)
                else:
                    pe.wait_ge(s["x4_sum"], TILES * B)
                for dst, n0, n1 in ((b_m0, 0, 3), (b_m1, 3, PT)):
                    for i in range(n0, n1):
                        last = TR(dst[:, P * (i - n0):P * (i - n0 + 1)], outT[w % 2][:, P * i:P * (i + 1)], ident)
                    last.then_inc(s["out_tr"], 1)

            turn_in(0)
            expert_fc(0)
            for w in range(PAIRS):
                if w + 1 < PAIRS:
                    turn_in(w + 1)
                expert_fc(2 * w + 1)
                expert_proj(2 * w)
                if w:
                    turn_out(w - 1)
                if w + 1 < PAIRS:
                    expert_fc(2 * w + 2)
                expert_proj(2 * w + 1)
            turn_out(PAIRS - 1)


def kernel(**inputs):
    import concourse.bacc as bacc
    from concourse.bass_utils import run_bass_kernel_spmd

    a = {k: np.asarray(v) for k, v in inputs.items()}
    f32 = np.float32
    dh = np.arange(C).reshape(H, D).T.reshape(-1)

    def column(v):
        return v.reshape(-1, P).T

    def pack(columns, parts):
        return np.concatenate([parts[name] for name in columns], axis=1)

    table = constants()
    qkv = np.concatenate([a[f"L0_attn_{n}_w"][dh].T for n in "qkv"], axis=1)
    early = pack(EARLY, dict(
        table, ln1_w=column(a["L0_attn_ln1_w"]), ln1_b=column(a["L0_attn_ln1_b"]),
        q_b=column(a["L0_attn_q_b"][dh]), k_b=column(a["L0_attn_k_b"][dh]), v_b=column(a["L0_attn_v_b"][dh]),
        o_b=column(a["L0_attn_o_b"]), ln2_w=column(a["L0_attn_ln2_w"]), ln2_b=column(a["L0_attn_ln2_b"]),
        fc_b=column(a["L0_attn_fc_b"]), proj_b=column(a["L0_attn_proj_b"]), qkv=qkv))
    bv = np.zeros((P, C), f32)
    bv[0] = a["L0_xattn_bv"]
    context = pack(CONTEXT, dict(
        table, ctxT=np.tile(a["ctx_1024"], (1, TILES, 1)).reshape(-1, C).T, Wk=a["L0_xattn_Wk"], Wv=a["L0_xattn_Wv"],
        WqT=a["L0_xattn_Wq"].T, bk=column(a["L0_xattn_bk"]), bq=column(a["L0_xattn_bq"]), bv=bv,
        w_g=a["L0_ffn_w_g"]))
    d, h = np.arange(C) // H, np.arange(C) % H
    wo_rot = np.stack([a["L0_attn_o_w"].T[h * D + (d + j) % D] for j in range(D)], axis=1)
    mlp = pack(MLP, dict(fcT=a["L0_attn_fc_w"].T,
                         projT=a["L0_attn_proj_w"].T.reshape(FC, P, C).transpose(1, 0, 2).reshape(P, FC * C)))
    c_fc = a["L0_ffn_c_fc"].transpose(1, 0, 2)
    c_proj = a["L0_ffn_c_proj"].reshape(E, FC, P, C).transpose(2, 0, 1, 3)
    arrays = dict(x=a["x"], early=early, context=context, wo_rot=wo_rot, mlp=mlp, c_fc=c_fc, c_proj=c_proj)
    arrays = {k: np.ascontiguousarray(v) for k, v in arrays.items()}

    nc = bacc.Bacc("TRN2", target_bir_lowering=False, num_devices=1)
    ins = [nc.dram_tensor(k, v.shape, F32, kind="ExternalInput").ap() for k, v in arrays.items()]
    out = nc.dram_tensor("out", (B, N, C), F32, kind="ExternalOutput").ap()
    program(nc, *ins, out)
    r = run_bass_kernel_spmd(nc, [arrays], core_ids=[0])
    return r.results[0]["out"]
```

```python
import numpy as np
import concourse.bass as bass
from concourse import mybir
from contextlib import ExitStack

F32, F32R, BF16, U32 = mybir.dt.float32, mybir.dt.float32r, mybir.dt.bfloat16, mybir.dt.uint32
ALU, ACT, AX = mybir.AluOpType, mybir.ActivationFunctionType, mybir.AxisListType

P = 128
C = 128
B, L = 2, 512
CH, N = 4, 256
TILES = N // P
T = B * L
H, D = 16, 8
MW = 4 * C
FC = MW // P
S = 32
E, TOP = 8, 2
CAP = 2 * 5 * T // (4 * E)
GROUPS = TOP * T // P
SLOTS = E * CAP
PAIRS = E // 2
PT = 2 * CAP // P
ROW = C + 2
EPS = 1e-5
KVB = 3
ZREP = 4
ZW = SLOTS * ROW // P // ZREP
NP1 = 4

EARLY = dict(ident=P, ln1_w=1, ln1_b=1, q_b=1, k_b=1, v_b=1, o_b=1, ln2_w=1, ln2_b=1, fc_b=FC, proj_b=1,
             qkv=3 * C, same_d=P, head=H)
CONTEXT = dict(ctxT=B * TILES * S, Wk=C, Wv=C, WqT=C, bk=1, bq=1, bv=C, quad=TILES, w_g=E, tri=P, expert=E,
               from_trash=GROUPS, trash=GROUPS, slot=PAIRS * PT)
MLP = dict(fcT=MW, projT=FC * C)


def places(columns):
    at, out = 0, {}
    for name, n in columns.items():
        out[name] = (at, at + n)
        at += n
    return out, at


def constants():
    p = np.arange(P)
    d_of, h_of = p // H, p % H
    same_d = d_of[:, None] == d_of[None]
    head = h_of[:, None] == np.arange(H)[None]
    quad = (p // S)[:, None] == np.arange(TILES)[None]
    row = p[:, None, None, None] + P * np.arange(GROUPS).reshape(CH, TOP, TILES)[None]
    trash = SLOTS + row
    last = (CAP - 1) * np.arange(TOP)[None, None, :, None]
    slot = p[:, None] + P * np.arange(PAIRS * PT)[None]
    tables = dict(ident=np.eye(P), same_d=same_d, head=head, quad=quad, tri=p[:, None] < p[None],
                  expert=np.tile(np.arange(E), (P, 1)), from_trash=last - trash, trash=trash, slot=slot + TOP * T)
    return {k: np.asarray(v, np.float32).reshape(P, -1) for k, v in tables.items()}


def program(nc, x, early, context, wo_rot, mlp, c_fc, c_proj, out):
    at_early, n_early = places(EARLY)
    at_context, n_context = places(CONTEXT)
    at_mlp, n_mlp = places(MLP)
    ctx = ExitStack()
    with ctx:
        def sb(name, shape, dt=F32):
            return ctx.enter_context(nc.sbuf_tensor(name, shape, dt))

        def sem(name):
            return ctx.enter_context(nc.semaphore(name))

        v_twice = nc.dram_tensor("v_twice", (CH, 2, P, N), F32, kind="Internal").ap()
        slots = nc.dram_tensor("slots", (SLOTS + TOP * T, ROW), F32, kind="Internal").ap()
        results = nc.dram_tensor("results", (TOP * T + SLOTS, C), F32, kind="Internal").ap()

        early_sb = sb("early_sb", [P, n_early])
        context_sb = sb("context_sb", [P, n_context])
        mlp_sb = sb("mlp_sb", [P, n_mlp])
        wo_sb = sb("wo_sb", [P, D, C])
        c_fc_hi = sb("c_fc_hi", [P, E, MW], F32R)
        c_fc_lo = sb("c_fc_lo", [P, E, MW], F32R)
        c_proj_sb = sb("c_proj_sb", [P, E, FC, C])

        def par(name):
            for sbuf, at in ((early_sb, at_early), (context_sb, at_context), (mlp_sb, at_mlp)):
                if name in at:
                    return sbuf[:, at[name][0]:at[name][1]]
            raise KeyError(name)

        def by_chunk(name, shape, dt=F32):
            return [sb(f"{name}{c}", shape, dt) for c in range(CH)]

        def by_turn(name, shape, dt=F32):
            two = [sb(f"{name}{i}", shape, dt) for i in range(2)]
            return [two[c % 2] for c in range(CH)]

        zeros = sb("zeros", [P, ZW])
        minus_half = sb("minus_half", [P, TILES])
        warm = sb("warm", [P, TILES])
        ones_row = sb("ones_row", [1, P])
        ones_bf = sb("ones_bf", [P, P], BF16)
        tri_bf = sb("tri_bf", [P, P], BF16)

        x_sb = by_chunk("x_sb", [P, TILES, C])
        xn = by_chunk("xn", [P, TILES, C])
        xnT = by_chunk("xnT", [P, N])
        stats = by_chunk("stats", [P, TILES, 6])
        mean_var = by_chunk("mean_var", [P, TILES, 2])
        var_eps = by_chunk("var_eps", [P, TILES])
        rstd = by_chunk("rstd", [P, TILES])
        k_exp = by_turn("k_exp", [P, N])
        q_exp = by_turn("q_exp", [P, N])
        k_relu = by_turn("k_relu", [P, N])
        q_relu = by_turn("q_relu", [P, N])
        kT = by_chunk("kT", [P, N])
        qT = by_chunk("qT", [P, N])
        vT = by_chunk("vT", [P, N])
        qkT = by_turn("qkT", [P, N])
        qnT = by_chunk("qnT", [P, N])
        late = sb("late", [P, 2 * (D - 1) * N])
        v_rot = [late[:, (D - 1) * N * i:(D - 1) * N * (i + 1)].rearrange("p (j t) -> p j t", t=N) for i in range(2)]
        got = [late[:, TOP * N * c:TOP * N * (c + 1)].rearrange("p (k a c) -> p k a c", k=TOP, a=TILES) for c in range(CH)]
        fc_in = [late[:, 2 * MW * i:2 * MW * (i + 1)].rearrange("p (e f) -> p e f", e=2) for i in (0, 1, 2, 0)]
        norm = by_chunk("norm", [P, TILES, H])
        norm_d = by_chunk("norm_d", [P, TILES, D, H])
        p1_0 = by_turn("p1_0", [P, N])
        p1 = [sb(f"p1_{i}", [P, N]) for i in range(NP1)]
        p2 = [sb(f"p2_{i}", [P, N]) for i in range(NP1)]
        yT = by_chunk("yT", [P, N])
        x2 = by_chunk("x2", [P, TILES, C])
        xx2 = by_chunk("xx2", [P, TILES, C])
        hT = by_turn("hT", [P, FC, N])
        x3 = by_chunk("x3", [P, TILES, C])
        KT = sb("KT", [P, B * S])
        WqK = sb("WqK", [P, B * S])
        bqK = sb("bqK", [1, B * S])
        V_tile = [sb(f"V_tile{b}", [TILES * S, TILES, C]) for b in range(B)]
        s_max = by_chunk("s_max", [P, TILES])
        s_sub = by_chunk("s_sub", [P, TILES, S])
        s_exp = by_chunk("s_exp", [P, TILES, S])
        s_sum = by_chunk("s_sum", [P, TILES])
        s_inv = by_chunk("s_inv", [P, TILES])
        expT = by_chunk("expT", [TILES * S, P])
        pay = [by_chunk(f"pay{k}_", [P, TILES, ROW]) for k in range(TOP)]
        logits = by_chunk("logits", [P, TILES, E])
        top_v = by_chunk("top_v", [P, TILES, 8])
        top_i = by_chunk("top_i", [P, TILES, 8], U32)
        gap = by_chunk("gap", [P, TILES])
        gap_tanh = by_chunk("gap_tanh", [P, TILES])
        one_hot = by_chunk("one_hot", [P, 3, TILES, E], BF16)
        rank_all = by_chunk("rank_all", [P, 3 * TILES, E])
        rank = by_chunk("rank", [P, 3, TILES])
        from_trash = by_chunk("from_trash", [P, TOP, TILES])
        away = by_chunk("away", [P, TOP, TILES])
        away_kept = by_chunk("away_kept", [P, TOP, TILES])
        target = by_chunk("target", [P, TOP, TILES], U32)
        minus_mean = by_chunk("minus_mean", [P, TILES])
        shift = by_chunk("shift", [P, TILES])
        rows_in = [sb(f"rows_in{i}", [P, PT, ROW]) for i in range(2)]
        send_to = sb("send_to", [P, PAIRS, PT], U32)
        send_w = sb("send_w", [P, PAIRS, PT])
        in_hi = [sb(f"in_hi{i}", [P, 2 * CAP], F32R) for i in range(2)]
        in_lo = [sb(f"in_lo{i}", [P, 2 * CAP], F32R) for i in range(2)]
        heT = [sb(f"heT{i}", [P, FC, CAP]) for i in range(2)]
        outT = [sb(f"outT{i}", [P, 2 * CAP]) for i in range(2)]
        rows_out = [late[:, TOP * N * CH + PT * C * i:TOP * N * CH + PT * C * (i + 1)].rearrange("p (i c) -> p i c", c=C)
                    for i in range(2)]

        bank = [ctx.enter_context(nc.psum_tensor(f"bank{i}", [P, 512], F32)) for i in range(8)]
        kv_bank, y_bank = bank[4:4 + KVB], bank[7]

        names = """early_in context_in wo_in mlp_in zero_slots zero_results
            pool_order dve_order act_order pool_consts filled
            ln1_var ln1_rstd ln1_done ln2_var ln2_rstd ln2_done post1_var post1_rstd post1_done
            post2_var post2_rstd post2_done post3_var post3_rstd post3_done
            exp_parts k_sb q_sb norm_d_sb p1_first p1_rest kv_mm p2_ready y_step y_sb xx2_sb h_sb
            V_tile_sb exp_sb pay1_sb gap_ready gap_tanh_sb hot_ready ranks_read
            minus_mean_sb shift_sb targets first_sent last_done fc_hi_sb fc_lo_sb in_hi_sb send_ready out_sb out_stored"""
        s = {name: sem(name) for name in names.split()}
        x_in = [sem(f"x_in{c}") for c in range(CH)]
        fc_loaded = [sem(f"fc_loaded{w}") for w in range(PAIRS)]
        proj_loaded = [sem(f"proj_loaded{w}") for w in range(PAIRS)]
        v_stored = [sem(f"v_stored{c}") for c in range(CH)]
        v_back = [[sem(f"v_back{i}_{part}") for part in range(2)] for i in range(2)]
        results_sent = [sem(f"results_sent{i}") for i in range(2)]
        rows_loaded = [[sem(f"rows_loaded{i}_{part}") for part in range(2)] for i in range(2)]
        second_sent = [sem(f"second_sent{c}") for c in range(CH)]
        got_in = [sem(f"got_in{c}") for c in range(CH)]
        IN_PARTS = ((0, 3), (3, PT))
        V_PARTS = ((1, 4), (4, 8))

        class Order:

            def __init__(self, eng, semaphore):
                self.eng, self.sem, self.n = eng, semaphore, 0

            def __call__(self, ins):
                self.n += 1
                ins.then_inc(self.sem, 1)
                return ins

            def wait(self, back=1):
                self.eng.wait_ge(self.sem, self.n - back + 1)

        class Ring:

            fillings = 0

            def __init__(self, name, banks):
                self.banks, self.n, self.at = banks, 0, {}
                self.read = [sem(f"{name}{i}_read") for i in range(len(banks))]

            def claim(self, pe, what, c):
                i, turn = self.n % len(self.banks), self.n // len(self.banks)
                self.at[what, c] = (i, turn)
                self.n += 1
                if turn:
                    pe.wait_ge(self.read[i], turn)
                return self.banks[i]

            def fill(self, what, c, last):
                Ring.fillings += 1
                self.at[what, c] += (Ring.fillings,)
                last.then_inc(s["filled"], 1)

            def take(self, eng, what, c):
                i, _, n = self.at[what, c]
                eng.wait_ge(s["filled"], n)
                return self.banks[i]

            def release(self, what, c, reader):
                reader.then_inc(self.read[self.at[what, c][0]], 1)

            def wait_read(self, eng, what, c):
                i, turn, _ = self.at[what, c]
                eng.wait_ge(self.read[i], turn + 1)

        Ring.fillings = 0
        ring = Ring("ring", bank[:4])
        side = Ring("side", bank[4:8])
        block = ctx.enter_context(nc.Block())

        @block.tensor
        def _(pe):
            M, TR = nc.tensor.matmul, nc.tensor.transpose
            ident = par("ident")

            def turn(what, c, tile):
                dst = ring.claim(pe, what, c)
                for a in range(TILES):
                    last = TR(dst[:, P * a:P * (a + 1)], tile(a), ident)
                ring.fill(what, c, last)

            def ln1_in(c):
                pe.wait_ge(s["ln1_done"], TILES * (c + 1))
                turn("ln1T", c, lambda a: xn[c][:, a, :])

            def head_in(name, c):
                i = "qkv".index(name)
                ring.wait_read(pe, "ln1T", c)
                dst = ring.claim(pe, name, c)
                ring.fill(name, c, M(dst[:, 0:N], par("qkv")[:, C * i:C * (i + 1)], xnT[c][:, :], start=True, stop=True))

            def head_sums(c):
                pe.wait_ge(s["k_sb"], c + 1)
                dst = ring.claim(pe, "k_sum", c)
                ring.fill("k_sum", c, M(dst[:, 0:N], par("same_d"), kT[c][:, :], start=True, stop=True))

            def norm_sums(c):
                ring.wait_read(pe, "k_sum", c)
                dst = ring.claim(pe, "norm", c)
                for a in range(TILES):
                    last = M(dst[:, H * a:H * (a + 1)], qkT[c][:, P * a:P * (a + 1)], par("head"), start=True, stop=True)
                ring.fill("norm", c, last)

            def norm_back(c):
                pe.wait_ge(s["norm_d_sb"], c + 1)
                turn("norm_back", c, lambda a: norm_d[c][:, a, :, :].rearrange("p d h -> p (d h)"))

            def kv(c, j):
                n = D * c + j
                if j == 0:
                    pe.wait_ge(s["p1_first"], c + 1)
                else:
                    pe.wait_ge(s["p1_rest"], (D - 1) * c + j)
                if n >= KVB:
                    pe.wait_ge(s["p2_ready"], n - KVB + 1)
                src = p1_0[c] if j == 0 else p1[((D - 1) * c + j - 1) % NP1]
                M(kv_bank[n % KVB][:, 0:N], par("same_d"), src[:, :], start=True, stop=True).then_inc(s["kv_mm"], 1)

            def y_part(c, j):
                n = D * c + j
                pe.wait_ge(s["p2_ready"], n + 1)
                if n == 0:
                    pe.wait_ge(s["wo_in"], 16)
                if j == 0 and c:
                    pe.wait_ge(s["y_sb"], c)
                M(y_bank[:, 0:N], wo_sb[:, j, :], p2[n % NP1][:, :], start=(j == 0), stop=(j == D - 1))\
                    .then_inc(s["y_step"], 1)

            def y_back(c):
                pe.wait_ge(s["y_sb"], c + 1)
                turn("y_back", c, lambda a: yT[c][:, P * a:P * (a + 1)])

            def ln2_in(c):
                pe.wait_ge(s["ln2_done"], TILES * (c + 1))
                turn("ln2T", c, lambda a: xn[c][:, a, :])

            def fc(c, f):
                ring.wait_read(pe, "ln2T", c)
                if c == f == 0:
                    pe.wait_ge(s["mlp_in"], 16)
                dst = ring.claim(pe, f"fc{f}", c)
                ring.fill(f"fc{f}", c, M(dst[:, 0:N], par("fcT")[:, P * f:P * (f + 1)], xnT[c][:, :],
                                         start=True, stop=True))

            def proj(c):
                dst = ring.claim(pe, "proj", c)
                for f in range(FC):
                    ring.wait_read(pe, f"fc{f}", c)
                    last = M(dst[:, 0:N], par("projT")[:, C * f:C * (f + 1)], hT[c][:, f, :], start=(f == 0), stop=(f == FC - 1))
                ring.fill("proj", c, last)

            def mlp_back(c):
                ring.wait_read(pe, "proj", c)
                turn("mlp_back", c, lambda a: yT[c][:, P * a:P * (a + 1)])

            def cross_in(c):
                pe.wait_ge(s["post1_done"], TILES * (c + 1))
                turn("x3T", c, lambda a: x3[c][:, a, :])

            def scores(c):
                ring.wait_read(pe, "x3T", c)
                if c == 0:
                    ring.wait_read(pe, "WqK", 0)
                    ring.wait_read(pe, "bqK", 0)
                dst, b = ring.claim(pe, "scores", c), c * N // L
                keys = slice(S * b, S * (b + 1))
                M(dst[:, 0:TILES * S], ones_row[:, :], bqK[:, keys].unsqueeze(1).to_broadcast((1, TILES, S)),
                  start=True, stop=False)
                for a in range(TILES):
                    last = M(dst[:, S * a:S * (a + 1)], xnT[c][:, P * a:P * (a + 1)], WqK[:, keys], start=False,
                             stop=(a == TILES - 1))
                ring.fill("scores", c, last)

            def weights_turned(c):
                pe.wait_ge(s["exp_sb"], c + 1)
                dst = ring.claim(pe, "expT", c)
                ring.fill("expT", c, TR(dst[0:TILES * S, 0:P], s_exp[c][:, :, :].rearrange("p a k -> p (a k)"), ident))

            def attend(c):
                ring.wait_read(pe, "expT", c)
                if c == 0:
                    pe.wait_ge(s["V_tile_sb"], B * (TILES - 1))
                    ring.wait_read(pe, "V", B - 1)
                dst, b = ring.claim(pe, "attend", c), c * N // L
                ring.fill("attend", c, M(dst[:, 0:N], expT[c][:, :], V_tile[b][:, :, :].rearrange("p a c -> p (a c)"),
                                         start=True, stop=True))

            def route_in(c):
                pe.wait_ge(s["post2_done"], TILES * (c + 1))
                turn("x4T", c, lambda a: pay[0][c][:, a, 0:C])

            def logits_of(c):
                ring.wait_read(pe, "x4T", c)
                dst = ring.claim(pe, "logits", c)
                for a in range(TILES):
                    last = M(dst[:, E * a:E * (a + 1)], xnT[c][:, P * a:P * (a + 1)], par("w_g"), start=True, stop=True)
                ring.fill("logits", c, last)

            def count(c):
                ranks = ring.claim(pe, "ranks", c)[:, 0:3 * TILES * E].rearrange("p (s a e) -> p s a e", s=3, a=TILES)

                def ones_times(dst, rows, start=False, stop=False):
                    return M(dst, ones_bf[:, :], rows.to_broadcast((P, *dst.shape[1:])), start=start, stop=stop)

                for b in range(c):
                    for a in range(TILES):
                        ones_times(ranks, one_hot[b][:, :, a:a + 1, :], start=(b == a == 0))
                        ones_times(ranks[:, 2:3, :, :], one_hot[b][:, 0:1, a:a + 1, :])
                pe.wait_ge(s["hot_ready"], 3 * (c + 1))
                M(ranks, tri_bf[:, :], one_hot[c][:, :, :, :], start=(c == 0), stop=False)
                ones_times(ranks[:, :, 1:2, :], one_hot[c][:, :, 0:1, :])
                for a in range(TILES):
                    last = ones_times(ranks[:, 2:3, :, :], one_hot[c][:, 0:1, a:a + 1, :], stop=(a == TILES - 1))
                ring.fill("ranks", c, last)

            def context_key():
                pe.wait_ge(s["context_in"], 16)
                dst = ring.claim(pe, "KT", 0)
                ring.fill("KT", 0, M(dst[:, 0:B * S], par("Wk"),
                                     par("ctxT").rearrange("p (b a k) -> p b a k", b=B, a=TILES)[:, :, 0, :],
                                     start=True, stop=True))

            def context_value(b):
                pe.wait_ge(s["context_in"], 16)
                pe.wait_ge(s["pool_order"], 3)
                dst = ring.claim(pe, "V", b)[0:TILES * S, 0:C]
                rows = slice(TILES * S * b, TILES * S * (b + 1))
                M(dst, par("ctxT")[:, rows], par("Wv"), start=True, stop=False)
                ring.fill("V", b, M(dst, ones_row[:, 0:TILES * S], par("bv")[0:1, :], start=False, stop=True))

            def keys_times_Wq():
                ring.wait_read(pe, "KT", 0)
                dst = ring.claim(pe, "WqK", 0)
                ring.fill("WqK", 0, M(dst[:, 0:B * S], par("WqT"), KT[:, :], start=True, stop=True))

            def keys_times_bq():
                ring.wait_read(pe, "KT", 0)
                dst = ring.claim(pe, "bqK", 0)
                ring.fill("bqK", 0, M(dst[0:1, 0:B * S], par("bq"), KT[:, :], start=True, stop=True))

            pe.wait_ge(s["early_in"], 16)
            ln1_in(0)
            context_value(0)
            head_in("k", 0)
            head_in("v", 0)
            head_in("q", 0)
            context_value(1)
            kv(0, 0)
            head_sums(0)
            context_key()
            ln1_in(1)
            ln1_in(2)
            norm_sums(0)
            keys_times_bq()
            head_in("v", 1)
            head_in("v", 2)
            norm_back(0)
            head_in("k", 1)
            keys_times_Wq()
            head_in("q", 1)
            head_in("k", 2)
            head_in("q", 2)
            head_sums(1)
            kv(0, 1)
            ln1_in(3)
            kv(0, 2)
            norm_sums(1)
            kv(0, 3)
            head_in("k", 3)
            kv(0, 4)
            norm_back(1)
            kv(0, 5)
            head_sums(2)
            kv(0, 6)
            head_in("v", 3)
            for j in range(0, 6):
                y_part(0, j)
            kv(0, 7)
            for j in range(0, 4):
                kv(1, j)
            y_part(0, 6)
            kv(1, 4)
            y_part(0, 7)
            kv(1, 5)
            norm_sums(2)
            y_back(0)
            y_part(1, 0)
            kv(1, 6)
            for j in range(1, 4):
                y_part(1, j)
            norm_back(2)
            kv(1, 7)
            for j in range(4, 6):
                y_part(1, j)
            ln2_in(0)
            kv(2, 0)
            for j in range(6, 8):
                y_part(1, j)
            for f in range(0, 2):
                fc(0, f)
            y_back(1)
            fc(0, 2)
            for j in range(1, 3):
                kv(2, j)
            fc(0, 3)
            for j in range(3, 5):
                kv(2, j)
            proj(0)
            ln2_in(1)
            kv(2, 5)
            mlp_back(0)
            y_part(2, 0)
            for f in range(0, 4):
                fc(1, f)
            for j in range(6, 8):
                kv(2, j)
            head_sums(3)
            cross_in(0)
            head_in("q", 3)
            y_part(2, 1)
            scores(0)
            y_part(2, 2)
            kv(3, 0)
            for j in range(3, 5):
                y_part(2, j)
            for j in range(1, 3):
                kv(3, j)
            weights_turned(0)
            norm_sums(3)
            y_part(2, 5)
            attend(0)
            y_part(2, 6)
            norm_back(3)
            proj(1)
            y_part(2, 7)
            kv(3, 3)
            mlp_back(1)
            y_back(2)
            route_in(0)
            y_part(3, 0)
            kv(3, 4)
            logits_of(0)
            kv(3, 5)
            y_part(3, 1)
            kv(3, 6)
            for j in range(2, 4):
                y_part(3, j)
            cross_in(1)
            kv(3, 7)
            y_part(3, 4)
            scores(1)
            count(0)
            ln2_in(2)
            weights_turned(1)
            y_part(3, 5)
            fc(2, 0)
            attend(1)
            y_part(3, 6)
            fc(2, 1)
            y_part(3, 7)
            for f in range(2, 4):
                fc(2, f)
            y_back(3)
            proj(2)
            route_in(1)
            mlp_back(2)
            ln2_in(3)
            logits_of(1)
            for f in range(0, 3):
                fc(3, f)
            count(1)
            fc(3, 3)
            cross_in(2)
            proj(3)
            scores(2)
            mlp_back(3)
            weights_turned(2)
            attend(2)
            cross_in(3)
            scores(3)
            weights_turned(3)
            attend(3)
            route_in(2)
            logits_of(2)
            count(2)
            route_in(3)
            logits_of(3)
            count(3)

            def rows_turned(w, part):
                pe.wait_ge(rows_loaded[w % 2][part], 16 * (w // 2 + 1))
                dst = side.claim(pe, f"in{part}", w)
                for i in ((0, 1, 2), (3, 4))[part]:
                    last = TR(dst[:, P * (i - 3 * part):P * (i - 3 * part + 1)], rows_in[w % 2][:, i, 0:C], ident)
                side.fill(f"in{part}", w, last)

            def expert_fc(e):
                w = e // 2
                pe.wait_ge(s["in_hi_sb"], e + 1)
                pe.wait_ge(s["fc_lo_sb"], e + 1)
                at = slice(CAP * (e % 2), CAP * (e % 2 + 1))
                for f in range(FC):
                    dst = ring.claim(pe, f"expert_fc{f}", e)[:, 0:CAP]
                    hi, lo = c_fc_hi[:, e, P * f:P * (f + 1)], c_fc_lo[:, e, P * f:P * (f + 1)]
                    M(dst, hi, in_hi[w % 2][:, at], start=True, stop=False)
                    M(dst, lo, in_hi[w % 2][:, at], start=False, stop=False)
                    if f == 0:
                        side.wait_read(pe, f"in{e % 2}", w)
                    ring.fill(f"expert_fc{f}", e, M(dst, hi, in_lo[w % 2][:, at], start=False, stop=True))

            def expert_proj(e):
                dst = side.claim(pe, "expert_proj", e)
                if e % 2 == 0:
                    pe.wait_ge(proj_loaded[e // 2], 16)
                for f in range(FC):
                    ring.wait_read(pe, f"expert_fc{f}", e)
                    last = M(dst[:, 0:CAP], c_proj_sb[:, e, f, :], heT[e % 2][:, f, :], start=(f == 0), stop=(f == FC - 1))
                side.fill("expert_proj", e, last)

            def results_turned(w, part):
                side.wait_read(pe, "expert_proj", 2 * w + part)
                dst = side.claim(pe, f"out{part}", w)
                for i in ((0, 1), (2, 3, 4))[part]:
                    last = TR(dst[:, P * (i - 2 * part):P * (i - 2 * part + 1)], outT[w % 2][:, P * i:P * (i + 1)], ident)
                side.fill(f"out{part}", w, last)

            pe.wait_ge(s["p2_ready"], CH * D)
            pe.wait_ge(s["y_sb"], CH)
            for part in range(2):
                rows_turned(0, part)
            expert_fc(0)
            for w in range(PAIRS):
                if w + 1 < PAIRS:
                    for part in range(2):
                        rows_turned(w + 1, part)
                if w:
                    results_turned(w - 1, 1)
                expert_fc(2 * w + 1)
                expert_proj(2 * w)
                if w + 1 < PAIRS:
                    expert_fc(2 * w + 2)
                results_turned(w, 0)
                expert_proj(2 * w + 1)
            results_turned(PAIRS - 1, 1)
            sums = [ring.claim(pe, "sum", c) for c in range(CH)]
            for c in range(CH):
                M(sums[c][:, 0:N], ident, pay[0][c][:, :, 0:C], start=True, stop=False)
            for c in range(CH):
                pe.wait_ge(got_in[c], 16)
                ring.fill("sum", c, M(sums[c][:, 0:N], ident, got[c][:, 0, :, :], start=False, stop=True))

        @block.sync
        def _(sp):
            def load_x(c):
                rows = x.rearrange("b l c -> (b l) c")[N * c:N * (c + 1), :]
                sp.dma_start(x_sb[c][:, :, :], rows.rearrange("(a p) c -> p a c", p=P)).then_inc(x_in[c], 16)

            def rotate_v(c):
                ring.wait_read(sp, "v", c)
                sp.dma_start(v_twice[c].rearrange("r p t -> p r t"),
                             vT[c][:, :].unsqueeze(1).to_broadcast((P, 2, N))).then_inc(v_stored[c], 16)

            def bring_v(c):
                sp.wait_ge(v_stored[c], 16)
                if c >= 2:
                    sp.wait_ge(s["p1_rest"], (D - 1) * (c - 1))
                for i, (j0, j1) in enumerate(V_PARTS):
                    windows = v_twice[c, 0]
                    windows = bass.AP(windows.tensor, windows.offset + H * N * j0, [[N, P], [H * N, j1 - j0], [1, N]])
                    sp.dma_start(v_rot[c % 2][:, j0 - 1:j1 - 1, :], windows).then_inc(v_back[c % 2][i], 16)

            load_x(0)
            sp.dma_start(early_sb[:, :], early).then_inc(s["early_in"], 16)
            load_x(1)
            sp.dma_start(context_sb[:, :], context).then_inc(s["context_in"], 16)
            load_x(2)
            load_x(3)
            rotate_v(0)
            bring_v(0)
            sp.dma_start(wo_sb[:, :, :], wo_rot).then_inc(s["wo_in"], 16)
            rotate_v(1)
            bring_v(1)
            sp.dma_start(mlp_sb[:, :], mlp).then_inc(s["mlp_in"], 16)
            rotate_v(2)
            bring_v(2)
            rotate_v(3)
            bring_v(3)
            sp.wait_ge(s["pool_consts"], 1)
            for dst, name in ((slots[0:SLOTS, :], "zero_slots"), (results[0:TOP * T, :], "zero_results")):
                n = dst.shape[0] // P // ZREP * dst.shape[1]
                sp.dma_start(dst.rearrange("(p n i) r -> p n (i r)", p=P, n=ZREP),
                             zeros[:, 0:n].unsqueeze(1).to_broadcast((P, ZREP, n))).then_inc(s[name], 16)
            for w in range(PAIRS):
                sp.dma_start(c_proj_sb[:, 2 * w:2 * w + 2, :, :], c_proj[:, 2 * w:2 * w + 2, :, :])\
                  .then_inc(proj_loaded[w], 16)
            sp.wait_ge(s["p1_rest"], (D - 1) * CH)
            for w in range(PAIRS):
                if w == PAIRS - 1:
                    sp.wait_ge(s["fc_lo_sb"], 2)
                sp.dma_start(fc_in[w], c_fc[:, 2 * w:2 * w + 2, :]).then_inc(fc_loaded[w], 16)
            sp.wait_ge(s["first_sent"], 16 * TILES * CH)
            sp.wait_ge(second_sent[CH - 1], 16 * TILES)
            for w in range(PAIRS):
                for part, (n0, n1) in enumerate(IN_PARTS):
                    if w >= 2:
                        side.wait_read(sp, f"in{part}", w - 2)
                        sp.wait_ge(s["send_ready"], 2 * (w - 1))
                    sp.dma_start(rows_in[w % 2][:, n0:n1, :],
                                 slots[P * (PT * w + n0):P * (PT * w + n1), :].rearrange("(i p) r -> p i r", p=P))\
                      .then_inc(rows_loaded[w % 2][part], 16)
            for i in range(2):
                sp.wait_ge(results_sent[i], 16 * PT * PAIRS // 2)
            for c in range(CH):
                rows = results[TOP * N * c:TOP * N * (c + 1), :].rearrange("(g p) r -> p g r", p=P)
                sp.dma_start(got[c].rearrange("p k a r -> p (k a) r"), rows).then_inc(got_in[c], 16)
            for c in range(CH):
                if c < CH - 1:
                    sp.wait_ge(s["post3_done"], TILES * (c + 1))
                else:
                    sp.wait_ge(s["last_done"], TILES)
                rows = out.rearrange("b l c -> (b l) c")[N * c:N * (c + 1), :]
                sp.dma_start(rows.rearrange("(a p) c -> p a c", p=P), xn[c][:, :, :]).then_inc(s["out_stored"], 16)
            sp.wait_ge(s["out_stored"], 16 * CH)

        @block.gpsimd
        def _(pool):
            order = Order(pool, s["pool_order"])

            def rstd_of(name, c):
                pool.wait_ge(s[f"{name}_var"], c + 1)
                nc.gpsimd.tensor_tensor(rstd[c][:, :], var_eps[c][:, :], minus_half[:, :], ALU.pow)\
                  .then_inc(s[f"{name}_rstd"], 1)

            def product(c, j):
                m = (D - 1) * c + j - 1
                if j == 1:
                    pool.wait_ge(s["k_sb"], c + 1)
                for i, (j0, _) in enumerate(V_PARTS):
                    if j == j0:
                        pool.wait_ge(v_back[c % 2][i], 16 * (c // 2 + 1))
                if m >= NP1:
                    c0, j0 = (m - NP1) // (D - 1), (m - NP1) % (D - 1) + 1
                    pool.wait_ge(s["kv_mm"], D * c0 + j0 + 1)
                nc.gpsimd.tensor_tensor(p1[m % NP1][:, :], kT[c][:, :], v_rot[c % 2][:, j - 1, :], ALU.mult)\
                  .then_inc(s["p1_rest"], 1)

            def twice_residual(c):
                ring.wait_read(pool, "y_back", c)
                nc.gpsimd.tensor_tensor(xx2[c][:, :, :], x_sb[c][:, :, :], x2[c][:, :, :], ALU.add)\
                  .then_inc(s["xx2_sb"], 1)

            def send(c, k, a):
                pool.wait_ge(s["targets"], c + 1)
                if k == 1:
                    pool.wait_ge(s["pay1_sb"], c + 1)
                elif c:
                    pool.wait_ge(second_sent[c - 1], 16 * TILES)
                pool.indirect_dma_start(slots, bass.IndirectOffsetOnAxis(ap=target[c][:, k, a:a + 1], axis=0),
                                        pay[k][c][:, a, :], None).then_inc(second_sent[c] if k else s["first_sent"], 16)

            order(nc.gpsimd.memset(minus_half[:, :], -0.5))
            order(nc.gpsimd.memset(ones_row[:, :], 1.0))
            order(nc.gpsimd.memset(ones_bf[:, :], 1.0))
            order.wait()
            rstd_of("ln1", 0)
            rstd_of("ln1", 1)
            rstd_of("ln1", 2)
            rstd_of("ln1", 3)
            pool.wait_ge(s["context_in"], 16)
            order(nc.gpsimd.tensor_copy(tri_bf[:, :], par("tri")))
            order.wait()
            nc.gpsimd.memset(zeros[:, :], 0.0).then_inc(s["pool_consts"], 1)
            for j in range(1, 8):
                product(0, j)
            for j in range(1, 8):
                product(1, j)
            for j in range(1, 4):
                product(2, j)
            rstd_of("ln2", 0)
            twice_residual(0)
            for j in range(4, 6):
                product(2, j)
            rstd_of("ln2", 1)
            product(2, 6)
            twice_residual(1)
            product(2, 7)
            for j in range(1, 3):
                product(3, j)
            rstd_of("post1", 0)
            for j in range(3, 7):
                product(3, j)
            rstd_of("post2", 0)
            product(3, 7)
            rstd_of("post1", 1)
            rstd_of("ln2", 2)
            twice_residual(2)
            pool.wait_ge(s["zero_slots"], 16)
            send(0, 1, 0)
            send(0, 1, 1)
            send(0, 0, 0)
            send(0, 0, 1)
            rstd_of("post2", 1)
            rstd_of("ln2", 3)
            twice_residual(3)
            rstd_of("post1", 2)
            send(1, 1, 0)
            send(1, 1, 1)
            send(1, 0, 0)
            send(1, 0, 1)
            rstd_of("post1", 3)
            rstd_of("post2", 2)
            rstd_of("post2", 3)
            send(2, 1, 0)
            send(2, 1, 1)
            send(2, 0, 0)
            send(2, 0, 1)
            send(3, 1, 0)
            send(3, 1, 1)
            send(3, 0, 0)
            send(3, 0, 1)
            pool.wait_ge(s["zero_results"], 16)
            for w in range(PAIRS):
                for part, tiles in enumerate(((0, 1), (2, 3, 4))):
                    pool.wait_ge(s["send_ready"], 2 * (w + 1))
                    for i in tiles:
                        if i < tiles[-1]:
                            pool.wait_ge(s["out_sb"], (PT - 2) * w + i - part + 1)
                        else:
                            side.wait_read(pool, f"out{part}", w)
                        pool.indirect_dma_start(results, bass.IndirectOffsetOnAxis(ap=send_to[:, w, i:i + 1], axis=0),
                                                rows_out[w % 2][:, i, :], None).then_inc(results_sent[w % 2], 16)
            for c in range(CH):
                rstd_of("post3", c)
                if c == CH - 1:
                    break
                pool.wait_ge(s["post3_rstd"], c + 1)
                pool.wait_ge(s["minus_mean_sb"], c + 1)
                nc.gpsimd.tensor_tensor(shift[c][:, :], minus_mean[c][:, :], rstd[c][:, :], ALU.mult)\
                  .then_inc(s["shift_sb"], 1)

        @block.scalar
        def _(act):
            order = Order(act, s["act_order"])
            A = nc.scalar.activation

            def col(name, i=0):
                return par(name)[:, i:i + 1]

            def read(what, c, dst, func=ACT.Copy, **kw):
                src = ring.take(act, what, c)
                ring.release(what, c, A(dst, src[0:dst.shape[0], 0:dst.free_size()], func, **kw))

            def ln1_out(c):
                read("ln1T", c, xnT[c][:, :], ACT.Identity, bias=col("ln1_b"), scale=col("ln1_w"))

            def elu_parts(name, c):
                exp, relu = (k_exp, k_relu) if name == "k" else (q_exp, q_relu)
                if c >= 2:
                    act.wait_ge(s[f"{name}_sb"], c - 1)
                src = ring.take(act, name, c)
                A(exp[c][:, :], src[:, 0:N], ACT.Exp, bias=col(f"{name}_b")).then_inc(s["exp_parts"], 1)
                ring.release(name, c, A(relu[c][:, :], src[:, 0:N], ACT.Relu, bias=col(f"{name}_b")))

            def v_out(c):
                read("v", c, vT[c][:, :], ACT.Identity, bias=col("v_b"))

            def y_out(c):
                act.wait_ge(s["y_step"], D * (c + 1))
                A(yT[c][:, :], y_bank[:, 0:N], ACT.Identity, bias=col("o_b")).then_inc(s["y_sb"], 1)

            def ln2_out(c):
                read("ln2T", c, xnT[c][:, :], ACT.Identity, bias=col("ln2_b"), scale=col("ln2_w"))

            def gelu(c, f):
                if c >= 2 and f == 0:
                    ring.wait_read(act, "proj", c - 2)
                read(f"fc{f}", c, hT[c][:, f, :], ACT.Gelu, bias=col("fc_b", f))

            def mlp_out(c):
                read("proj", c, yT[c][:, :], ACT.Identity, bias=col("proj_b"))

            def cross_exp(c):
                ring.wait_read(act, "scores", c)
                A(s_exp[c][:, :, :], s_sub[c][:, :, :], ACT.Exp, scale=float(C) ** -0.5).then_inc(s["exp_sb"], 1)

            def weights_out(c):
                read("expT", c, expT[c][:, :])

            def x3_out(c):
                read("x3T", c, xnT[c][:, :])

            def x4_out(c):
                read("x4T", c, xnT[c][:, :])

            def second_rows(c):
                act.wait_ge(s["post2_done"], TILES * (c + 1))
                A(pay[1][c][:, :, 0:C], pay[0][c][:, :, 0:C], ACT.Copy).then_inc(s["pay1_sb"], 1)

            def key_out():
                act.wait_ge(s["context_in"], 16)
                read("KT", 0, KT[:, :], ACT.Identity, bias=col("bk"))

            def value_out(b):
                act.wait_ge(s["context_in"], 16)
                src = ring.take(act, "V", b)
                for a in range(TILES):
                    ins = A(V_tile[b][:, a, :], src[0:TILES * S, 0:C], ACT.Copy, scale=par("quad")[0:TILES * S, a:a + 1])
                    if a < TILES - 1:
                        ins.then_inc(s["V_tile_sb"], 1)
                ring.release("V", b, ins)

            def gap_out(c):
                act.wait_ge(s["gap_ready"], c + 1)
                A(gap_tanh[c][:, :], gap[c][:, :], ACT.Tanh, scale=-0.5).then_inc(s["gap_tanh_sb"], 1)

            act.wait_ge(s["pool_order"], 1)
            order(A(warm[:, :], minus_half[:, :], ACT.Exp))
            act.wait_ge(s["early_in"], 16)
            ln1_out(0)
            value_out(0)
            elu_parts("k", 0)
            v_out(0)
            elu_parts("q", 0)
            value_out(1)
            key_out()
            ln1_out(1)
            ln1_out(2)
            read("bqK", 0, bqK[:, :])
            v_out(1)
            v_out(2)
            elu_parts("k", 1)
            read("WqK", 0, WqK[:, :])
            elu_parts("q", 1)
            elu_parts("k", 2)
            elu_parts("q", 2)
            ln1_out(3)
            elu_parts("k", 3)
            v_out(3)
            y_out(0)
            ln2_out(0)
            y_out(1)
            for f in range(0, 4):
                gelu(0, f)
            mlp_out(0)
            ln2_out(1)
            for f in range(0, 4):
                gelu(1, f)
            x3_out(0)
            elu_parts("q", 3)
            cross_exp(0)
            weights_out(0)
            mlp_out(1)
            y_out(2)
            second_rows(0)
            x4_out(0)
            x3_out(1)
            gap_out(0)
            cross_exp(1)
            ln2_out(2)
            weights_out(1)
            for f in range(0, 2):
                gelu(2, f)
            y_out(3)
            for f in range(2, 4):
                gelu(2, f)
            mlp_out(2)
            second_rows(1)
            x4_out(1)
            ln2_out(3)
            for f in range(0, 3):
                gelu(3, f)
            gap_out(1)
            gelu(3, 3)
            x3_out(2)
            mlp_out(3)
            cross_exp(2)
            weights_out(2)
            x3_out(3)
            cross_exp(3)
            weights_out(3)
            second_rows(2)
            x4_out(2)
            gap_out(2)
            second_rows(3)
            x4_out(3)
            gap_out(3)
            for e in range(E):
                act.wait_ge(fc_loaded[e // 2], 16)
                A(c_fc_hi[:, e, :], fc_in[e // 2][:, e % 2, :], ACT.Copy).then_inc(s["fc_hi_sb"], 1)

            def rows_hi(w, part):
                n0, n1 = IN_PARTS[part]
                src = side.take(act, f"in{part}", w)
                if w >= 2 and part == 0:
                    ring.wait_read(act, f"expert_fc{FC - 1}", 2 * w - 3)
                A(in_hi[w % 2][:, P * n0:P * n1], src[:, 0:P * (n1 - n0)], ACT.Copy).then_inc(s["in_hi_sb"], 1)

            def expert_gelus(e):
                if e >= 2:
                    side.wait_read(act, "expert_proj", e - 2)
                for f in range(FC):
                    read(f"expert_fc{f}", e, heT[e % 2][:, f, :], ACT.Gelu)

            rows_hi(0, 0)
            rows_hi(0, 1)
            expert_gelus(0)
            for w in range(PAIRS):
                if w + 1 < PAIRS:
                    rows_hi(w + 1, 0)
                    rows_hi(w + 1, 1)
                expert_gelus(2 * w + 1)
                if w + 1 < PAIRS:
                    expert_gelus(2 * w + 2)
            for c in range(CH - 1):
                act.wait_ge(s["shift_sb"], c + 1)
                ring.wait_read(act, "sum", c)
                for a in range(TILES):
                    A(xn[c][:, a, :], x2[c][:, a, :], ACT.Identity, bias=shift[c][:, a:a + 1],
                      scale=rstd[c][:, a:a + 1]).then_inc(s["post3_done"], 1)

        @block.vector
        def _(dve):
            order = Order(dve, s["dve_order"])
            V = nc.vector
            flat = "p a c -> p (a c)"

            def normalise(name, c, src):
                for a in range(TILES):
                    order(V.bn_stats(stats[c][:, a, :], src[:, a, :]))
                for a in range(TILES):
                    order.wait(TILES)
                    order(V.bn_aggr(mean_var[c][:, a, :], stats[c][:, a, :]))
                order.wait()
                V.tensor_scalar(var_eps[c][:, :], mean_var[c][:, :, 1], EPS, None, ALU.add)\
                 .then_inc(s[f"{name}_var"], 1)

            def scale(name, c, src, dst):
                dve.wait_ge(s[f"{name}_rstd"], c + 1)
                for a in range(TILES):
                    V.tensor_scalar(dst[:, a, 0:C], src[:, a, :], mean_var[c][:, a, 0:1], rstd[c][:, a:a + 1],
                                    ALU.subtract, ALU.mult).then_inc(s[f"{name}_done"], 1)

            def elu(name, c):
                exp, relu, dst = (k_exp, k_relu, kT) if name == "k" else (q_exp, q_relu, qT)
                dve.wait_ge(s["exp_parts"], 2 * c + (1 if name == "k" else 2))
                ring.wait_read(dve, name, c)
                V.scalar_tensor_tensor(out=dst[c][:, :], in0=exp[c][:, :], scalar=1.0, in1=relu[c][:, :],
                                       op0=ALU.min, op1=ALU.add).then_inc(s[f"{name}_sb"], 1)

            def first_product(c):
                dve.wait_ge(s["k_sb"], c + 1)
                ring.wait_read(dve, "v", c)
                if c >= 2:
                    dve.wait_ge(s["kv_mm"], D * (c - 2) + 1)
                V.tensor_tensor(p1_0[c][:, :], kT[c][:, :], vT[c][:, :], ALU.mult).then_inc(s["p1_first"], 1)

            def q_times_sums(c):
                dve.wait_ge(s["q_sb"], c + 1)
                src = ring.take(dve, "k_sum", c)
                ring.release("k_sum", c, V.tensor_tensor(qkT[c][:, :], qT[c][:, :], src[:, 0:N], ALU.mult))

            def invert(c):
                src = ring.take(dve, "norm", c)
                ring.release("norm", c, V.reciprocal(norm[c][:, :, :].rearrange("p a h -> p (a h)"), src[:, 0:TILES * H]))
                ring.wait_read(dve, "norm", c)
                V.tensor_copy(norm_d[c][:, :, :, :], norm[c][:, :, :].unsqueeze(2).to_broadcast((P, TILES, D, H)))\
                 .then_inc(s["norm_d_sb"], 1)

            def q_over_norm(c):
                src = ring.take(dve, "norm_back", c)
                ring.release("norm_back", c, V.tensor_tensor(qnT[c][:, :], qT[c][:, :], src[:, 0:N], ALU.mult))

            def second(c, j):
                n = D * c + j
                if j == 0:
                    ring.wait_read(dve, "norm_back", c)
                dve.wait_ge(s["kv_mm"], n + 1)
                if n >= NP1:
                    dve.wait_ge(s["y_step"], n - NP1 + 1)
                V.tensor_tensor(p2[n % NP1][:, :], qnT[c][:, :], kv_bank[n % KVB][:, 0:N], ALU.mult)\
                 .then_inc(s["p2_ready"], 1)

            def add_back(what, c, residual, name):
                src = ring.take(dve, what, c)
                ring.release(what, c, V.tensor_tensor(x2[c][:, :, :].rearrange(flat), residual[c][:, :, :].rearrange(flat),
                                                      src[:, 0:N], ALU.add))
                ring.wait_read(dve, what, c)
                normalise(name, c, x2[c])

            def attended(c):
                add_back("y_back", c, x_sb, "ln2")

            def mlp_added(c):
                dve.wait_ge(s["xx2_sb"], c + 1)
                add_back("mlp_back", c, xx2, "post1")

            def softmax_in(c):
                src = ring.take(dve, "scores", c)[:, 0:TILES * S].rearrange("p (a k) -> p a k", k=S)
                order(V.tensor_reduce(s_max[c][:, :], src, AX.X, ALU.max))
                order.wait()
                ring.release("scores", c, V.tensor_tensor(
                    s_sub[c][:, :, :], src, s_max[c][:, :].unsqueeze(2).to_broadcast((P, TILES, S)), ALU.subtract))

            def softmax_sum(c):
                dve.wait_ge(s["exp_sb"], c + 1)
                order(V.tensor_reduce(s_sum[c][:, :], s_exp[c][:, :, :], AX.X, ALU.add))
                order.wait()
                order(V.reciprocal(s_inv[c][:, :], s_sum[c][:, :]))

            def cross_added(c):
                order.wait()
                src = ring.take(dve, "attend", c)
                dve.wait_ge(s["post1_done"], TILES * (c + 1))
                for a in range(TILES):
                    ins = V.scalar_tensor_tensor(out=x2[c][:, a, :], in0=src[:, C * a:C * (a + 1)],
                                                 scalar=s_inv[c][:, a:a + 1], in1=x3[c][:, a, :],
                                                 op0=ALU.mult, op1=ALU.add)
                    if a < TILES - 1:
                        order(ins)
                ring.release("attend", c, ins)
                order.wait()
                ring.wait_read(dve, "attend", c)
                normalise("post2", c, x2[c])

            def table(name, c):
                return par(name)[:, TOP * TILES * c:TOP * TILES * (c + 1)].rearrange("p (k a) -> p k a", a=TILES)

            def choose(c):
                src = ring.take(dve, "logits", c)
                for a in range(TILES):
                    order(V.max(top_v[c][:, a, :], src[:, E * a:E * (a + 1)]))
                order.wait()
                V.tensor_tensor(gap[c][:, :], top_v[c][:, :, 1], top_v[c][:, :, 0], ALU.subtract)\
                 .then_inc(s["gap_ready"], 1)
                for a in range(TILES):
                    ins = V.max_index(top_i[c][:, a, :], top_v[c][:, a, :], src[:, E * a:E * (a + 1)])
                    if a < TILES - 1:
                        order(ins)
                ring.release("logits", c, ins)
                order.wait()
                ring.wait_read(dve, "logits", c)
                if c == 0:
                    dve.wait_ge(s["context_in"], 16)
                expert = par("expert").unsqueeze(1).to_broadcast((P, TILES, E))
                for i, k in enumerate((0, 1, 1)):
                    V.tensor_tensor(one_hot[c][:, i, :, :], top_i[c][:, :, k:k + 1].to_broadcast((P, TILES, E)), expert,
                                    ALU.is_equal).then_inc(s["hot_ready"], 1)
                order(V.scalar_tensor_tensor(out=from_trash[c][:, :, :], in0=top_i[c][:, :, 0:TOP].rearrange("p a k -> p k a"),
                                             scalar=float(CAP), in1=table("from_trash", c), op0=ALU.mult, op1=ALU.add))

            def weights(c):
                dve.wait_ge(s["gap_tanh_sb"], c + 1)
                for k in range(TOP):
                    order(V.tensor_scalar(pay[k][c][:, :, C + 1], gap_tanh[c][:, :], 0.5 if k == 0 else -0.5, 0.5,
                                          ALU.mult, ALU.add))

            def places_of(c):
                src = ring.take(dve, "ranks", c)[:, 0:3 * TILES * E].rearrange("p (g e) -> p g e", e=E)
                dve.wait_ge(s["hot_ready"], 3 * (c + 1))
                ring.release("ranks", c, V.tensor_tensor(rank_all[c][:, :, :], src,
                                                         one_hot[c][:, :, :, :].rearrange("p s a e -> p (s a) e"), ALU.mult))
                ring.wait_read(dve, "ranks", c)
                order(V.tensor_reduce(rank[c][:, :, :].rearrange("p s a -> p (s a)"), rank_all[c][:, :, :], AX.X, ALU.add))
                order.wait()
                for k, way in enumerate((ALU.add, ALU.subtract)):
                    order(V.tensor_tensor(away[c][:, k, :], from_trash[c][:, k, :], rank[c][:, k, :], way))
                order.wait()
                order(V.scalar_tensor_tensor(out=away_kept[c][:, :, :], in0=rank[c][:, 0:3:2, :], scalar=float(CAP),
                                             in1=away[c][:, :, :], op0=ALU.is_lt, op1=ALU.mult))
                for k in range(TOP):
                    order(V.tensor_scalar(pay[k][c][:, :, C], away[c][:, k, :], -1.0, -float(TOP * T + SLOTS),
                                          ALU.mult, ALU.add))
                order.wait()
                V.tensor_tensor(target[c][:, :, :], away_kept[c][:, :, :], table("trash", c), ALU.add)\
                 .then_inc(s["targets"], 1)

            def ln1(c):
                dve.wait_ge(x_in[c], 16)
                normalise("ln1", c, x_sb[c])

            ln1(0)
            ln1(1)
            scale("ln1", 0, x_sb[0], xn[0])
            ln1(2)
            scale("ln1", 1, x_sb[1], xn[1])
            ln1(3)
            scale("ln1", 2, x_sb[2], xn[2])
            scale("ln1", 3, x_sb[3], xn[3])
            elu("k", 0)
            first_product(0)
            elu("q", 0)
            q_times_sums(0)
            invert(0)
            q_over_norm(0)
            second(0, 0)
            elu("k", 1)
            first_product(1)
            elu("q", 1)
            q_times_sums(1)
            second(0, 1)
            elu("k", 2)
            second(0, 2)
            elu("q", 2)
            invert(1)
            second(0, 3)
            first_product(2)
            q_over_norm(1)
            elu("k", 3)
            q_times_sums(2)
            for j in range(4, 8):
                second(0, j)
            second(1, 0)
            first_product(3)
            for j in range(1, 4):
                second(1, j)
            invert(2)
            attended(0)
            for j in range(4, 6):
                second(1, j)
            q_over_norm(2)
            scale("ln2", 0, x2[0], xn[0])
            for j in range(6, 8):
                second(1, j)
            second(2, 0)
            attended(1)
            for j in range(1, 4):
                second(2, j)
            scale("ln2", 1, x2[1], xn[1])
            mlp_added(0)
            second(2, 4)
            scale("post1", 0, x2[0], x3[0])
            second(2, 5)
            softmax_in(0)
            second(2, 6)
            elu("q", 3)
            second(2, 7)
            q_times_sums(3)
            softmax_sum(0)
            invert(3)
            cross_added(0)
            q_over_norm(3)
            for j in range(0, 2):
                second(3, j)
            scale("post2", 0, x2[0], pay[0][0])
            second(3, 2)
            mlp_added(1)
            second(3, 3)
            attended(2)
            scale("post1", 1, x2[1], x3[1])
            second(3, 4)
            choose(0)
            scale("ln2", 2, x2[2], xn[2])
            weights(0)
            softmax_in(1)
            second(3, 5)
            places_of(0)
            second(3, 6)
            softmax_sum(1)
            second(3, 7)
            cross_added(1)
            attended(3)
            scale("post2", 1, x2[1], pay[0][1])
            scale("ln2", 3, x2[3], xn[3])
            mlp_added(2)
            choose(1)
            scale("post1", 2, x2[2], x3[2])
            weights(1)
            places_of(1)
            softmax_in(2)
            mlp_added(3)
            softmax_sum(2)
            scale("post1", 3, x2[3], x3[3])
            cross_added(2)
            softmax_in(3)
            softmax_sum(3)
            scale("post2", 2, x2[2], pay[0][2])
            cross_added(3)
            choose(2)
            scale("post2", 3, x2[3], pay[0][3])
            weights(2)
            places_of(2)
            choose(3)
            weights(3)
            places_of(3)

            def take_in(w, part):
                n0, n1 = IN_PARTS[part]
                src = side.take(dve, f"in{part}", w)
                if w >= 2 and part == 0:
                    ring.wait_read(dve, f"expert_fc{FC - 1}", 2 * w - 3)
                at = slice(P * n0, P * n1)
                dve.wait_ge(s["in_hi_sb"], 2 * w + part + 1)
                side.release(f"in{part}", w, V.tensor_tensor(in_lo[w % 2][:, at], src[:, 0:P * (n1 - n0)],
                                                             in_hi[w % 2][:, at].bitcast(F32), ALU.subtract))
                if part:
                    for loaded in rows_loaded[w % 2]:
                        dve.wait_ge(loaded, 16 * (w // 2 + 1))
                    V.tensor_tensor(send_to[:, w, :], rows_in[w % 2][:, :, C], par("slot")[:, PT * w:PT * (w + 1)],
                                    ALU.add).then_inc(s["send_ready"], 1)
                    V.tensor_copy(send_w[:, w, :], rows_in[w % 2][:, :, C + 1]).then_inc(s["send_ready"], 1)

            def expert_out(e):
                w = e // 2
                src = side.take(dve, "expert_proj", e)
                if w >= 2 and e % 2 == 0:
                    side.wait_read(dve, "out1", w - 2)
                side.release("expert_proj", e, V.tensor_copy(outT[w % 2][:, CAP * (e % 2):CAP * (e % 2 + 1)], src[:, 0:CAP]))

            def hand_out(w, part):
                tiles = ((0, 1), (2, 3, 4))[part]
                src = side.take(dve, f"out{part}", w)
                dve.wait_ge(s["send_ready"], 2 * (w + 1))
                if w >= 2 and part == 0:
                    dve.wait_ge(results_sent[w % 2], 16 * PT * (w // 2))
                for i in tiles:
                    at = P * (i - 2 * part)
                    ins = V.tensor_scalar(rows_out[w % 2][:, i, :], src[:, at:at + P], send_w[:, w, i:i + 1], None,
                                          ALU.mult)
                    if i < tiles[-1]:
                        ins.then_inc(s["out_sb"], 1)
                side.release(f"out{part}", w, ins)

            for e in range(E):
                dve.wait_ge(s["fc_hi_sb"], e + 1)
                V.tensor_tensor(c_fc_lo[:, e, :], fc_in[e // 2][:, e % 2, :], c_fc_hi[:, e, :].bitcast(F32), ALU.subtract)\
                 .then_inc(s["fc_lo_sb"], 1)
            take_in(0, 0)
            take_in(0, 1)
            for w in range(PAIRS):
                if w + 1 < PAIRS:
                    take_in(w + 1, 0)
                    take_in(w + 1, 1)
                if w:
                    hand_out(w - 1, 1)
                expert_out(2 * w)
                hand_out(w, 0)
                expert_out(2 * w + 1)
            hand_out(PAIRS - 1, 1)

            def both_added(c):
                src = ring.take(dve, "sum", c)
                dve.wait_ge(got_in[c], 16)
                ring.release("sum", c, V.tensor_tensor(x2[c][:, :, :].rearrange(flat), src[:, 0:N],
                                                       got[c][:, 1, :, :].rearrange(flat), ALU.add))

            for c in range(CH + 2):
                if c >= 2:
                    for a in range(TILES):
                        order.wait(TILES)
                        order(V.bn_aggr(mean_var[c - 2][:, a, :], stats[c - 2][:, a, :]))
                if c < CH:
                    both_added(c)
                if c >= 2:
                    order.wait()
                    V.tensor_scalar(var_eps[c - 2][:, :], mean_var[c - 2][:, :, 1], EPS, None, ALU.add)\
                     .then_inc(s["post3_var"], 1)
                    if c - 2 < CH - 1:
                        V.tensor_scalar(minus_mean[c - 2][:, :], mean_var[c - 2][:, :, 0], -1.0, None, ALU.mult)\
                         .then_inc(s["minus_mean_sb"], 1)
                if 1 <= c <= CH:
                    ring.wait_read(dve, "sum", c - 1)
                    for a in range(TILES):
                        order(V.bn_stats(stats[c - 1][:, a, :], x2[c - 1][:, a, :]))
            dve.wait_ge(s["post3_rstd"], CH)
            for a in range(TILES):
                V.tensor_scalar(xn[CH - 1][:, a, :], x2[CH - 1][:, a, :], mean_var[CH - 1][:, a, 0:1],
                                rstd[CH - 1][:, a:a + 1], ALU.subtract, ALU.mult).then_inc(s["last_done"], 1)


def kernel(**inputs):
    import concourse.bacc as bacc
    from concourse.bass_utils import run_bass_kernel_spmd

    a = {k: np.asarray(v) for k, v in inputs.items()}
    f32 = np.float32
    dh = np.arange(C).reshape(H, D).T.reshape(-1)

    def column(v):
        return v.reshape(-1, P).T

    def pack(columns, parts):
        return np.concatenate([parts[name] for name in columns], axis=1)

    table = constants()
    qkv = np.concatenate([a[f"L0_attn_{n}_w"][dh].T for n in "qkv"], axis=1)
    early = pack(EARLY, dict(
        table, ln1_w=column(a["L0_attn_ln1_w"]), ln1_b=column(a["L0_attn_ln1_b"]),
        q_b=column(a["L0_attn_q_b"][dh]), k_b=column(a["L0_attn_k_b"][dh]), v_b=column(a["L0_attn_v_b"][dh]),
        o_b=column(a["L0_attn_o_b"]), ln2_w=column(a["L0_attn_ln2_w"]), ln2_b=column(a["L0_attn_ln2_b"]),
        fc_b=column(a["L0_attn_fc_b"]), proj_b=column(a["L0_attn_proj_b"]), qkv=qkv))
    bv = np.zeros((P, C), f32)
    bv[0] = a["L0_xattn_bv"]
    context = pack(CONTEXT, dict(
        table, ctxT=np.tile(a["ctx_1024"], (1, TILES, 1)).reshape(-1, C).T, Wk=a["L0_xattn_Wk"], Wv=a["L0_xattn_Wv"],
        WqT=a["L0_xattn_Wq"].T, bk=column(a["L0_xattn_bk"]), bq=column(a["L0_xattn_bq"]), bv=bv,
        w_g=a["L0_ffn_w_g"]))
    d, h = np.arange(C) // H, np.arange(C) % H
    wo_rot = np.stack([a["L0_attn_o_w"].T[h * D + (d + j) % D] for j in range(D)], axis=1)
    mlp = pack(MLP, dict(fcT=a["L0_attn_fc_w"].T,
                         projT=a["L0_attn_proj_w"].T.reshape(FC, P, C).transpose(1, 0, 2).reshape(P, FC * C)))
    c_fc = a["L0_ffn_c_fc"].transpose(1, 0, 2)
    c_proj = a["L0_ffn_c_proj"].reshape(E, FC, P, C).transpose(2, 0, 1, 3)
    arrays = dict(x=a["x"], early=early, context=context, wo_rot=wo_rot, mlp=mlp, c_fc=c_fc, c_proj=c_proj)
    arrays = {k: np.ascontiguousarray(v) for k, v in arrays.items()}

    nc = bacc.Bacc("TRN2", target_bir_lowering=False, num_devices=1)
    ins = [nc.dram_tensor(k, v.shape, F32, kind="ExternalInput").ap() for k, v in arrays.items()]
    out = nc.dram_tensor("out", (B, L, C), F32, kind="ExternalOutput").ap()
    program(nc, *ins, out)
    r = run_bass_kernel_spmd(nc, [arrays], core_ids=[0])
    return r.results[0]["out"]
```

```python
import numpy as np
import concourse.bass as bass
from concourse import mybir
from contextlib import ExitStack

F32, F32R, BF16, U32 = mybir.dt.float32, mybir.dt.float32r, mybir.dt.bfloat16, mybir.dt.uint32
ALU, ACT, AX = mybir.AluOpType, mybir.ActivationFunctionType, mybir.AxisListType

P = 128
C = 128
B, L = 2, 512
CH, N = 4, 256
TILES = N // P
T = B * L
H, D = 16, 8
MW = 4 * C
FC = MW // P
S = 32
E, TOP = 8, 2
CAP = 2 * 5 * T // (4 * E)
GROUPS = TOP * T // P
SLOTS = E * CAP
PAIRS = E // 2
PT = 2 * CAP // P
ROW = C + 2
EPS = 1e-5
KVB = 3
ZREP = 4
ZW = SLOTS * ROW // P // ZREP
WARM = 15
NP1 = 4

CONTEXT = dict(ctxT=B * TILES * S, Wk=C, Wv=C, WqT=C, bk=1, bq=1, bv=C, quad=TILES)
EARLY = dict(ident=P, ln1_w=1, ln1_b=1, q_b=1, k_b=1, v_b=1, o_b=1, ln2_w=1, ln2_b=1, fc_b=FC, proj_b=1,
             qkv=3 * C, same_d=P, head=H)
ROUTING = dict(w_g=E, tri=P, expert=E, from_trash=GROUPS, trash=GROUPS, slot=PAIRS * PT)
MLP = dict(fcT=MW, projT=FC * C)


def places(columns):
    at, out = 0, {}
    for name, n in columns.items():
        out[name] = (at, at + n)
        at += n
    return out, at


def constants():
    p = np.arange(P)
    d_of, h_of = p // H, p % H
    same_d = d_of[:, None] == d_of[None]
    head = h_of[:, None] == np.arange(H)[None]
    quad = (p // S)[:, None] == np.arange(TILES)[None]
    row = p[:, None, None, None] + P * np.arange(GROUPS).reshape(CH, TOP, TILES)[None]
    trash = SLOTS + row
    last = (CAP - 1) * np.arange(TOP)[None, None, :, None]
    slot = p[:, None] + P * np.arange(PAIRS * PT)[None]
    tables = dict(ident=np.eye(P), same_d=same_d, head=head, quad=quad, tri=p[:, None] < p[None],
                  expert=np.tile(np.arange(E), (P, 1)), from_trash=last - trash, trash=trash, slot=slot + TOP * T)
    return {k: np.asarray(v, np.float32).reshape(P, -1) for k, v in tables.items()}


def program(nc, x, context, early, routing, wo_rot, mlp, c_fc, c_proj, out):
    at_early, n_early = places(EARLY)
    at_context, n_context = places(CONTEXT)
    at_routing, n_routing = places(ROUTING)
    at_mlp, n_mlp = places(MLP)
    ctx = ExitStack()
    with ctx:
        def sb(name, shape, dt=F32):
            return (for_a_time or ctx).enter_context(nc.sbuf_tensor(name, shape, dt))

        for_a_time = None

        def sem(name):
            return ctx.enter_context(nc.semaphore(name))

        v_twice = nc.dram_tensor("v_twice", (CH, 2, P, N), F32, kind="Internal").ap()
        slots = nc.dram_tensor("slots", (SLOTS + TOP * T, ROW), F32, kind="Internal").ap()
        results = nc.dram_tensor("results", (TOP * T + SLOTS, C), F32, kind="Internal").ap()

        early_sb = sb("early_sb", [P, n_early])
        context_sb = sb("context_sb", [P, n_context])
        routing_sb = sb("routing_sb", [P, n_routing])
        mlp_sb = sb("mlp_sb", [P, n_mlp])
        wo_sb = sb("wo_sb", [P, D, C])
        c_fc_hi = sb("c_fc_hi", [P, E, MW], F32R)
        c_fc_lo = sb("c_fc_lo", [P, E, MW], F32R)
        c_proj_sb = sb("c_proj_sb", [P, E, FC, C])

        def par(name):
            for sbuf, at in ((early_sb, at_early), (context_sb, at_context), (routing_sb, at_routing),
                             (mlp_sb, at_mlp)):
                if name in at:
                    return sbuf[:, at[name][0]:at[name][1]]
            raise KeyError(name)

        def by_chunk(name, shape, dt=F32):
            return [sb(f"{name}{c}", shape, dt) for c in range(CH)]

        def by_turn(name, shape, dt=F32):
            two = [sb(f"{name}{i}", shape, dt) for i in range(2)]
            return [two[c % 2] for c in range(CH)]

        zeros = sb("zeros", [P, ZW])
        minus_half = sb("minus_half", [P, TILES])
        warm = sb("warm", [P, TILES])
        ones_row = sb("ones_row", [1, P])
        ones_bf = sb("ones_bf", [P, P], BF16)
        tri_bf = sb("tri_bf", [P, P], BF16)

        x_sb = by_chunk("x_sb", [P, TILES, C])
        xn = by_chunk("xn", [P, TILES, C])
        xnT = by_chunk("xnT", [P, N])
        stats = by_chunk("stats", [P, TILES, 6])
        mean_var = by_chunk("mean_var", [P, TILES, 2])
        var_eps = by_chunk("var_eps", [P, TILES])
        rstd = by_chunk("rstd", [P, TILES])
        late = sb("late", [P, 2 * (D - 1) * N])
        v_rot = [late[:, (D - 1) * N * i:(D - 1) * N * (i + 1)].rearrange("p (j t) -> p j t", t=N) for i in range(2)]
        got = [late[:, TOP * N * c:TOP * N * (c + 1)].rearrange("p (k a c) -> p k a c", k=TOP, a=TILES) for c in range(CH)]
        fc_in = [late[:, 2 * MW * i:2 * MW * (i + 1)].rearrange("p (e f) -> p e f", e=2) for i in (0, 1, 2, 0)]
        norm = by_chunk("norm", [P, TILES, H])
        norm_d = by_chunk("norm_d", [P, TILES, D, H])
        x2 = by_chunk("x2", [P, TILES, C])
        x3 = by_chunk("x3", [P, TILES, C])
        KT = sb("KT", [P, B * S])
        WqK = sb("WqK", [P, B * S])
        bqK = sb("bqK", [1, B * S])
        V_tile = [sb(f"V_tile{b}", [TILES * S, TILES, C]) for b in range(B)]
        s_max = by_chunk("s_max", [P, TILES])
        s_sub = by_chunk("s_sub", [P, TILES, S])
        s_exp = by_chunk("s_exp", [P, TILES, S])
        s_sum = by_chunk("s_sum", [P, TILES])
        s_inv = by_chunk("s_inv", [P, TILES])
        expT = by_chunk("expT", [TILES * S, P])
        pay = [by_chunk(f"pay{k}_", [P, TILES, ROW]) for k in range(TOP)]
        top_v = by_chunk("top_v", [P, TILES, 8])
        top_i = by_chunk("top_i", [P, TILES, 8], U32)
        gap = by_chunk("gap", [P, TILES])
        gap_tanh = by_chunk("gap_tanh", [P, TILES])
        one_hot = by_chunk("one_hot", [P, 3, TILES, E], BF16)
        rank_all = by_chunk("rank_all", [P, 3 * TILES, E])
        rank = by_chunk("rank", [P, 3, TILES])
        from_trash = by_chunk("from_trash", [P, TOP, TILES])
        away = by_chunk("away", [P, TOP, TILES])
        away_kept = by_chunk("away_kept", [P, TOP, TILES])
        target = by_chunk("target", [P, TOP, TILES], U32)
        minus_mean = by_chunk("minus_mean", [P, TILES])
        shift = by_chunk("shift", [P, TILES])
        rows_in = [sb(f"rows_in{i}", [P, PT, ROW]) for i in range(2)]
        send_to = sb("send_to", [P, PAIRS, PT], U32)
        send_w = sb("send_w", [P, PAIRS, PT])
        in_hi = [sb(f"in_hi{i}", [P, 2 * CAP], F32R) for i in range(2)]
        in_lo = [sb(f"in_lo{i}", [P, 2 * CAP], F32R) for i in range(2)]
        he_hi = [sb(f"he_hi{i}", [P, FC, CAP], F32R) for i in range(2)]
        outT = [sb(f"outT{i}", [P, 2 * CAP]) for i in range(2)]
        rows_out = [late[:, TOP * N * CH + PT * C * i:TOP * N * CH + PT * C * (i + 1)].rearrange("p (i c) -> p i c", c=C)
                    for i in range(2)]

        with ExitStack() as for_a_time:
            k_exp = by_turn("k_exp", [P, N])
            q_exp = by_turn("q_exp", [P, N])
            k_relu = by_turn("k_relu", [P, N])
            q_relu = by_turn("q_relu", [P, N])
            kT = by_chunk("kT", [P, N])
            qT = by_chunk("qT", [P, N])
            vT = by_chunk("vT", [P, N])
            qkT = by_turn("qkT", [P, N])
            qnT = by_chunk("qnT", [P, N])
            p1_0 = by_turn("p1_0", [P, N])
            p1 = [sb(f"p1_{i}", [P, N]) for i in range(NP1)]
            p2 = [sb(f"p2_{i}", [P, N]) for i in range(NP1)]
            yT = by_chunk("yT", [P, N])
            xx2 = by_chunk("xx2", [P, TILES, C])
            hT = by_turn("hT", [P, FC, N])
        for_a_time = None
        c_proj_hi = sb("c_proj_hi", [P, E, FC, C], F32R)
        c_proj_lo = sb("c_proj_lo", [P, E, FC, C], F32R)
        he = [sb(f"he{f}", [P, CAP]) for f in range(FC)]
        he_lo = [sb(f"he_lo{i}", [P, FC, CAP], F32R) for i in range(2)]

        bank = [ctx.enter_context(nc.psum_tensor(f"bank{i}", [P, 512], F32)) for i in range(8)]
        kv_bank, y_bank = bank[4:4 + KVB], bank[7]

        names = """early_in context_in routing_in wo_in mlp_in zero_slots zero_results
            pool_order dve_order act_order pool_consts filled
            ln1_var ln1_rstd ln1_done ln2_var ln2_rstd ln2_done post1_var post1_rstd post1_done
            post2_var post2_rstd post2_done post3_var post3_rstd post3_done
            exp_parts k_sb q_sb norm_d_sb p1_first p1_rest kv_mm p2_ready y_step y_sb xx2_sb
            V_tile_sb exp_sb pay1_sb gap_ready gap_tanh_sb hot_ready
            minus_mean_sb shift_sb targets first_sent last_done fc_hi_sb fc_lo_sb proj_hi_sb proj_lo_sb
            in_hi_sb he_hi_sb he_lo_sb send_ready out_sb out_stored"""
        s = {name: sem(name) for name in names.split()}
        x_in = [sem(f"x_in{c}") for c in range(CH)]
        fc_loaded = [sem(f"fc_loaded{w}") for w in range(PAIRS)]
        proj_loaded = [sem(f"proj_loaded{w}") for w in range(PAIRS)]
        v_stored = [sem(f"v_stored{c}") for c in range(CH)]
        v_back = [[sem(f"v_back{i}_{part}") for part in range(2)] for i in range(2)]
        results_sent = [sem(f"results_sent{i}") for i in range(2)]
        rows_loaded = [[sem(f"rows_loaded{i}_{part}") for part in range(2)] for i in range(2)]
        second_sent = [sem(f"second_sent{c}") for c in range(CH)]
        got_in = [sem(f"got_in{c}") for c in range(CH)]
        IN_PARTS = ((0, 3), (3, PT))
        V_PARTS = ((1, 4), (4, 8))

        class Order:

            def __init__(self, eng, semaphore):
                self.eng, self.sem, self.n = eng, semaphore, 0

            def __call__(self, ins):
                self.n += 1
                ins.then_inc(self.sem, 1)
                return self.n

            def wait_for(self, n):
                self.eng.wait_ge(self.sem, n)

            def wait(self):
                self.wait_for(self.n)

        class Ring:

            fillings = 0

            def __init__(self, name, banks):
                self.banks, self.n, self.at = banks, 0, {}
                self.read = [sem(f"{name}{i}_read") for i in range(len(banks))]

            def claim(self, pe, what, c):
                i, turn = self.n % len(self.banks), self.n // len(self.banks)
                self.at[what, c] = (i, turn)
                self.n += 1
                if turn:
                    pe.wait_ge(self.read[i], turn)
                return self.banks[i]

            def fill(self, what, c, last):
                Ring.fillings += 1
                self.at[what, c] += (Ring.fillings,)
                last.then_inc(s["filled"], 1)

            def take(self, eng, what, c):
                i, _, n = self.at[what, c]
                eng.wait_ge(s["filled"], n)
                return self.banks[i]

            def release(self, what, c, reader):
                reader.then_inc(self.read[self.at[what, c][0]], 1)

            def wait_read(self, eng, what, c):
                i, turn, _ = self.at[what, c]
                eng.wait_ge(self.read[i], turn + 1)

        Ring.fillings = 0
        ring = Ring("ring", bank[:4])
        side = Ring("side", bank[4:8])
        block = ctx.enter_context(nc.Block())

        @block.tensor
        def _(pe):
            M, TR = nc.tensor.matmul, nc.tensor.transpose
            ident = par("ident")

            def turn(what, c, tile):
                dst = ring.claim(pe, what, c)
                for a in range(TILES):
                    last = TR(dst[:, P * a:P * (a + 1)], tile(a), ident)
                ring.fill(what, c, last)

            def ln1_in(c):
                if c == 0:
                    pe.wait_ge(s["early_in"], 16)
                pe.wait_ge(s["ln1_done"], TILES * (c + 1))
                turn("ln1T", c, lambda a: xn[c][:, a, :])

            def head_in(name, c):
                i = "qkv".index(name)
                ring.wait_read(pe, "ln1T", c)
                dst = ring.claim(pe, name, c)
                ring.fill(name, c, M(dst[:, 0:N], par("qkv")[:, C * i:C * (i + 1)], xnT[c][:, :], start=True, stop=True))

            def head_sums(c):
                pe.wait_ge(s["k_sb"], c + 1)
                dst = ring.claim(pe, "k_sum", c)
                ring.fill("k_sum", c, M(dst[:, 0:N], par("same_d"), kT[c][:, :], start=True, stop=True))

            def norm_sums(c):
                ring.wait_read(pe, "k_sum", c)
                dst = ring.claim(pe, "norm", c)
                for a in range(TILES):
                    last = M(dst[:, H * a:H * (a + 1)], qkT[c][:, P * a:P * (a + 1)], par("head"), start=True, stop=True)
                ring.fill("norm", c, last)

            def norm_back(c):
                pe.wait_ge(s["norm_d_sb"], c + 1)
                turn("norm_back", c, lambda a: norm_d[c][:, a, :, :].rearrange("p d h -> p (d h)"))

            def kv(c, j):
                n = D * c + j
                if j == 0:
                    pe.wait_ge(s["p1_first"], c + 1)
                else:
                    pe.wait_ge(s["p1_rest"], (D - 1) * c + j)
                if n >= KVB:
                    pe.wait_ge(s["p2_ready"], n - KVB + 1)
                src = p1_0[c] if j == 0 else p1[((D - 1) * c + j - 1) % NP1]
                M(kv_bank[n % KVB][:, 0:N], par("same_d"), src[:, :], start=True, stop=True).then_inc(s["kv_mm"], 1)

            def y_part(c, j):
                n = D * c + j
                pe.wait_ge(s["p2_ready"], n + 1)
                if n == 0:
                    pe.wait_ge(s["wo_in"], 16)
                if j == 0 and c:
                    pe.wait_ge(s["y_sb"], c)
                M(y_bank[:, 0:N], wo_sb[:, j, :], p2[n % NP1][:, :], start=(j == 0), stop=(j == D - 1))\
                    .then_inc(s["y_step"], 1)

            def y_back(c):
                pe.wait_ge(s["y_sb"], c + 1)
                turn("y_back", c, lambda a: yT[c][:, P * a:P * (a + 1)])

            def ln2_in(c):
                pe.wait_ge(s["ln2_done"], TILES * (c + 1))
                turn("ln2T", c, lambda a: xn[c][:, a, :])

            def fc(c, f):
                ring.wait_read(pe, "ln2T", c)
                if c == f == 0:
                    pe.wait_ge(s["mlp_in"], 16)
                dst = ring.claim(pe, f"fc{f}", c)
                ring.fill(f"fc{f}", c, M(dst[:, 0:N], par("fcT")[:, P * f:P * (f + 1)], xnT[c][:, :],
                                         start=True, stop=True))

            mlp_bank = {}

            def proj(c, f):
                if f == 0:
                    mlp_bank[c] = ring.claim(pe, "proj", c)
                ring.wait_read(pe, f"fc{f}", c)
                last = M(mlp_bank[c][:, 0:N], par("projT")[:, C * f:C * (f + 1)], hT[c][:, f, :], start=(f == 0),
                         stop=(f == FC - 1))
                if f == FC - 1:
                    ring.fill("proj", c, last)

            def mlp_back(c):
                ring.wait_read(pe, "proj", c)
                turn("mlp_back", c, lambda a: yT[c][:, P * a:P * (a + 1)])

            def cross_in(c):
                pe.wait_ge(s["post1_done"], TILES * (c + 1))
                turn("x3T", c, lambda a: x3[c][:, a, :])

            def scores(c):
                if c == 0:
                    ring.wait_read(pe, "WqK", 0)
                    ring.wait_read(pe, "bqK", 0)
                dst, b = ring.claim(pe, "scores", c), c * N // L
                keys = slice(S * b, S * (b + 1))
                M(dst[:, 0:TILES * S], ones_row[:, :], bqK[:, keys].unsqueeze(1).to_broadcast((1, TILES, S)),
                  start=True, stop=False)
                ring.wait_read(pe, "x3T", c)
                for a in range(TILES):
                    last = M(dst[:, S * a:S * (a + 1)], xnT[c][:, P * a:P * (a + 1)], WqK[:, keys], start=False,
                             stop=(a == TILES - 1))
                ring.fill("scores", c, last)

            def weights_turned(c):
                pe.wait_ge(s["exp_sb"], c + 1)
                dst = ring.claim(pe, "expT", c)
                ring.fill("expT", c, TR(dst[0:TILES * S, 0:P], s_exp[c][:, :, :].rearrange("p a k -> p (a k)"), ident))

            def attend(c):
                ring.wait_read(pe, "expT", c)
                if c == 0:
                    pe.wait_ge(s["V_tile_sb"], B * (TILES - 1))
                    ring.wait_read(pe, "V", B - 1)
                dst, b = ring.claim(pe, "attend", c), c * N // L
                ring.fill("attend", c, M(dst[:, 0:N], expT[c][:, :], V_tile[b][:, :, :].rearrange("p a c -> p (a c)"),
                                         start=True, stop=True))

            def route_in(c):
                pe.wait_ge(s["post2_done"], TILES * (c + 1))
                turn("x4T", c, lambda a: pay[0][c][:, a, 0:C])

            def logits_of(c):
                if c == 0:
                    pe.wait_ge(s["routing_in"], 16)
                ring.wait_read(pe, "x4T", c)
                dst = ring.claim(pe, "logits", c)
                for a in range(TILES):
                    last = M(dst[:, E * a:E * (a + 1)], xnT[c][:, P * a:P * (a + 1)], par("w_g"), start=True, stop=True)
                ring.fill("logits", c, last)

            def count(c):
                ranks = ring.claim(pe, "ranks", c)[:, 0:3 * TILES * E].rearrange("p (s a e) -> p s a e", s=3, a=TILES)

                def ones_times(dst, rows, start=False, stop=False):
                    return M(dst, ones_bf[:, :], rows.to_broadcast((P, *dst.shape[1:])), start=start, stop=stop)

                for b in range(c):
                    for a in range(TILES):
                        ones_times(ranks, one_hot[b][:, :, a:a + 1, :], start=(b == a == 0))
                        ones_times(ranks[:, 2:3, :, :], one_hot[b][:, 0:1, a:a + 1, :])
                pe.wait_ge(s["hot_ready"], 3 * (c + 1))
                M(ranks, tri_bf[:, :], one_hot[c][:, :, :, :], start=(c == 0), stop=False)
                ones_times(ranks[:, :, 1:2, :], one_hot[c][:, :, 0:1, :])
                for a in range(TILES):
                    last = ones_times(ranks[:, 2:3, :, :], one_hot[c][:, 0:1, a:a + 1, :], stop=(a == TILES - 1))
                ring.fill("ranks", c, last)

            def context_key():
                pe.wait_ge(s["context_in"], 16)
                dst = ring.claim(pe, "KT", 0)
                ring.fill("KT", 0, M(dst[:, 0:B * S], par("Wk"),
                                     par("ctxT").rearrange("p (b a k) -> p b a k", b=B, a=TILES)[:, :, 0, :],
                                     start=True, stop=True))

            def context_value(b):
                pe.wait_ge(s["context_in"], 16)
                pe.wait_ge(s["pool_order"], 3)
                dst = ring.claim(pe, "V", b)[0:TILES * S, 0:C]
                rows = slice(TILES * S * b, TILES * S * (b + 1))
                M(dst, par("ctxT")[:, rows], par("Wv"), start=True, stop=False)
                ring.fill("V", b, M(dst, ones_row[:, 0:TILES * S], par("bv")[0:1, :], start=False, stop=True))

            def keys_times_Wq():
                ring.wait_read(pe, "KT", 0)
                dst = ring.claim(pe, "WqK", 0)
                ring.fill("WqK", 0, M(dst[:, 0:B * S], par("WqT"), KT[:, :], start=True, stop=True))

            def keys_times_bq():
                ring.wait_read(pe, "KT", 0)
                dst = ring.claim(pe, "bqK", 0)
                ring.fill("bqK", 0, M(dst[0:1, 0:B * S], par("bq"), KT[:, :], start=True, stop=True))

            context_key()
            context_value(0)
            keys_times_bq()
            ln1_in(0)
            context_value(1)
            keys_times_Wq()
            head_in("v", 0)
            head_in("k", 0)
            ln1_in(1)
            head_in("q", 0)
            ln1_in(2)
            ln1_in(3)
            head_sums(0)
            kv(0, 0)
            head_in("v", 1)
            head_in("v", 2)
            head_in("k", 1)
            norm_sums(0)
            head_in("q", 1)
            head_in("v", 3)
            head_in("k", 2)
            norm_back(0)
            head_sums(1)
            head_in("q", 2)
            kv(0, 1)
            norm_sums(1)
            kv(0, 2)
            head_sums(2)
            for j in range(3, 5):
                kv(0, j)
            norm_back(1)
            head_in("k", 3)
            kv(0, 5)
            norm_sums(2)
            kv(0, 6)
            head_in("q", 3)
            head_sums(3)
            for j in range(0, 5):
                y_part(0, j)
            kv(0, 7)
            for j in range(5, 8):
                y_part(0, j)
            norm_back(2)
            for j in range(0, 3):
                kv(1, j)
            y_part(1, 0)
            kv(1, 3)
            for j in range(1, 4):
                y_part(1, j)
            for j in range(4, 6):
                kv(1, j)
            y_back(0)
            kv(1, 6)
            for j in range(4, 7):
                y_part(1, j)
            kv(1, 7)
            for j in range(0, 2):
                kv(2, j)
            y_part(1, 7)
            for j in range(2, 4):
                kv(2, j)
            for j in range(0, 4):
                y_part(2, j)
            ln2_in(0)
            kv(2, 4)
            y_back(1)
            kv(2, 5)
            fc(0, 0)
            for j in range(4, 6):
                y_part(2, j)
            for f in range(1, 3):
                fc(0, f)
            kv(2, 6)
            fc(0, 3)
            kv(2, 7)
            ln2_in(1)
            y_part(2, 6)
            proj(0, 0)
            y_part(2, 7)
            for f in range(0, 2):
                fc(1, f)
            y_back(2)
            for f in range(1, 4):
                proj(0, f)
            for j in range(0, 2):
                kv(3, j)
            mlp_back(0)
            for f in range(2, 4):
                fc(1, f)
            ln2_in(2)
            kv(3, 2)
            norm_sums(3)
            proj(1, 0)
            fc(2, 0)
            proj(1, 1)
            norm_back(3)
            fc(2, 1)
            for f in range(2, 4):
                proj(1, f)
            for j in range(0, 2):
                y_part(3, j)
            cross_in(0)
            y_part(3, 2)
            mlp_back(1)
            kv(3, 3)
            scores(0)
            y_part(3, 3)
            for j in range(4, 7):
                kv(3, j)
            y_part(3, 4)
            kv(3, 7)
            y_part(3, 5)
            cross_in(1)
            for j in range(6, 8):
                y_part(3, j)
            scores(1)
            weights_turned(0)
            y_back(3)
            for f in range(2, 4):
                fc(2, f)
            attend(0)
            weights_turned(1)
            for f in range(0, 4):
                proj(2, f)
            ln2_in(3)
            attend(1)
            mlp_back(2)
            fc(3, 0)
            route_in(0)
            for f in range(1, 3):
                fc(3, f)
            logits_of(0)
            fc(3, 3)
            for f in range(0, 3):
                proj(3, f)
            count(0)
            route_in(1)
            proj(3, 3)
            cross_in(2)
            mlp_back(3)
            scores(2)
            logits_of(1)
            count(1)
            weights_turned(2)
            cross_in(3)
            attend(2)
            scores(3)
            weights_turned(3)
            attend(3)
            route_in(2)
            logits_of(2)
            count(2)
            route_in(3)
            logits_of(3)
            count(3)

            pe.wait_ge(s["fc_hi_sb"], 6)
            for _ in range(WARM):
                M(y_bank[:, :], c_fc_hi[:, 0, 0:P], c_fc_hi[:, 0, :], start=True, stop=True)

            def rows_turned(w, part):
                pe.wait_ge(rows_loaded[w % 2][part], 16 * (w // 2 + 1))
                dst = side.claim(pe, f"in{part}", w)
                for i in ((0, 1, 2), (3, 4))[part]:
                    last = TR(dst[:, P * (i - 3 * part):P * (i - 3 * part + 1)], rows_in[w % 2][:, i, 0:C], ident)
                side.fill(f"in{part}", w, last)

            def expert_fc(e, f):
                w = e // 2
                at = slice(CAP * (e % 2), CAP * (e % 2 + 1))
                if f == 0:
                    pe.wait_ge(s["in_hi_sb"], e + 1)
                    pe.wait_ge(s["fc_lo_sb"], e + 1)
                dst = ring.claim(pe, f"expert_fc{f}", e)[:, 0:CAP]
                hi, lo = c_fc_hi[:, e, P * f:P * (f + 1)], c_fc_lo[:, e, P * f:P * (f + 1)]
                M(dst, hi, in_hi[w % 2][:, at], start=True, stop=False)
                M(dst, lo, in_hi[w % 2][:, at], start=False, stop=False)
                if f == 0:
                    side.wait_read(pe, f"in{e % 2}", w)
                ring.fill(f"expert_fc{f}", e, M(dst, hi, in_lo[w % 2][:, at], start=False, stop=True))

            proj_bank = {}

            def expert_proj(e, f):
                if f == 0:
                    proj_bank[e] = side.claim(pe, "expert_proj", e)[:, 0:CAP]
                    pe.wait_ge(s["proj_lo_sb"], e + 1)
                dst, hi, lo = proj_bank[e], c_proj_hi[:, e, f, :], c_proj_lo[:, e, f, :]
                pe.wait_ge(s["he_hi_sb"], FC * e + f + 1)
                M(dst, hi, he_hi[e % 2][:, f, :], start=(f == 0), stop=False)
                M(dst, lo, he_hi[e % 2][:, f, :], start=False, stop=False)
                pe.wait_ge(s["he_lo_sb"], FC * e + f + 1)
                last = M(dst, hi, he_lo[e % 2][:, f, :], start=False, stop=(f == FC - 1))
                if f == FC - 1:
                    side.fill("expert_proj", e, last)

            def results_turned(w, part):
                side.wait_read(pe, "expert_proj", 2 * w + part)
                dst = side.claim(pe, f"out{part}", w)
                for i in ((0, 1), (2, 3, 4))[part]:
                    last = TR(dst[:, P * (i - 2 * part):P * (i - 2 * part + 1)], outT[w % 2][:, P * i:P * (i + 1)], ident)
                side.fill(f"out{part}", w, last)

            pe.wait_ge(s["p2_ready"], CH * D)
            pe.wait_ge(s["y_sb"], CH)
            rows_turned(0, 0)
            rows_turned(0, 1)
            rows_turned(1, 0)
            expert_fc(0, 0)
            rows_turned(1, 1)
            for f in range(1, 4):
                expert_fc(0, f)
            expert_fc(1, 0)
            expert_proj(0, 0)
            for f in range(1, 3):
                expert_fc(1, f)
            expert_proj(0, 1)
            expert_fc(1, 3)
            for f in range(2, 4):
                expert_proj(0, f)
            for f in range(0, 2):
                expert_fc(2, f)
            results_turned(0, 0)
            for f in range(0, 3):
                expert_proj(1, f)
            expert_fc(2, 2)
            expert_proj(1, 3)
            expert_fc(2, 3)
            for f in range(0, 2):
                expert_proj(2, f)
            results_turned(0, 1)
            expert_proj(2, 2)
            expert_fc(3, 0)
            expert_proj(2, 3)
            rows_turned(2, 0)
            for f in range(1, 3):
                expert_fc(3, f)
            results_turned(1, 0)
            expert_proj(3, 0)
            expert_fc(3, 3)
            rows_turned(2, 1)
            for f in range(0, 2):
                expert_fc(4, f)
            for f in range(1, 3):
                expert_proj(3, f)
            expert_fc(4, 2)
            expert_proj(3, 3)
            expert_fc(4, 3)
            expert_fc(5, 0)
            expert_proj(4, 0)
            results_turned(1, 1)
            for f in range(1, 3):
                expert_proj(4, f)
            rows_turned(3, 0)
            for f in range(1, 3):
                expert_fc(5, f)
            expert_proj(4, 3)
            expert_proj(5, 0)
            expert_fc(5, 3)
            results_turned(2, 0)
            rows_turned(3, 1)
            expert_proj(5, 1)
            expert_fc(6, 0)
            expert_proj(5, 2)
            expert_fc(6, 1)
            expert_proj(5, 3)
            for f in range(2, 4):
                expert_fc(6, f)
            expert_proj(6, 0)
            results_turned(2, 1)
            for f in range(0, 4):
                expert_fc(7, f)
            for f in range(1, 4):
                expert_proj(6, f)
            for f in range(0, 2):
                expert_proj(7, f)
            results_turned(3, 0)
            for f in range(2, 4):
                expert_proj(7, f)
            results_turned(3, 1)
            sums = [ring.claim(pe, "sum", c) for c in range(1, CH)]
            for c in range(1, CH):
                M(sums[c - 1][:, 0:N], ident, pay[0][c][:, :, 0:C], start=True, stop=False)
            for c in range(1, CH):
                pe.wait_ge(got_in[c], 16)
                ring.fill("sum", c, M(sums[c - 1][:, 0:N], ident, got[c][:, 0, :, :], start=False, stop=True))

        @block.sync
        def _(sp):
            def load_x(c):
                rows = x.rearrange("b l c -> (b l) c")[N * c:N * (c + 1), :]
                sp.dma_start(x_sb[c][:, :, :], rows.rearrange("(a p) c -> p a c", p=P)).then_inc(x_in[c], 16)

            def rotate_v(c):
                ring.wait_read(sp, "v", c)
                sp.dma_start(v_twice[c].rearrange("r p t -> p r t"),
                             vT[c][:, :].unsqueeze(1).to_broadcast((P, 2, N))).then_inc(v_stored[c], 16)

            def bring_v(c):
                sp.wait_ge(v_stored[c], 16)
                if c >= 2:
                    sp.wait_ge(s["p1_rest"], (D - 1) * (c - 1))
                for i, (j0, j1) in enumerate(V_PARTS):
                    windows = v_twice[c, 0]
                    windows = bass.AP(windows.tensor, windows.offset + H * N * j0, [[N, P], [H * N, j1 - j0], [1, N]])
                    sp.dma_start(v_rot[c % 2][:, j0 - 1:j1 - 1, :], windows).then_inc(v_back[c % 2][i], 16)

            load_x(0)
            sp.dma_start(context_sb[:, :], context).then_inc(s["context_in"], 16)
            sp.dma_start(early_sb[:, :], early).then_inc(s["early_in"], 16)
            for c in range(1, CH):
                load_x(c)
            sp.dma_start(routing_sb[:, :], routing).then_inc(s["routing_in"], 16)
            rotate_v(0)
            bring_v(0)
            sp.dma_start(wo_sb[:, :, :], wo_rot).then_inc(s["wo_in"], 16)
            rotate_v(1)
            bring_v(1)
            sp.dma_start(mlp_sb[:, :], mlp).then_inc(s["mlp_in"], 16)
            rotate_v(2)
            bring_v(2)
            rotate_v(3)
            bring_v(3)
            sp.wait_ge(s["pool_consts"], 1)
            for dst, name in ((slots[0:SLOTS, :], "zero_slots"), (results[0:TOP * T, :], "zero_results")):
                n = dst.shape[0] // P // ZREP * dst.shape[1]
                sp.dma_start(dst.rearrange("(p n i) r -> p n (i r)", p=P, n=ZREP),
                             zeros[:, 0:n].unsqueeze(1).to_broadcast((P, ZREP, n))).then_inc(s[name], 16)
            for w in range(PAIRS):
                sp.dma_start(c_proj_sb[:, 2 * w:2 * w + 2, :, :], c_proj[:, 2 * w:2 * w + 2, :, :])\
                  .then_inc(proj_loaded[w], 16)
            sp.wait_ge(s["p1_rest"], (D - 1) * CH)
            for w in range(PAIRS):
                if w == PAIRS - 1:
                    sp.wait_ge(s["fc_lo_sb"], 2)
                sp.dma_start(fc_in[w], c_fc[:, 2 * w:2 * w + 2, :]).then_inc(fc_loaded[w], 16)
            sp.wait_ge(s["first_sent"], 16 * TILES * CH)
            sp.wait_ge(second_sent[CH - 1], 16 * TILES)
            for w in range(PAIRS):
                for part, (n0, n1) in enumerate(IN_PARTS):
                    if w >= 2:
                        side.wait_read(sp, f"in{part}", w - 2)
                        sp.wait_ge(s["send_ready"], 2 * (w - 1))
                    sp.dma_start(rows_in[w % 2][:, n0:n1, :],
                                 slots[P * (PT * w + n0):P * (PT * w + n1), :].rearrange("(i p) r -> p i r", p=P))\
                      .then_inc(rows_loaded[w % 2][part], 16)
            for i in range(2):
                sp.wait_ge(results_sent[i], 16 * PT * PAIRS // 2)
            for c in range(CH):
                rows = results[TOP * N * c:TOP * N * (c + 1), :].rearrange("(g p) r -> p g r", p=P)
                sp.dma_start(got[c].rearrange("p k a r -> p (k a) r"), rows).then_inc(got_in[c], 16)
            for c in range(CH):
                if c < CH - 1:
                    sp.wait_ge(s["post3_done"], TILES * (c + 1))
                else:
                    sp.wait_ge(s["last_done"], TILES)
                rows = out.rearrange("b l c -> (b l) c")[N * c:N * (c + 1), :]
                sp.dma_start(rows.rearrange("(a p) c -> p a c", p=P), xn[c][:, :, :]).then_inc(s["out_stored"], 16)
            sp.wait_ge(s["out_stored"], 16 * CH)

        @block.gpsimd
        def _(pool):
            order = Order(pool, s["pool_order"])

            def rstd_of(name, c):
                pool.wait_ge(s[f"{name}_var"], c + 1)
                nc.gpsimd.tensor_tensor(rstd[c][:, :], var_eps[c][:, :], minus_half[:, :], ALU.pow)\
                  .then_inc(s[f"{name}_rstd"], 1)

            def product(c, j):
                m = (D - 1) * c + j - 1
                if j == 1:
                    pool.wait_ge(s["k_sb"], c + 1)
                for i, (j0, _) in enumerate(V_PARTS):
                    if j == j0:
                        pool.wait_ge(v_back[c % 2][i], 16 * (c // 2 + 1))
                if m >= NP1:
                    c0, j0 = (m - NP1) // (D - 1), (m - NP1) % (D - 1) + 1
                    pool.wait_ge(s["kv_mm"], D * c0 + j0 + 1)
                nc.gpsimd.tensor_tensor(p1[m % NP1][:, :], kT[c][:, :], v_rot[c % 2][:, j - 1, :], ALU.mult)\
                  .then_inc(s["p1_rest"], 1)

            def twice_residual(c):
                ring.wait_read(pool, "y_back", c)
                nc.gpsimd.tensor_tensor(xx2[c][:, :, :], x_sb[c][:, :, :], x2[c][:, :, :], ALU.add)\
                  .then_inc(s["xx2_sb"], 1)

            def send(c, k, a):
                pool.wait_ge(s["targets"], c + 1)
                if k == 1:
                    pool.wait_ge(s["pay1_sb"], c + 1)
                elif c:
                    pool.wait_ge(second_sent[c - 1], 16 * TILES)
                pool.indirect_dma_start(slots, bass.IndirectOffsetOnAxis(ap=target[c][:, k, a:a + 1], axis=0),
                                        pay[k][c][:, a, :], None).then_inc(second_sent[c] if k else s["first_sent"], 16)

            order(nc.gpsimd.memset(minus_half[:, :], -0.5))
            order(nc.gpsimd.memset(ones_row[:, :], 1.0))
            order(nc.gpsimd.memset(ones_bf[:, :], 1.0))
            order.wait()
            rstd_of("ln1", 0)
            rstd_of("ln1", 1)
            rstd_of("ln1", 2)
            rstd_of("ln1", 3)
            pool.wait_ge(s["routing_in"], 16)
            order(nc.gpsimd.tensor_copy(tri_bf[:, :], par("tri")))
            order.wait()
            nc.gpsimd.memset(zeros[:, :], 0.0).then_inc(s["pool_consts"], 1)
            for j in range(1, 8):
                product(0, j)
            for j in range(1, 8):
                product(1, j)
            for j in range(1, 3):
                product(2, j)
            twice_residual(0)
            product(2, 3)
            rstd_of("ln2", 0)
            for j in range(4, 8):
                product(2, j)
            for j in range(1, 3):
                product(3, j)
            twice_residual(1)
            rstd_of("ln2", 1)
            for j in range(3, 5):
                product(3, j)
            twice_residual(2)
            rstd_of("ln2", 2)
            for j in range(5, 7):
                product(3, j)
            rstd_of("post1", 0)
            product(3, 7)
            rstd_of("post1", 1)
            twice_residual(3)
            rstd_of("ln2", 3)
            rstd_of("post2", 0)
            rstd_of("post2", 1)
            rstd_of("post1", 2)
            pool.wait_ge(s["zero_slots"], 16)
            send(0, 1, 0)
            send(0, 1, 1)
            rstd_of("post1", 3)
            send(0, 0, 0)
            send(0, 0, 1)
            send(1, 1, 0)
            send(1, 1, 1)
            rstd_of("post2", 2)
            send(1, 0, 0)
            send(1, 0, 1)
            rstd_of("post2", 3)
            send(2, 1, 0)
            send(2, 1, 1)
            send(2, 0, 0)
            send(2, 0, 1)
            send(3, 1, 0)
            send(3, 1, 1)
            send(3, 0, 0)
            send(3, 0, 1)
            pool.wait_ge(s["zero_results"], 16)
            for w in range(PAIRS):
                for part, tiles in enumerate(((0, 1), (2, 3, 4))):
                    pool.wait_ge(s["send_ready"], 2 * (w + 1))
                    for i in tiles:
                        if i < tiles[-1]:
                            pool.wait_ge(s["out_sb"], (PT - 2) * w + i - part + 1)
                        else:
                            side.wait_read(pool, f"out{part}", w)
                        pool.indirect_dma_start(results, bass.IndirectOffsetOnAxis(ap=send_to[:, w, i:i + 1], axis=0),
                                                rows_out[w % 2][:, i, :], None).then_inc(results_sent[w % 2], 16)
            for c in range(CH):
                rstd_of("post3", c)
                if c == CH - 1:
                    break
                pool.wait_ge(s["post3_rstd"], c + 1)
                pool.wait_ge(s["minus_mean_sb"], c + 1)
                nc.gpsimd.tensor_tensor(shift[c][:, :], minus_mean[c][:, :], rstd[c][:, :], ALU.mult)\
                  .then_inc(s["shift_sb"], 1)

        @block.scalar
        def _(act):
            order = Order(act, s["act_order"])
            A = nc.scalar.activation

            def col(name, i=0):
                return par(name)[:, i:i + 1]

            def read(what, c, dst, func=ACT.Copy, **kw):
                src = ring.take(act, what, c)
                ring.release(what, c, A(dst, src[0:dst.shape[0], 0:dst.free_size()], func, **kw))

            def ln1_out(c):
                if c == 0:
                    act.wait_ge(s["early_in"], 16)
                read("ln1T", c, xnT[c][:, :], ACT.Identity, bias=col("ln1_b"), scale=col("ln1_w"))

            def elu_parts(name, c):
                exp, relu = (k_exp, k_relu) if name == "k" else (q_exp, q_relu)
                if c >= 2:
                    act.wait_ge(s[f"{name}_sb"], c - 1)
                src = ring.take(act, name, c)
                A(exp[c][:, :], src[:, 0:N], ACT.Exp, bias=col(f"{name}_b")).then_inc(s["exp_parts"], 1)
                ring.release(name, c, A(relu[c][:, :], src[:, 0:N], ACT.Relu, bias=col(f"{name}_b")))

            def v_out(c):
                read("v", c, vT[c][:, :], ACT.Identity, bias=col("v_b"))

            def y_out(c):
                act.wait_ge(s["y_step"], D * (c + 1))
                A(yT[c][:, :], y_bank[:, 0:N], ACT.Identity, bias=col("o_b")).then_inc(s["y_sb"], 1)

            def ln2_out(c):
                read("ln2T", c, xnT[c][:, :], ACT.Identity, bias=col("ln2_b"), scale=col("ln2_w"))

            def gelu(c, f):
                if c >= 2 and f == 0:
                    ring.wait_read(act, "proj", c - 2)
                read(f"fc{f}", c, hT[c][:, f, :], ACT.Gelu, bias=col("fc_b", f))

            def mlp_out(c):
                read("proj", c, yT[c][:, :], ACT.Identity, bias=col("proj_b"))

            def cross_exp(c):
                ring.wait_read(act, "scores", c)
                A(s_exp[c][:, :, :], s_sub[c][:, :, :], ACT.Exp, scale=float(C) ** -0.5).then_inc(s["exp_sb"], 1)

            def weights_out(c):
                read("expT", c, expT[c][:, :])

            def x3_out(c):
                read("x3T", c, xnT[c][:, :])

            def x4_out(c):
                read("x4T", c, xnT[c][:, :])

            def second_rows(c):
                act.wait_ge(s["post2_done"], TILES * (c + 1))
                A(pay[1][c][:, :, 0:C], pay[0][c][:, :, 0:C], ACT.Copy).then_inc(s["pay1_sb"], 1)

            def key_out():
                act.wait_ge(s["context_in"], 16)
                read("KT", 0, KT[:, :], ACT.Identity, bias=col("bk"))

            def value_out(b):
                act.wait_ge(s["context_in"], 16)
                src = ring.take(act, "V", b)
                for a in range(TILES):
                    ins = A(V_tile[b][:, a, :], src[0:TILES * S, 0:C], ACT.Copy, scale=par("quad")[0:TILES * S, a:a + 1])
                    if a < TILES - 1:
                        ins.then_inc(s["V_tile_sb"], 1)
                ring.release("V", b, ins)

            def gap_out(c):
                act.wait_ge(s["gap_ready"], c + 1)
                A(gap_tanh[c][:, :], gap[c][:, :], ACT.Tanh, scale=-0.5).then_inc(s["gap_tanh_sb"], 1)

            act.wait_ge(s["pool_order"], 1)
            order(A(warm[:, :], minus_half[:, :], ACT.Exp))
            key_out()
            value_out(0)
            read("bqK", 0, bqK[:, :])
            ln1_out(0)
            value_out(1)
            read("WqK", 0, WqK[:, :])
            v_out(0)
            elu_parts("k", 0)
            ln1_out(1)
            elu_parts("q", 0)
            ln1_out(2)
            ln1_out(3)
            v_out(1)
            v_out(2)
            elu_parts("k", 1)
            elu_parts("q", 1)
            v_out(3)
            elu_parts("k", 2)
            elu_parts("q", 2)
            elu_parts("k", 3)
            elu_parts("q", 3)
            y_out(0)
            y_out(1)
            ln2_out(0)
            for f in range(0, 4):
                gelu(0, f)
            ln2_out(1)
            y_out(2)
            for f in range(0, 2):
                gelu(1, f)
            mlp_out(0)
            for f in range(2, 4):
                gelu(1, f)
            ln2_out(2)
            for f in range(0, 2):
                gelu(2, f)
            mlp_out(1)
            x3_out(0)
            cross_exp(0)
            x3_out(1)
            y_out(3)
            weights_out(0)
            cross_exp(1)
            gelu(2, 2)
            weights_out(1)
            gelu(2, 3)
            mlp_out(2)
            ln2_out(3)
            second_rows(0)
            gelu(3, 0)
            x4_out(0)
            for f in range(1, 4):
                gelu(3, f)
            gap_out(0)
            second_rows(1)
            x4_out(1)
            mlp_out(3)
            x3_out(2)
            cross_exp(2)
            gap_out(1)
            weights_out(2)
            x3_out(3)
            cross_exp(3)
            weights_out(3)
            second_rows(2)
            x4_out(2)
            gap_out(2)
            second_rows(3)
            x4_out(3)
            gap_out(3)
            def fc_hi(e):
                act.wait_ge(fc_loaded[e // 2], 16)
                A(c_fc_hi[:, e, :], fc_in[e // 2][:, e % 2, :], ACT.Copy).then_inc(s["fc_hi_sb"], 1)

            def proj_hi(e):
                act.wait_ge(proj_loaded[e // 2], 16)
                A(c_proj_hi[:, e, :, :], c_proj_sb[:, e, :, :], ACT.Copy).then_inc(s["proj_hi_sb"], 1)

            order(A(warm[:, :], minus_half[:, :], ACT.Gelu))
            for e in range(E - 2):
                fc_hi(e)
            for e in range(2):
                proj_hi(e)
            for e in range(E - 2, E):
                fc_hi(e)
            for e in range(2, E):
                proj_hi(e)

            def rows_hi(w, part):
                n0, n1 = IN_PARTS[part]
                src = side.take(act, f"in{part}", w)
                if w >= 2 and part == 0:
                    ring.wait_read(act, f"expert_fc{FC - 1}", 2 * w - 3)
                A(in_hi[w % 2][:, P * n0:P * n1], src[:, 0:P * (n1 - n0)], ACT.Copy).then_inc(s["in_hi_sb"], 1)

            def gelu_of(e, f):
                if e:
                    act.wait_ge(s["he_lo_sb"], FC * (e - 1) + f + 1)
                read(f"expert_fc{f}", e, he[f][:, :], ACT.Gelu)

            def gelu_hi(e, f):
                if e >= 2 and f == 0:
                    side.wait_read(act, "expert_proj", e - 2)
                ring.wait_read(act, f"expert_fc{f}", e)
                A(he_hi[e % 2][:, f, :], he[f][:, :], ACT.Copy).then_inc(s["he_hi_sb"], 1)

            rows_hi(0, 0)
            rows_hi(0, 1)
            rows_hi(1, 0)
            gelu_of(0, 0)
            gelu_hi(0, 0)
            rows_hi(1, 1)
            for f in range(1, 3):
                gelu_of(0, f)
            gelu_hi(0, 1)
            gelu_of(0, 3)
            gelu_hi(0, 2)
            gelu_of(1, 0)
            gelu_hi(0, 3)
            gelu_of(1, 1)
            gelu_hi(1, 0)
            gelu_of(1, 2)
            gelu_hi(1, 1)
            gelu_of(1, 3)
            gelu_hi(1, 2)
            gelu_of(2, 0)
            gelu_hi(1, 3)
            gelu_of(2, 1)
            for f in range(0, 2):
                gelu_hi(2, f)
            gelu_of(2, 2)
            gelu_hi(2, 2)
            gelu_of(2, 3)
            gelu_hi(2, 3)
            gelu_of(3, 0)
            gelu_hi(3, 0)
            rows_hi(2, 0)
            for f in range(1, 3):
                gelu_of(3, f)
            for f in range(1, 3):
                gelu_hi(3, f)
            gelu_of(3, 3)
            rows_hi(2, 1)
            gelu_hi(3, 3)
            for f in range(0, 2):
                gelu_of(4, f)
            gelu_hi(4, 0)
            gelu_of(4, 2)
            for f in range(1, 3):
                gelu_hi(4, f)
            gelu_of(4, 3)
            gelu_of(5, 0)
            gelu_hi(4, 3)
            gelu_hi(5, 0)
            rows_hi(3, 0)
            for f in range(1, 3):
                gelu_of(5, f)
            for f in range(1, 3):
                gelu_hi(5, f)
            gelu_of(5, 3)
            gelu_hi(5, 3)
            rows_hi(3, 1)
            gelu_of(6, 0)
            gelu_hi(6, 0)
            gelu_of(6, 1)
            gelu_hi(6, 1)
            for f in range(2, 4):
                gelu_of(6, f)
            for f in range(2, 4):
                gelu_hi(6, f)
            for f in range(0, 2):
                gelu_of(7, f)
            gelu_hi(7, 0)
            gelu_of(7, 2)
            gelu_hi(7, 1)
            gelu_of(7, 3)
            for f in range(2, 4):
                gelu_hi(7, f)
            for c in range(CH - 1):
                act.wait_ge(s["shift_sb"], c + 1)
                if c:
                    ring.wait_read(act, "sum", c)
                for a in range(TILES):
                    A(xn[c][:, a, :], x2[c][:, a, :], ACT.Identity, bias=shift[c][:, a:a + 1],
                      scale=rstd[c][:, a:a + 1]).then_inc(s["post3_done"], 1)

        @block.vector
        def _(dve):
            order = Order(dve, s["dve_order"])
            V = nc.vector
            flat = "p a c -> p (a c)"

            marks = {}
            summed = dict(ln2="y_back", post1="mlp_back", post2="attend", post3="sum")

            def stats_of(name, c):
                if name == "ln1":
                    dve.wait_ge(x_in[c], 16)
                elif name == "post3" and c == 0:
                    order.wait_for(marks["sum"])
                else:
                    ring.wait_read(dve, summed[name], c)
                if name == "post2":
                    order.wait_for(marks["cross", c])
                src = x_sb[c] if name == "ln1" else x2[c]
                for a in range(TILES):
                    marks["stats", c, a] = order(V.bn_stats(stats[c][:, a, :], src[:, a, :]))

            def aggregate(c):
                for a in range(TILES):
                    order.wait_for(marks["stats", c, a])
                    marks["aggregate", c] = order(V.bn_aggr(mean_var[c][:, a, :], stats[c][:, a, :]))

            def variance(name, c):
                order.wait_for(marks["aggregate", c])
                V.tensor_scalar(var_eps[c][:, :], mean_var[c][:, :, 1], EPS, None, ALU.add)\
                 .then_inc(s[f"{name}_var"], 1)

            def scale(name, c, src, dst):
                dve.wait_ge(s[f"{name}_rstd"], c + 1)
                for a in range(TILES):
                    V.tensor_scalar(dst[:, a, 0:C], src[:, a, :], mean_var[c][:, a, 0:1], rstd[c][:, a:a + 1],
                                    ALU.subtract, ALU.mult).then_inc(s[f"{name}_done"], 1)

            def elu(name, c):
                exp, relu, dst = (k_exp, k_relu, kT) if name == "k" else (q_exp, q_relu, qT)
                dve.wait_ge(s["exp_parts"], 2 * c + (1 if name == "k" else 2))
                ring.wait_read(dve, name, c)
                V.scalar_tensor_tensor(out=dst[c][:, :], in0=exp[c][:, :], scalar=1.0, in1=relu[c][:, :],
                                       op0=ALU.min, op1=ALU.add).then_inc(s[f"{name}_sb"], 1)

            def first_product(c):
                dve.wait_ge(s["k_sb"], c + 1)
                ring.wait_read(dve, "v", c)
                if c >= 2:
                    dve.wait_ge(s["kv_mm"], D * (c - 2) + 1)
                V.tensor_tensor(p1_0[c][:, :], kT[c][:, :], vT[c][:, :], ALU.mult).then_inc(s["p1_first"], 1)

            def q_times_sums(c):
                dve.wait_ge(s["q_sb"], c + 1)
                src = ring.take(dve, "k_sum", c)
                ring.release("k_sum", c, V.tensor_tensor(qkT[c][:, :], qT[c][:, :], src[:, 0:N], ALU.mult))

            def invert(c):
                src = ring.take(dve, "norm", c)
                ring.release("norm", c, V.reciprocal(norm[c][:, :, :].rearrange("p a h -> p (a h)"), src[:, 0:TILES * H]))
                ring.wait_read(dve, "norm", c)
                V.tensor_copy(norm_d[c][:, :, :, :], norm[c][:, :, :].unsqueeze(2).to_broadcast((P, TILES, D, H)))\
                 .then_inc(s["norm_d_sb"], 1)

            def q_over_norm(c):
                src = ring.take(dve, "norm_back", c)
                ring.release("norm_back", c, V.tensor_tensor(qnT[c][:, :], qT[c][:, :], src[:, 0:N], ALU.mult))

            def second(c, j):
                n = D * c + j
                if j == 0:
                    ring.wait_read(dve, "norm_back", c)
                dve.wait_ge(s["kv_mm"], n + 1)
                if n >= NP1:
                    dve.wait_ge(s["y_step"], n - NP1 + 1)
                V.tensor_tensor(p2[n % NP1][:, :], qnT[c][:, :], kv_bank[n % KVB][:, 0:N], ALU.mult)\
                 .then_inc(s["p2_ready"], 1)

            def add_back(what, c, residual):
                src = ring.take(dve, what, c)
                ring.release(what, c, V.tensor_tensor(x2[c][:, :, :].rearrange(flat), residual[c][:, :, :].rearrange(flat),
                                                      src[:, 0:N], ALU.add))

            def attended(c):
                add_back("y_back", c, x_sb)

            def mlp_added(c):
                dve.wait_ge(s["xx2_sb"], c + 1)
                add_back("mlp_back", c, xx2)

            def softmax_in(c):
                src = ring.take(dve, "scores", c)[:, 0:TILES * S].rearrange("p (a k) -> p a k", k=S)
                order(V.tensor_reduce(s_max[c][:, :], src, AX.X, ALU.max))
                order.wait()
                ring.release("scores", c, V.tensor_tensor(
                    s_sub[c][:, :, :], src, s_max[c][:, :].unsqueeze(2).to_broadcast((P, TILES, S)), ALU.subtract))

            def softmax_sum(c):
                dve.wait_ge(s["exp_sb"], c + 1)
                order(V.tensor_reduce(s_sum[c][:, :], s_exp[c][:, :, :], AX.X, ALU.add))
                order.wait()
                marks["s_inv", c] = order(V.reciprocal(s_inv[c][:, :], s_sum[c][:, :]))

            def cross_added(c):
                order.wait_for(marks["s_inv", c])
                src = ring.take(dve, "attend", c)
                dve.wait_ge(s["post1_done"], TILES * (c + 1))
                for a in range(TILES):
                    ins = V.scalar_tensor_tensor(out=x2[c][:, a, :], in0=src[:, C * a:C * (a + 1)],
                                                 scalar=s_inv[c][:, a:a + 1], in1=x3[c][:, a, :],
                                                 op0=ALU.mult, op1=ALU.add)
                    if a < TILES - 1:
                        marks["cross", c] = order(ins)
                ring.release("attend", c, ins)

            def table(name, c):
                return par(name)[:, TOP * TILES * c:TOP * TILES * (c + 1)].rearrange("p (k a) -> p k a", a=TILES)

            def choose(c):
                src = ring.take(dve, "logits", c)
                for a in range(TILES):
                    order(V.max(top_v[c][:, a, :], src[:, E * a:E * (a + 1)]))
                order.wait()
                V.tensor_tensor(gap[c][:, :], top_v[c][:, :, 1], top_v[c][:, :, 0], ALU.subtract)\
                 .then_inc(s["gap_ready"], 1)
                for a in range(TILES):
                    ins = V.max_index(top_i[c][:, a, :], top_v[c][:, a, :], src[:, E * a:E * (a + 1)])
                    if a < TILES - 1:
                        order(ins)
                ring.release("logits", c, ins)
                order.wait()
                ring.wait_read(dve, "logits", c)
                if c == 0:
                    dve.wait_ge(s["routing_in"], 16)
                expert = par("expert").unsqueeze(1).to_broadcast((P, TILES, E))
                for i, k in enumerate((0, 1, 1)):
                    V.tensor_tensor(one_hot[c][:, i, :, :], top_i[c][:, :, k:k + 1].to_broadcast((P, TILES, E)), expert,
                                    ALU.is_equal).then_inc(s["hot_ready"], 1)
                order(V.scalar_tensor_tensor(out=from_trash[c][:, :, :], in0=top_i[c][:, :, 0:TOP].rearrange("p a k -> p k a"),
                                             scalar=float(CAP), in1=table("from_trash", c), op0=ALU.mult, op1=ALU.add))

            def weights(c):
                dve.wait_ge(s["gap_tanh_sb"], c + 1)
                for k in range(TOP):
                    order(V.tensor_scalar(pay[k][c][:, :, C + 1], gap_tanh[c][:, :], 0.5 if k == 0 else -0.5, 0.5,
                                          ALU.mult, ALU.add))

            def places_of(c):
                src = ring.take(dve, "ranks", c)[:, 0:3 * TILES * E].rearrange("p (g e) -> p g e", e=E)
                dve.wait_ge(s["hot_ready"], 3 * (c + 1))
                ring.release("ranks", c, V.tensor_tensor(rank_all[c][:, :, :], src,
                                                         one_hot[c][:, :, :, :].rearrange("p s a e -> p (s a) e"), ALU.mult))
                ring.wait_read(dve, "ranks", c)
                order(V.tensor_reduce(rank[c][:, :, :].rearrange("p s a -> p (s a)"), rank_all[c][:, :, :], AX.X, ALU.add))
                order.wait()
                for k, way in enumerate((ALU.add, ALU.subtract)):
                    order(V.tensor_tensor(away[c][:, k, :], from_trash[c][:, k, :], rank[c][:, k, :], way))
                order.wait()
                order(V.scalar_tensor_tensor(out=away_kept[c][:, :, :], in0=rank[c][:, 0:3:2, :], scalar=float(CAP),
                                             in1=away[c][:, :, :], op0=ALU.is_lt, op1=ALU.mult))
                for k in range(TOP):
                    order(V.tensor_scalar(pay[k][c][:, :, C], away[c][:, k, :], -1.0, -float(TOP * T + SLOTS),
                                          ALU.mult, ALU.add))
                order.wait()
                V.tensor_tensor(target[c][:, :, :], away_kept[c][:, :, :], table("trash", c), ALU.add)\
                 .then_inc(s["targets"], 1)

            stats_of("ln1", 0)
            aggregate(0)
            variance("ln1", 0)
            scale("ln1", 0, x_sb[0], xn[0])
            stats_of("ln1", 1)
            stats_of("ln1", 2)
            stats_of("ln1", 3)
            aggregate(1)
            aggregate(2)
            variance("ln1", 1)
            aggregate(3)
            variance("ln1", 2)
            variance("ln1", 3)
            scale("ln1", 1, x_sb[1], xn[1])
            scale("ln1", 2, x_sb[2], xn[2])
            scale("ln1", 3, x_sb[3], xn[3])
            elu("k", 0)
            first_product(0)
            elu("q", 0)
            q_times_sums(0)
            invert(0)
            elu("k", 1)
            first_product(1)
            elu("q", 1)
            q_over_norm(0)
            q_times_sums(1)
            second(0, 0)
            elu("k", 2)
            second(0, 1)
            elu("q", 2)
            first_product(2)
            invert(1)
            q_times_sums(2)
            second(0, 2)
            q_over_norm(1)
            second(0, 3)
            elu("k", 3)
            invert(2)
            elu("q", 3)
            second(0, 4)
            q_times_sums(3)
            for j in range(5, 8):
                second(0, j)
            q_over_norm(2)
            second(1, 0)
            first_product(3)
            for j in range(1, 6):
                second(1, j)
            attended(0)
            second(1, 6)
            stats_of("ln2", 0)
            aggregate(0)
            variance("ln2", 0)
            second(1, 7)
            second(2, 0)
            scale("ln2", 0, x2[0], xn[0])
            for j in range(1, 5):
                second(2, j)
            attended(1)
            second(2, 5)
            stats_of("ln2", 1)
            aggregate(1)
            variance("ln2", 1)
            scale("ln2", 1, x2[1], xn[1])
            for j in range(6, 8):
                second(2, j)
            attended(2)
            stats_of("ln2", 2)
            aggregate(2)
            variance("ln2", 2)
            scale("ln2", 2, x2[2], xn[2])
            mlp_added(0)
            stats_of("post1", 0)
            aggregate(0)
            variance("post1", 0)
            invert(3)
            scale("post1", 0, x2[0], x3[0])
            q_over_norm(3)
            for j in range(0, 3):
                second(3, j)
            mlp_added(1)
            second(3, 3)
            stats_of("post1", 1)
            aggregate(1)
            softmax_in(0)
            variance("post1", 1)
            second(3, 4)
            scale("post1", 1, x2[1], x3[1])
            second(3, 5)
            softmax_sum(0)
            for j in range(6, 8):
                second(3, j)
            softmax_in(1)
            attended(3)
            softmax_sum(1)
            stats_of("ln2", 3)
            aggregate(3)
            cross_added(0)
            variance("ln2", 3)
            stats_of("post2", 0)
            aggregate(0)
            scale("ln2", 3, x2[3], xn[3])
            variance("post2", 0)
            scale("post2", 0, x2[0], pay[0][0])
            cross_added(1)
            mlp_added(2)
            stats_of("post2", 1)
            stats_of("post1", 2)
            aggregate(1)
            aggregate(2)
            variance("post2", 1)
            variance("post1", 2)
            choose(0)
            scale("post2", 1, x2[1], pay[0][1])
            weights(0)
            scale("post1", 2, x2[2], x3[2])
            places_of(0)
            mlp_added(3)
            stats_of("post1", 3)
            aggregate(3)
            softmax_in(2)
            variance("post1", 3)
            choose(1)
            scale("post1", 3, x2[3], x3[3])
            weights(1)
            softmax_sum(2)
            places_of(1)
            cross_added(2)
            stats_of("post2", 2)
            aggregate(2)
            softmax_in(3)
            variance("post2", 2)
            softmax_sum(3)
            scale("post2", 2, x2[2], pay[0][2])
            cross_added(3)
            stats_of("post2", 3)
            aggregate(3)
            variance("post2", 3)
            choose(2)
            scale("post2", 3, x2[3], pay[0][3])
            weights(2)
            places_of(2)
            choose(3)
            weights(3)
            places_of(3)

            def take_in(w, part):
                n0, n1 = IN_PARTS[part]
                src = side.take(dve, f"in{part}", w)
                if w >= 2 and part == 0:
                    ring.wait_read(dve, f"expert_fc{FC - 1}", 2 * w - 3)
                at = slice(P * n0, P * n1)
                dve.wait_ge(s["in_hi_sb"], 2 * w + part + 1)
                side.release(f"in{part}", w, V.tensor_tensor(in_lo[w % 2][:, at], src[:, 0:P * (n1 - n0)],
                                                             in_hi[w % 2][:, at].bitcast(F32), ALU.subtract))
                if part:
                    for loaded in rows_loaded[w % 2]:
                        dve.wait_ge(loaded, 16 * (w // 2 + 1))
                    V.tensor_tensor(send_to[:, w, :], rows_in[w % 2][:, :, C], par("slot")[:, PT * w:PT * (w + 1)],
                                    ALU.add).then_inc(s["send_ready"], 1)
                    V.tensor_copy(send_w[:, w, :], rows_in[w % 2][:, :, C + 1]).then_inc(s["send_ready"], 1)

            def expert_out(e):
                w = e // 2
                src = side.take(dve, "expert_proj", e)
                if w >= 2 and e % 2 == 0:
                    side.wait_read(dve, "out1", w - 2)
                side.release("expert_proj", e, V.tensor_copy(outT[w % 2][:, CAP * (e % 2):CAP * (e % 2 + 1)], src[:, 0:CAP]))

            def hand_out(w, part):
                tiles = ((0, 1), (2, 3, 4))[part]
                src = side.take(dve, f"out{part}", w)
                dve.wait_ge(s["send_ready"], 2 * (w + 1))
                if w >= 2 and part == 0:
                    dve.wait_ge(results_sent[w % 2], 16 * PT * (w // 2))
                for i in tiles:
                    at = P * (i - 2 * part)
                    ins = V.tensor_scalar(rows_out[w % 2][:, i, :], src[:, at:at + P], send_w[:, w, i:i + 1], None,
                                          ALU.mult)
                    if i < tiles[-1]:
                        ins.then_inc(s["out_sb"], 1)
                side.release(f"out{part}", w, ins)

            def fc_lo(e):
                dve.wait_ge(s["fc_hi_sb"], e + 1)
                V.tensor_tensor(c_fc_lo[:, e, :], fc_in[e // 2][:, e % 2, :], c_fc_hi[:, e, :].bitcast(F32), ALU.subtract)\
                 .then_inc(s["fc_lo_sb"], 1)

            def proj_lo(e):
                dve.wait_ge(s["proj_hi_sb"], e + 1)
                V.tensor_tensor(c_proj_lo[:, e, :, :], c_proj_sb[:, e, :, :], c_proj_hi[:, e, :, :].bitcast(F32),
                                ALU.subtract).then_inc(s["proj_lo_sb"], 1)

            def gelu_lo(e, f):
                if e >= 2 and f == 0:
                    side.wait_read(dve, "expert_proj", e - 2)
                ring.wait_read(dve, f"expert_fc{f}", e)
                dve.wait_ge(s["he_hi_sb"], FC * e + f + 1)
                V.tensor_tensor(he_lo[e % 2][:, f, :], he[f][:, :], he_hi[e % 2][:, f, :].bitcast(F32), ALU.subtract)\
                 .then_inc(s["he_lo_sb"], 1)

            for e in range(E - 2):
                fc_lo(e)
            for e in range(2):
                proj_lo(e)
            for e in range(E - 2, E):
                fc_lo(e)
            for e in range(2, E):
                proj_lo(e)
            take_in(0, 0)
            take_in(0, 1)
            take_in(1, 0)
            gelu_lo(0, 0)
            take_in(1, 1)
            for f in range(1, 4):
                gelu_lo(0, f)
            gelu_lo(1, 0)
            expert_out(0)
            for f in range(1, 3):
                gelu_lo(1, f)
            hand_out(0, 0)
            gelu_lo(1, 3)
            for f in range(0, 2):
                gelu_lo(2, f)
            expert_out(1)
            for f in range(2, 4):
                gelu_lo(2, f)
            hand_out(0, 1)
            expert_out(2)
            gelu_lo(3, 0)
            take_in(2, 0)
            hand_out(1, 0)
            for f in range(1, 3):
                gelu_lo(3, f)
            take_in(2, 1)
            gelu_lo(3, 3)
            gelu_lo(4, 0)
            expert_out(3)
            for f in range(1, 3):
                gelu_lo(4, f)
            hand_out(1, 1)
            gelu_lo(4, 3)
            gelu_lo(5, 0)
            take_in(3, 0)
            expert_out(4)
            for f in range(1, 3):
                gelu_lo(5, f)
            hand_out(2, 0)
            gelu_lo(5, 3)
            take_in(3, 1)
            gelu_lo(6, 0)
            expert_out(5)
            gelu_lo(6, 1)
            hand_out(2, 1)
            for f in range(2, 4):
                gelu_lo(6, f)
            for f in range(0, 2):
                gelu_lo(7, f)
            expert_out(6)
            for f in range(2, 4):
                gelu_lo(7, f)
            hand_out(3, 0)
            expert_out(7)
            hand_out(3, 1)

            def both_added(c):
                if c == 0:
                    dve.wait_ge(got_in[c], 16)
                    for k in range(TOP):
                        marks["sum"] = order(V.tensor_tensor(x2[c][:, :, :], got[c][:, k, :, :],
                                                             x2[c][:, :, :] if k else pay[0][c][:, :, 0:C], ALU.add))
                        if k == 0:
                            order.wait()
                    return
                src = ring.take(dve, "sum", c)
                dve.wait_ge(got_in[c], 16)
                ring.release("sum", c, V.tensor_tensor(x2[c][:, :, :].rearrange(flat), src[:, 0:N],
                                                       got[c][:, 1, :, :].rearrange(flat), ALU.add))

            for c in range(CH + 2):
                if c >= 2:
                    aggregate(c - 2)
                if c < CH:
                    both_added(c)
                if c >= 2:
                    variance("post3", c - 2)
                    if c - 2 < CH - 1:
                        V.tensor_scalar(minus_mean[c - 2][:, :], mean_var[c - 2][:, :, 0], -1.0, None, ALU.mult)\
                         .then_inc(s["minus_mean_sb"], 1)
                if 1 <= c <= CH:
                    stats_of("post3", c - 1)
            dve.wait_ge(s["post3_rstd"], CH)
            for a in range(TILES):
                V.tensor_scalar(xn[CH - 1][:, a, :], x2[CH - 1][:, a, :], mean_var[CH - 1][:, a, 0:1],
                                rstd[CH - 1][:, a:a + 1], ALU.subtract, ALU.mult).then_inc(s["last_done"], 1)


def kernel(**inputs):
    import concourse.bacc as bacc
    from concourse.bass_utils import run_bass_kernel_spmd

    a = {k: np.asarray(v) for k, v in inputs.items()}
    f32 = np.float32
    dh = np.arange(C).reshape(H, D).T.reshape(-1)

    def column(v):
        return v.reshape(-1, P).T

    def pack(columns, parts):
        return np.concatenate([parts[name] for name in columns], axis=1)

    table = constants()
    qkv = np.concatenate([a[f"L0_attn_{n}_w"][dh].T for n in "qkv"], axis=1)
    early = pack(EARLY, dict(
        table, ln1_w=column(a["L0_attn_ln1_w"]), ln1_b=column(a["L0_attn_ln1_b"]),
        q_b=column(a["L0_attn_q_b"][dh]), k_b=column(a["L0_attn_k_b"][dh]), v_b=column(a["L0_attn_v_b"][dh]),
        o_b=column(a["L0_attn_o_b"]), ln2_w=column(a["L0_attn_ln2_w"]), ln2_b=column(a["L0_attn_ln2_b"]),
        fc_b=column(a["L0_attn_fc_b"]), proj_b=column(a["L0_attn_proj_b"]), qkv=qkv))
    bv = np.zeros((P, C), f32)
    bv[0] = a["L0_xattn_bv"]
    context = pack(CONTEXT, dict(
        table, ctxT=np.tile(a["ctx_1024"], (1, TILES, 1)).reshape(-1, C).T, Wk=a["L0_xattn_Wk"], Wv=a["L0_xattn_Wv"],
        WqT=a["L0_xattn_Wq"].T, bk=column(a["L0_xattn_bk"]), bq=column(a["L0_xattn_bq"]), bv=bv))
    routing = pack(ROUTING, dict(table, w_g=a["L0_ffn_w_g"]))
    d, h = np.arange(C) // H, np.arange(C) % H
    wo_rot = np.stack([a["L0_attn_o_w"].T[h * D + (d + j) % D] for j in range(D)], axis=1)
    mlp = pack(MLP, dict(fcT=a["L0_attn_fc_w"].T,
                         projT=a["L0_attn_proj_w"].T.reshape(FC, P, C).transpose(1, 0, 2).reshape(P, FC * C)))
    c_fc = a["L0_ffn_c_fc"].transpose(1, 0, 2)
    c_proj = a["L0_ffn_c_proj"].reshape(E, FC, P, C).transpose(2, 0, 1, 3)
    arrays = dict(x=a["x"], context=context, early=early, routing=routing, wo_rot=wo_rot, mlp=mlp, c_fc=c_fc, c_proj=c_proj)
    arrays = {k: np.ascontiguousarray(v) for k, v in arrays.items()}

    nc = bacc.Bacc("TRN2", target_bir_lowering=False, num_devices=1)
    ins = [nc.dram_tensor(k, v.shape, F32, kind="ExternalInput").ap() for k, v in arrays.items()]
    out = nc.dram_tensor("out", (B, L, C), F32, kind="ExternalOutput").ap()
    program(nc, *ins, out)
    r = run_bass_kernel_spmd(nc, [arrays], core_ids=[0])
    return r.results[0]["out"]
```
